# Optimizing a Trainium2 kernel written in Bass

```python
import numpy as np
import jax
import jax.numpy as jnp

def _softmax(x, axis=-1):
    return jax.nn.softmax(x, axis=axis)

def _gelu(x):
    return jax.nn.gelu(x, approximate=True)

def _silu(x):
    return jax.nn.silu(x)

def _sigmoid(x):
    return jax.nn.sigmoid(x)

def _layernorm(x, axis=-1, eps=1e-05):
    m = jnp.mean(x, axis=axis, keepdims=True)
    v = jnp.var(x, axis=axis, keepdims=True)
    return (x - m) / jnp.sqrt(v + eps)

def _scatter_add(tgt, idx, src, axis=0):
    return tgt.at[idx].add(src)

def _segment_sum(src, seg, n):
    return jax.ops.segment_sum(src, seg, n)
kernel_name = 'mk_perceiver_d2_seqx_r4_526a19'

def setup_inputs(seed: int=0):
    np.random.seed(seed)
    _w = jnp.asarray

    def _rec_inputs():
        import jax
        import jax.numpy as jnp
        _rk = jax.random.key(seed)
        x = -0.0002928 + 1 * jax.random.normal(jax.random.fold_in(_rk, 1), (16, 64, 256), jnp.float32)
        _lenS = 64 - jax.random.randint(jax.random.fold_in(_rk, 7), (16,), 0, max(1, 64 // 4) + 1, jnp.int32)
        _lenS2 = 256 - jax.random.randint(jax.random.fold_in(_rk, 8), (16,), 0, max(1, 256 // 4) + 1, jnp.int32)
        _ctx_1024P = jax.random.normal(jax.random.fold_in(_rk, 11), (16, 16, 256), jnp.float32)
        _ctx_1024c = jax.random.dirichlet(jax.random.fold_in(_rk, 511), 0.3 * jnp.ones((16,), jnp.float32), (16, 256))
        _ctx_1024t = jnp.einsum('bsk,bkd->bsd', _ctx_1024c, _ctx_1024P)
        _ctx_1024t = _ctx_1024t * jax.lax.rsqrt(jnp.mean(jnp.square(_ctx_1024t)) + 1e-12) * 0.953939
        ctx_1024 = -1.39393e-06 + 0.999914 * (_ctx_1024t + 0.3 * jax.random.normal(jax.random.fold_in(_rk, 611), (16, 256, 256), jnp.float32))
        fside_BxSxS2_0 = jax.random.uniform(jax.random.fold_in(_rk, 12), (16, 64, 256), jnp.float32, 0.0, 1)
        _validS = jnp.arange(64)[None, :] < _lenS[:, None]
        _validS2 = jnp.arange(256)[None, :] < _lenS2[:, None]
        _causal = jnp.tril(jnp.ones((64, 64), dtype=bool))
        mask_BxSxS2_ik1 = jnp.where(jnp.broadcast_to(_validS2[:, None, :], (16, 64, 256)), 1, 0).astype(jnp.int32)
        return (x, ctx_1024, fside_BxSxS2_0, mask_BxSxS2_ik1)
    x, ctx_1024, fside_BxSxS2_0, mask_BxSxS2_ik1 = _rec_inputs()

    def _L0_xattn_setup():
        import jax, jax.numpy as jnp
        import numpy as np
        NUM_HEADS = 16
        HIDDEN = 256
        B, S = (2, 512)

        def _split_heads(x, H):
            b, s, d = x.shape
            return x.reshape(b, s, H, d // H).transpose(0, 2, 1, 3)
        key = jax.random.key(seed)
        ks = jax.random.split(key, 14)
        D = HIDDEN
        scale = 1.0 / np.sqrt(D)
        inp = {'query': jax.random.normal(ks[0], (B, S, D), jnp.float32), 'key_in': jax.random.normal(ks[1], (B, S, D), jnp.float32), 'value': jax.random.normal(ks[2], (B, S, D), jnp.float32), 'group_prob': jax.random.uniform(ks[3], (B, S, S), jnp.float32), 'mask': jax.random.randint(ks[4], (B, S, S), 0, 2, jnp.int32), 'wq_k': jax.random.normal(ks[5], (D, D), jnp.float32) * scale, 'wq_b': jnp.zeros((D,), jnp.float32), 'wk_k': jax.random.normal(ks[6], (D, D), jnp.float32) * scale, 'wk_b': jnp.zeros((D,), jnp.float32), 'wv_k': jax.random.normal(ks[7], (D, D), jnp.float32) * scale, 'wv_b': jnp.zeros((D,), jnp.float32), 'wo_k': jax.random.normal(ks[8], (D, D), jnp.float32) * scale, 'wo_b': jnp.zeros((D,), jnp.float32)}
        return inp
    _L0_xattn_all = _L0_xattn_setup()
    _L0_xattn_in = {k: v for k, v in _L0_xattn_all.items() if k in ('wq_k', 'wq_b', 'wk_k', 'wk_b', 'wv_k', 'wv_b', 'wo_k', 'wo_b')}
    del _L0_xattn_all

    def _L0_attn_setup():
        import jax, jax.numpy as jnp
        import numpy as np
        import math
        D_MODEL = 256
        N_HEADS = 16
        HEAD_DIM = D_MODEL // N_HEADS
        ROT_DIM = min(32, D_MODEL // 4)

        def _xavier(key, fan_in, fan_out):
            lim = math.sqrt(6.0 / (fan_in + fan_out))
            return jax.random.uniform(key, (fan_in, fan_out), jnp.float32, -lim, lim)
        key = jax.random.key(seed)
        ks = jax.random.split(key, 6)
        x = jax.random.normal(ks[0], (2, 512, D_MODEL), jnp.float32)
        Wq = _xavier(ks[1], D_MODEL, D_MODEL)
        Wk = _xavier(ks[2], D_MODEL, D_MODEL)
        Wv = _xavier(ks[3], D_MODEL, D_MODEL)
        Wr = _xavier(ks[4], D_MODEL, N_HEADS * ROT_DIM)
        Wo = _xavier(ks[5], D_MODEL, D_MODEL)
        z = jnp.zeros((D_MODEL,), jnp.float32)
        zr = jnp.zeros((N_HEADS * ROT_DIM,), jnp.float32)
        return {'x': x, 'Wq': Wq, 'bq': z, 'Wk': Wk, 'bk': z, 'Wv': Wv, 'bv': z, 'Wr': Wr, 'br': zr, 'Wo': Wo, 'bo': z}
    _L0_attn_all = _L0_attn_setup()
    _L0_attn_in = {k: v for k, v in _L0_attn_all.items() if k in ('Wq', 'bq', 'Wk', 'bk', 'Wv', 'bv', 'Wr', 'br', 'Wo', 'bo')}
    del _L0_attn_all

    def _L0_ffn_setup():
        import jax, jax.numpy as jnp
        import numpy as np
        TOP_K = 2
        key = jax.random.key(seed)
        k1, k2, k3 = jax.random.split(key, 3)
        B, S, D, E = (8, 512, 256, 8)
        x = jax.random.normal(k1, (B, S, D), dtype=jnp.float32)
        gate_w = jax.random.normal(k2, (E, D), dtype=jnp.float32) * (1.0 / np.sqrt(D))
        gate_b = jnp.zeros((E,), dtype=jnp.float32)
        expert_w = jax.random.normal(k3, (E, D, D), dtype=jnp.float32) * (1.0 / np.sqrt(D))
        expert_b = jnp.zeros((E, D), dtype=jnp.float32)
        return {'x': x, 'gate_w': gate_w, 'gate_b': gate_b, 'expert_w': expert_w, 'expert_b': expert_b}
    _L0_ffn_all = _L0_ffn_setup()
    _L0_ffn_in = {k: v for k, v in _L0_ffn_all.items() if k in ('gate_w', 'gate_b', 'expert_w', 'expert_b')}
    del _L0_ffn_all

    def _L1_xattn_setup():
        import jax, jax.numpy as jnp
        import numpy as np
        D_MODEL = 256
        H = 16
        D_H = D_MODEL // H
        key = jax.random.key(seed)
        ks = jax.random.split(key, 10)
        B, T_dec, T_enc = (2, 512, 512)
        s = 1.0 / np.sqrt(D_MODEL)
        return {'tgt': jax.random.normal(ks[0], (B, T_dec, D_MODEL), jnp.float32), 'memory': jax.random.normal(ks[1], (B, T_enc, D_MODEL), jnp.float32), 'W_q': jax.random.normal(ks[2], (D_MODEL, D_MODEL), jnp.float32) * s, 'b_q': jnp.zeros((D_MODEL,), jnp.float32), 'W_k': jax.random.normal(ks[3], (D_MODEL, D_MODEL), jnp.float32) * s, 'b_k': jnp.zeros((D_MODEL,), jnp.float32), 'W_v': jax.random.normal(ks[4], (D_MODEL, D_MODEL), jnp.float32) * s, 'b_v': jnp.zeros((D_MODEL,), jnp.float32), 'W_o': jax.random.normal(ks[5], (D_MODEL, D_MODEL), jnp.float32) * s, 'b_o': jnp.zeros((D_MODEL,), jnp.float32)}
    _L1_xattn_all = _L1_xattn_setup()
    _L1_xattn_in = {k: v for k, v in _L1_xattn_all.items() if k in ('W_q', 'b_q', 'W_k', 'b_k', 'W_v', 'b_v', 'W_o', 'b_o')}
    del _L1_xattn_all

    def _L1_attn_setup():
        import jax, jax.numpy as jnp
        import numpy as np
        BATCH, SEQ, D_MODEL, STATE_DIM = (8, 512, 256, 256)

        def _cayley_circulant_eigenvalues(a_params, n):
            half_n = n // 2
            a_full = jnp.zeros((n,), dtype=a_params.dtype)
            a_full = a_full.at[1:half_n].set(a_params[:half_n - 1])
            a_full = a_full.at[half_n + 1:].set(-a_params[:half_n - 1][::-1])
            omega = jnp.fft.fft(a_full).imag
            w2 = omega * omega
            denom = 1.0 + w2
            return ((1.0 - w2) / denom + 1j * (-2.0 * omega / denom)).astype(jnp.complex64)
        key = jax.random.key(seed)
        k1, k2, k3, k4 = jax.random.split(key, 4)
        u = jax.random.normal(k1, (BATCH, SEQ, D_MODEL), dtype=jnp.float32)
        a_params = jax.random.normal(k2, (STATE_DIM // 2,), dtype=jnp.float32) * 0.1
        B_w = jax.random.normal(k3, (STATE_DIM, D_MODEL), dtype=jnp.float32) / np.sqrt(D_MODEL).astype(np.float32)
        C_w = jax.random.normal(k4, (D_MODEL, STATE_DIM), dtype=jnp.float32) / np.sqrt(STATE_DIM).astype(np.float32)
        D = jnp.zeros((D_MODEL,), dtype=jnp.float32)
        return {'u': u, 'a_params': a_params, 'B_w': B_w, 'C_w': C_w, 'D': D}
    _L1_attn_all = _L1_attn_setup()
    _L1_attn_in = {k: v for k, v in _L1_attn_all.items() if k in ('a_params', 'B_w', 'C_w', 'D')}
    del _L1_attn_all

    def _L1_ffn_setup():
        import jax, jax.numpy as jnp
        import numpy as np
        D_MODEL = 256
        N_HEADS = 16
        N_GROUPS = 4
        D_FF = 1024
        N_EXPERTS = 8
        TOP_K = 2
        BATCH = 2
        SEQ = 256
        D_K = D_MODEL // N_HEADS
        HPG = N_HEADS // N_GROUPS
        EPS = 1e-06

        def rms_norm(x, w):
            rms = jnp.sqrt(jnp.mean(x * x, axis=-1, keepdims=True) + EPS)
            return x / rms * w

        def rope(x):
            d = x.shape[-1]
            half = d // 2
            theta = 1.0 / 10000.0 ** (jnp.arange(half, dtype=jnp.float32) / half)
            pos = jnp.arange(x.shape[1], dtype=jnp.float32)[:, None]
            ang = pos * theta[None, :]
            cos, sin = (jnp.cos(ang), jnp.sin(ang))
            xe, xo = (x[..., 0::2], x[..., 1::2])
            return jnp.concatenate([xe * cos - xo * sin, xe * sin + xo * cos], axis=-1)

        def attention(x, Wq, Wk, Wv, Wo):
            B, S, _ = x.shape
            xr = rope(x)
            Q = (xr @ Wq).reshape(B, S, N_HEADS, D_K).transpose(0, 2, 1, 3)
            Q = Q.reshape(B, N_GROUPS, HPG, S, D_K)
            K = (xr @ Wk).reshape(B, S, N_GROUPS, D_K).transpose(0, 2, 1, 3)
            V = (xr @ Wv).reshape(B, S, N_GROUPS, D_K).transpose(0, 2, 1, 3)
            scores = jnp.einsum('bghsd,bgtd->bghst', Q, K) / jnp.sqrt(jnp.float32(D_K))
            mask = jnp.triu(jnp.full((S, S), -1000000000.0, dtype=scores.dtype), k=1)
            attn = jax.nn.softmax(scores + mask, axis=-1)
            out = jnp.einsum('bghst,bgtd->bghsd', attn, V)
            out = out.reshape(B, N_HEADS, S, D_K).transpose(0, 2, 1, 3).reshape(B, S, D_MODEL)
            return out @ Wo

        def moe(x, router_w, router_b, W1, b1, W2, b2, W3, b3):
            B, S, _ = x.shape
            logits = x @ router_w + router_b
            topv, topi = jax.lax.top_k(logits, TOP_K)
            topw = jax.nn.softmax(topv, axis=-1)
            onehot = jax.nn.one_hot(topi, N_EXPERTS, dtype=x.dtype)
            comb = jnp.einsum('bsk,bske->bse', topw, onehot)
            h1 = jnp.einsum('bsd,edf->ebsf', x, W1) + b1[:, None, None, :]
            h2 = jnp.einsum('bsd,edf->ebsf', x, W2) + b2[:, None, None, :]
            h = h2 * jax.nn.silu(h1)
            eo = jnp.einsum('ebsf,efd->ebsd', h, W3) + b3[:, None, None, :]
            return jnp.einsum('bse,ebsd->bsd', comb, eo)
        key = jax.random.key(seed)
        ks = jax.random.split(key, 16)
        s = 0.02
        return {'x': jax.random.normal(ks[0], (BATCH, SEQ, D_MODEL), dtype=jnp.float32), 'norm1_w': jnp.ones((D_MODEL,), jnp.float32), 'Wq': jax.random.normal(ks[1], (D_MODEL, D_MODEL), jnp.float32) * s, 'Wk': jax.random.normal(ks[2], (D_MODEL, N_GROUPS * D_K), jnp.float32) * s, 'Wv': jax.random.normal(ks[3], (D_MODEL, N_GROUPS * D_K), jnp.float32) * s, 'Wo': jax.random.normal(ks[4], (D_MODEL, D_MODEL), jnp.float32) * s, 'norm2_w': jnp.ones((D_MODEL,), jnp.float32), 'router_w': jax.random.normal(ks[5], (D_MODEL, N_EXPERTS), jnp.float32) * s, 'router_b': jnp.zeros((N_EXPERTS,), jnp.float32), 'W1': jax.random.normal(ks[6], (N_EXPERTS, D_MODEL, D_FF), jnp.float32) * s, 'b1': jnp.zeros((N_EXPERTS, D_FF), jnp.float32), 'W2': jax.random.normal(ks[7], (N_EXPERTS, D_MODEL, D_FF), jnp.float32) * s, 'b2': jnp.zeros((N_EXPERTS, D_FF), jnp.float32), 'W3': jax.random.normal(ks[8], (N_EXPERTS, D_FF, D_MODEL), jnp.float32) * s, 'b3': jnp.zeros((N_EXPERTS, D_MODEL), jnp.float32)}
    _L1_ffn_all = _L1_ffn_setup()
    _L1_ffn_in = {k: v for k, v in _L1_ffn_all.items() if k in ('norm1_w', 'Wq', 'Wk', 'Wv', 'Wo', 'norm2_w', 'router_w', 'router_b', 'W1', 'b1', 'W2', 'b2', 'W3', 'b3')}
    del _L1_ffn_all
    return {'x': x, 'ctx_1024': ctx_1024, 'fside_BxSxS2_0': fside_BxSxS2_0, 'mask_BxSxS2_ik1': mask_BxSxS2_ik1, 'L0_xattn_wq_k': _L0_xattn_in['wq_k'], 'L0_xattn_wq_b': _L0_xattn_in['wq_b'], 'L0_xattn_wk_k': _L0_xattn_in['wk_k'], 'L0_xattn_wk_b': _L0_xattn_in['wk_b'], 'L0_xattn_wv_k': _L0_xattn_in['wv_k'], 'L0_xattn_wv_b': _L0_xattn_in['wv_b'], 'L0_xattn_wo_k': _L0_xattn_in['wo_k'], 'L0_xattn_wo_b': _L0_xattn_in['wo_b'], 'L0_attn_Wq': _L0_attn_in['Wq'], 'L0_attn_bq': _L0_attn_in['bq'], 'L0_attn_Wk': _L0_attn_in['Wk'], 'L0_attn_bk': _L0_attn_in['bk'], 'L0_attn_Wv': _L0_attn_in['Wv'], 'L0_attn_bv': _L0_attn_in['bv'], 'L0_attn_Wr': _L0_attn_in['Wr'], 'L0_attn_br': _L0_attn_in['br'], 'L0_attn_Wo': _L0_attn_in['Wo'], 'L0_attn_bo': _L0_attn_in['bo'], 'L0_ffn_gate_w': _L0_ffn_in['gate_w'], 'L0_ffn_gate_b': _L0_ffn_in['gate_b'], 'L0_ffn_expert_w': _L0_ffn_in['expert_w'], 'L0_ffn_expert_b': _L0_ffn_in['expert_b'], 'L1_xattn_W_q': _L1_xattn_in['W_q'], 'L1_xattn_b_q': _L1_xattn_in['b_q'], 'L1_xattn_W_k': _L1_xattn_in['W_k'], 'L1_xattn_b_k': _L1_xattn_in['b_k'], 'L1_xattn_W_v': _L1_xattn_in['W_v'], 'L1_xattn_b_v': _L1_xattn_in['b_v'], 'L1_xattn_W_o': _L1_xattn_in['W_o'], 'L1_xattn_b_o': _L1_xattn_in['b_o'], 'L1_attn_a_params': _L1_attn_in['a_params'], 'L1_attn_B_w': _L1_attn_in['B_w'], 'L1_attn_C_w': _L1_attn_in['C_w'], 'L1_attn_D': _L1_attn_in['D'], 'L1_ffn_norm1_w': _L1_ffn_in['norm1_w'], 'L1_ffn_Wq': _L1_ffn_in['Wq'], 'L1_ffn_Wk': _L1_ffn_in['Wk'], 'L1_ffn_Wv': _L1_ffn_in['Wv'], 'L1_ffn_Wo': _L1_ffn_in['Wo'], 'L1_ffn_norm2_w': _L1_ffn_in['norm2_w'], 'L1_ffn_router_w': _L1_ffn_in['router_w'], 'L1_ffn_router_b': _L1_ffn_in['router_b'], 'L1_ffn_W1': _L1_ffn_in['W1'], 'L1_ffn_b1': _L1_ffn_in['b1'], 'L1_ffn_W2': _L1_ffn_in['W2'], 'L1_ffn_b2': _L1_ffn_in['b2'], 'L1_ffn_W3': _L1_ffn_in['W3'], 'L1_ffn_b3': _L1_ffn_in['b3']}

def reference(x, ctx_1024, fside_BxSxS2_0, mask_BxSxS2_ik1, L0_xattn_wq_k, L0_xattn_wq_b, L0_xattn_wk_k, L0_xattn_wk_b, L0_xattn_wv_k, L0_xattn_wv_b, L0_xattn_wo_k, L0_xattn_wo_b, L0_attn_Wq, L0_attn_bq, L0_attn_Wk, L0_attn_bk, L0_attn_Wv, L0_attn_bv, L0_attn_Wr, L0_attn_br, L0_attn_Wo, L0_attn_bo, L0_ffn_gate_w, L0_ffn_gate_b, L0_ffn_expert_w, L0_ffn_expert_b, L1_xattn_W_q, L1_xattn_b_q, L1_xattn_W_k, L1_xattn_b_k, L1_xattn_W_v, L1_xattn_b_v, L1_xattn_W_o, L1_xattn_b_o, L1_attn_a_params, L1_attn_B_w, L1_attn_C_w, L1_attn_D, L1_ffn_norm1_w, L1_ffn_Wq, L1_ffn_Wk, L1_ffn_Wv, L1_ffn_Wo, L1_ffn_norm2_w, L1_ffn_router_w, L1_ffn_router_b, L1_ffn_W1, L1_ffn_b1, L1_ffn_W2, L1_ffn_b2, L1_ffn_W3, L1_ffn_b3):
    import jax
    import jax.numpy as jnp

    def _L0_xattn_ref(query, key_in, value, group_prob, mask, wq_k, wq_b, wk_k, wk_b, wv_k, wv_b, wo_k, wo_b):
        import jax, jax.numpy as jnp
        import numpy as np
        NUM_HEADS = 16
        HIDDEN = 256
        B, S = (2, 512)

        def _split_heads(x, H):
            b, s, d = x.shape
            return x.reshape(b, s, H, d // H).transpose(0, 2, 1, 3)
        H = NUM_HEADS
        dh = query.shape[-1] // H
        q = _split_heads(query @ wq_k + wq_b, H)
        k = _split_heads(key_in @ wk_k + wk_b, H)
        v = _split_heads(value @ wv_k + wv_b, H)
        logits = jnp.einsum('bhqd,bhkd->bhqk', q, k) / jnp.sqrt(jnp.asarray(dh, q.dtype))
        neg = (1.0 - mask.astype(q.dtype)) * -1000000000.0
        logits = logits + neg[:, None, :, :]
        attn = jax.nn.softmax(logits, axis=-1)
        attn = attn * group_prob[:, None, :, :]
        out = jnp.einsum('bhqk,bhkd->bhqd', attn, v)
        out = out.transpose(0, 2, 1, 3).reshape(query.shape[0], -1, H * dh)
        return out @ wo_k + wo_b

    def _L0_attn_ref(x, Wq, bq, Wk, bk, Wv, bv, Wr, br, Wo, bo):
        import jax, jax.numpy as jnp
        import numpy as np
        import math
        D_MODEL = 256
        N_HEADS = 16
        HEAD_DIM = D_MODEL // N_HEADS
        ROT_DIM = min(32, D_MODEL // 4)

        def _xavier(key, fan_in, fan_out):
            lim = math.sqrt(6.0 / (fan_in + fan_out))
            return jax.random.uniform(key, (fan_in, fan_out), jnp.float32, -lim, lim)
        B, S, _ = x.shape
        H, Dh, Dr = (N_HEADS, HEAD_DIM, ROT_DIM)
        q = (x @ Wq + bq).reshape(B, S, H, Dh)
        k = (x @ Wk + bk).reshape(B, S, H, Dh)
        v = (x @ Wv + bv).reshape(B, S, H, Dh)
        r = (x @ Wr + br).reshape(B, S, H, Dr)
        q = jnp.concatenate([q, r], axis=-1)
        k = jnp.concatenate([k, r], axis=-1)
        scale = 1.0 / math.sqrt(Dh + Dr)
        scores = jnp.einsum('bqhd,bkhd->bhqk', q * scale, k)
        attn = jax.nn.softmax(scores, axis=-1)
        out = jnp.einsum('bhqk,bkhd->bqhd', attn, v).reshape(B, S, H * Dh)
        return out @ Wo + bo

    def _L0_ffn_ref(x, gate_w, gate_b, expert_w, expert_b):
        import jax, jax.numpy as jnp
        import numpy as np
        TOP_K = 2
        gate = jnp.einsum('bsd,ed->bse', x, gate_w) + gate_b
        _, idx = jax.lax.top_k(gate, TOP_K)
        E = gate_w.shape[0]
        flat_idx = idx.reshape(-1)
        counts = jnp.zeros((E,), dtype=x.dtype).at[flat_idx].add(1.0)
        expert_out = jax.nn.relu(jnp.einsum('bsd,ehd->bseh', x, expert_w) + expert_b)
        total = flat_idx.size
        out = jnp.einsum('bseh,e->bsh', expert_out, counts) / total
        return out

    def _L1_xattn_ref(tgt, memory, W_q, b_q, W_k, b_k, W_v, b_v, W_o, b_o):
        import jax, jax.numpy as jnp
        import numpy as np
        D_MODEL = 256
        H = 16
        D_H = D_MODEL // H
        B, T_dec, _ = tgt.shape
        T_enc = memory.shape[1]
        Q = tgt @ W_q + b_q
        K = memory @ W_k + b_k
        V = memory @ W_v + b_v
        Q = Q.reshape(B, T_dec, H, D_H).transpose(0, 2, 1, 3)
        K = K.reshape(B, T_enc, H, D_H).transpose(0, 2, 1, 3)
        V = V.reshape(B, T_enc, H, D_H).transpose(0, 2, 1, 3)
        S = jnp.einsum('bhqd,bhkd->bhqk', Q, K) / jnp.sqrt(jnp.float32(D_H)).astype(Q.dtype)
        A = jax.nn.softmax(S, axis=-1)
        Y = jnp.einsum('bhqk,bhkd->bhqd', A, V)
        Y = Y.transpose(0, 2, 1, 3).reshape(B, T_dec, D_MODEL)
        return Y @ W_o + b_o

    def _L1_attn_ref(u, a_params, B_w, C_w, D):
        import jax, jax.numpy as jnp
        import numpy as np
        BATCH, SEQ, D_MODEL, STATE_DIM = (8, 512, 256, 256)

        def _cayley_circulant_eigenvalues(a_params, n):
            half_n = n // 2
            a_full = jnp.zeros((n,), dtype=a_params.dtype)
            a_full = a_full.at[1:half_n].set(a_params[:half_n - 1])
            a_full = a_full.at[half_n + 1:].set(-a_params[:half_n - 1][::-1])
            omega = jnp.fft.fft(a_full).imag
            w2 = omega * omega
            denom = 1.0 + w2
            return ((1.0 - w2) / denom + 1j * (-2.0 * omega / denom)).astype(jnp.complex64)
        n = B_w.shape[0]
        lambdas = _cayley_circulant_eigenvalues(a_params, n)
        Bu = jnp.einsum('bsd,nd->bsn', u, B_w)

        def step(h, bu_t):
            Wh = jnp.fft.ifft(lambdas * jnp.fft.fft(h.astype(jnp.float32))).real.astype(h.dtype)
            h_new = Wh + bu_t
            return (h_new, h_new)
        h0 = jnp.zeros((u.shape[0], n), dtype=u.dtype)
        _, hs = jax.lax.scan(step, h0, jnp.swapaxes(Bu, 0, 1))
        y = jnp.einsum('sbn,dn->bsd', hs, C_w) + D * u
        return y

    def _L1_ffn_ref(x, norm1_w, Wq, Wk, Wv, Wo, norm2_w, router_w, router_b, W1, b1, W2, b2, W3, b3):
        import jax, jax.numpy as jnp
        import numpy as np
        D_MODEL = 256
        N_HEADS = 16
        N_GROUPS = 4
        D_FF = 1024
        N_EXPERTS = 8
        TOP_K = 2
        BATCH = 2
        SEQ = 256
        D_K = D_MODEL // N_HEADS
        HPG = N_HEADS // N_GROUPS
        EPS = 1e-06

        def rms_norm(x, w):
            rms = jnp.sqrt(jnp.mean(x * x, axis=-1, keepdims=True) + EPS)
            return x / rms * w

        def rope(x):
            d = x.shape[-1]
            half = d // 2
            theta = 1.0 / 10000.0 ** (jnp.arange(half, dtype=jnp.float32) / half)
            pos = jnp.arange(x.shape[1], dtype=jnp.float32)[:, None]
            ang = pos * theta[None, :]
            cos, sin = (jnp.cos(ang), jnp.sin(ang))
            xe, xo = (x[..., 0::2], x[..., 1::2])
            return jnp.concatenate([xe * cos - xo * sin, xe * sin + xo * cos], axis=-1)

        def attention(x, Wq, Wk, Wv, Wo):
            B, S, _ = x.shape
            xr = rope(x)
            Q = (xr @ Wq).reshape(B, S, N_HEADS, D_K).transpose(0, 2, 1, 3)
            Q = Q.reshape(B, N_GROUPS, HPG, S, D_K)
            K = (xr @ Wk).reshape(B, S, N_GROUPS, D_K).transpose(0, 2, 1, 3)
            V = (xr @ Wv).reshape(B, S, N_GROUPS, D_K).transpose(0, 2, 1, 3)
            scores = jnp.einsum('bghsd,bgtd->bghst', Q, K) / jnp.sqrt(jnp.float32(D_K))
            mask = jnp.triu(jnp.full((S, S), -1000000000.0, dtype=scores.dtype), k=1)
            attn = jax.nn.softmax(scores + mask, axis=-1)
            out = jnp.einsum('bghst,bgtd->bghsd', attn, V)
            out = out.reshape(B, N_HEADS, S, D_K).transpose(0, 2, 1, 3).reshape(B, S, D_MODEL)
            return out @ Wo

        def moe(x, router_w, router_b, W1, b1, W2, b2, W3, b3):
            B, S, _ = x.shape
            logits = x @ router_w + router_b
            topv, topi = jax.lax.top_k(logits, TOP_K)
            topw = jax.nn.softmax(topv, axis=-1)
            onehot = jax.nn.one_hot(topi, N_EXPERTS, dtype=x.dtype)
            comb = jnp.einsum('bsk,bske->bse', topw, onehot)
            h1 = jnp.einsum('bsd,edf->ebsf', x, W1) + b1[:, None, None, :]
            h2 = jnp.einsum('bsd,edf->ebsf', x, W2) + b2[:, None, None, :]
            h = h2 * jax.nn.silu(h1)
            eo = jnp.einsum('ebsf,efd->ebsd', h, W3) + b3[:, None, None, :]
            return jnp.einsum('bse,ebsd->bsd', comb, eo)
        h = x + attention(rms_norm(x, norm1_w), Wq, Wk, Wv, Wo)
        h = h + moe(rms_norm(h, norm2_w), router_w, router_b, W1, b1, W2, b2, W3, b3)
        return h
    x = x + _L0_xattn_ref(_layernorm(x, axis=-1), ctx_1024, ctx_1024, fside_BxSxS2_0, mask_BxSxS2_ik1, L0_xattn_wq_k, L0_xattn_wq_b, L0_xattn_wk_k, L0_xattn_wk_b, L0_xattn_wv_k, L0_xattn_wv_b, L0_xattn_wo_k, L0_xattn_wo_b)
    x = x + _L0_attn_ref(_layernorm(x, axis=-1), L0_attn_Wq, L0_attn_bq, L0_attn_Wk, L0_attn_bk, L0_attn_Wv, L0_attn_bv, L0_attn_Wr, L0_attn_br, L0_attn_Wo, L0_attn_bo)
    x = x + _L0_ffn_ref(_layernorm(x, axis=-1), L0_ffn_gate_w, L0_ffn_gate_b, L0_ffn_expert_w, L0_ffn_expert_b)
    x = x + _L1_xattn_ref(_layernorm(x, axis=-1), ctx_1024, L1_xattn_W_q, L1_xattn_b_q, L1_xattn_W_k, L1_xattn_b_k, L1_xattn_W_v, L1_xattn_b_v, L1_xattn_W_o, L1_xattn_b_o)
    x = x + _L1_attn_ref(_layernorm(x, axis=-1), L1_attn_a_params, L1_attn_B_w, L1_attn_C_w, L1_attn_D)
    x = x + _L1_ffn_ref(_layernorm(x, axis=-1), L1_ffn_norm1_w, L1_ffn_Wq, L1_ffn_Wk, L1_ffn_Wv, L1_ffn_Wo, L1_ffn_norm2_w, L1_ffn_router_w, L1_ffn_router_b, L1_ffn_W1, L1_ffn_b1, L1_ffn_W2, L1_ffn_b2, L1_ffn_W3, L1_ffn_b3)
    return x

_drawn_inputs = setup_inputs


def setup_inputs(seed=0):
    import zlib

    import numpy as np

    out = dict(_drawn_inputs(seed))
    spreads = {'L0_xattn_wq_b': (0.0, 0.631),
     'L0_xattn_wk_b': (0.0, 2.0),
     'L0_xattn_wv_b': (0.0, 0.1),
     'L0_xattn_wo_b': (0.0, 0.1),
     'L0_attn_bq': (0.0, 0.8),
     'L0_attn_bk': (0.0, 2.0),
     'L0_attn_bv': (0.0, 0.1),
     'L0_attn_br': (0.0, 0.735),
     'L0_attn_bo': (0.0, 0.1),
     'L0_ffn_gate_b': (0.0, 0.47),
     'L0_ffn_expert_b': (0.0, 0.393),
     'L1_xattn_b_q': (0.0, 0.42),
     'L1_xattn_b_k': (0.0, 2.0),
     'L1_xattn_b_v': (0.0, 0.1),
     'L1_xattn_b_o': (0.0, 0.1),
     'L1_attn_D': (0.0, 0.516),
     'L1_ffn_norm1_w': (1.0, 0.6),
     'L1_ffn_norm2_w': (1.0, 0.6),
     'L1_ffn_router_b': (0.0, 0.8),
     'L1_ffn_b1': (0.0, 0.8),
     'L1_ffn_b2': (0.0, 0.8),
     'L1_ffn_b3': (0.0, 2.0)}
    factors = {'L1_ffn_Wq': 8.0,
     'L1_ffn_Wk': 8.0,
     'L1_ffn_Wv': 8.0,
     'L1_ffn_Wo': 8.0,
     'L1_ffn_router_w': 6.163,
     'L1_ffn_W1': 8.0,
     'L1_ffn_W2': 8.0,
     'L1_ffn_W3': 8.0}
    for name, (base, spread) in spreads.items():
        noise = np.random.default_rng([zlib.crc32(name.encode()), seed]).standard_normal(out[name].shape)
        drawn = base * np.exp(spread * noise) if base else spread * noise
        out[name] = jnp.asarray(drawn.astype(out[name].dtype))
    for name, factor in factors.items():
        out[name] = (out[name] * factor).astype(out[name].dtype)
    return out
```

```python
from contextlib import ExitStack

import numpy as np

import concourse.bass as bass
from concourse import mybir

F32 = mybir.dt.float32
I32 = mybir.dt.int32
U32 = mybir.dt.uint32
ALU = mybir.AluOpType
ACT = mybir.ActivationFunctionType
AX = mybir.AxisListType

P = 128
SEQS, SEQ, D = 16, 64, 256
KEYS = 256
TOKENS = SEQS * SEQ
TILES = TOKENS // P
DC = D // P
HEADS, DH = 16, 16
PAIRS = HEADS // 2
ROT = 32
EXPERTS = 8
FF = 1024
FT = FF // P
CHUNK = 512
CHUNKS = TOKENS // CHUNK
LN_EPS, RMS_EPS = 1e-5, 1e-6
CREDIT = 1
BIG = 3.0e38

SA_ROWS = 2 * DH + 2 * ROT
LA_ROWS = 2 * DH

PACKS = {
    "const": {"ident": P, "par_x": 2, "par_s": 2, "iota": 8, "causal": SEQ, "tri": P, "cos": P, "sin": P},
    "xa0": {"wq": 512, "wk": 512, "wv": 512, "wo": 512, "bq": 2, "bk": 2, "bv": D, "bo": D},
    "sa": {"w": 2048, "wv": 512, "wo": 512, "b": 8, "bv": D, "bo": D},
    "ffn": {"gate_w": 16, "gate_b": 1, "we": 4096, "be": 16},
    "xa1": {"wq": 512, "wk": 512, "wv": 512, "wo": 512, "bq": 2, "bk": 2, "bv": D, "bo": D},
    "ssm": {"bw": 512, "ct": 512, "a": 1, "d": D},
    "four": {"fwd": 512, "inv": 512, "sines": P},
    "la": {"w": 1024, "wv": 512, "wo": 512, "norm1": D, "norm2": D},
    "moe": {"router_w": 16, "router_b": 1, "b1": 64, "b2": 64, "b3": D},
}


EARLY = ("xa0", "sa", "ffn")


def hold(eng, sem, n):
    if isinstance(n, int) and n <= 0:
        return
    eng.wait_ge(sem, n + CREDIT)


def at_most(n, top):
    return min(n, top) if isinstance(n, int) else n


def skewed(eng, n, lag, step, unroll=2):
    for k in range(unroll):
        step(k, k % unroll, k // unroll)
    with eng.Fori(1, n // unroll) as h:
        for s in range(unroll):
            step(unroll * h + s, s, h)
    for k in range(n, n + lag):
        step(k, k % unroll, k // unroll)


def live(k, lag, n):
    return 0 <= k - lag < n if isinstance(k, int) else True


class Chain:

    def __init__(self, eng, sem):
        self.eng, self.sem, self.n = eng, sem, 0

    def link(self, ins):
        ins.then_inc(self.sem, 1)
        self.n += 1
        self.eng.wait_ge(self.sem, self.n)

    def mark(self, ins):
        ins.then_inc(self.sem, 1)
        self.n += 1

    def join(self):
        self.eng.wait_ge(self.sem, self.n)

    def restart(self):
        if self.n:
            self.join()
            self.eng.sem_clear(self.sem)
            self.n = 0


def build(nc, t, upto=9):
    ctx = ExitStack()
    with ctx:
        def sb(name, cols, dt=F32):
            return ctx.enter_context(nc.sbuf_tensor(name, [P, cols], dt))

        def sem(name):
            return ctx.enter_context(nc.semaphore(name))

        W = {}
        early = sb("early", sum(sum(PACKS[pack].values()) for pack in EARLY))
        taken = 0
        for pack, fields in PACKS.items():
            cols = sum(fields.values())
            if pack in EARLY:
                whole = early[:, taken:taken + cols]
                taken += cols
            else:
                whole = sb("pack_" + pack, cols)[:, :]
            W[pack] = {"whole": whole}
            at = 0
            for name, cols in fields.items():
                W[pack][name] = whole[:, at:at + cols]
                at += cols

        def kc(ap, n):
            return ap.rearrange("p (c n) -> p c n", n=n)

        ident = W["const"]["ident"]
        x = sb("x", TILES * D)
        xn_all = sb("xn_all", TILES * D)
        xt_all = sb("xt_all", DC * TOKENS)
        XT = xt_all[:, :].rearrange("p (c n) -> p c n", c=DC)
        xn = sb("xn", D)
        stat6 = sb("stat6", 6)
        mv = sb("mv", 2)
        var = sb("var", 1)
        rstd = sb("rstd", 1)
        half = sb("half", 3)
        junk = sb("junk", D)
        probs = sb("probs", 2 * PAIRS * KEYS)
        pt = sb("pt", 2 * PAIRS * 2 * P)
        ctx_t = sb("ctx_t", 2 * DC * KEYS)
        gp = sb("gp", 2 * KEYS)
        mask_i = sb("mask_i", 2 * KEYS, I32)
        neg = sb("neg", 2 * KEYS)
        kbuf = sb("kbuf", 2 * 1024)
        vbuf = sb("vbuf", 2 * 512)
        qbuf = sb("qbuf", 2 * 2048)
        mx = sb("mx", 2 * HEADS)
        ssum = sb("ssum", 2 * HEADS)
        rsum = sb("rsum", 2 * HEADS)
        obuf = sb("obuf", 2 * 2 * P)
        ot = sb("ot", 2 * P)
        xs = sb("xs", 2 * DC * P)
        acc = sb("acc", 2 * DC * P)
        relu = sb("relu", 4 * P)
        bqm = sb("bqm", 2 * PAIRS)
        counts = sb("counts", EXPERTS)
        bec = sb("bec", 2 * EXPERTS)
        top = sb("top", TILES * 8)
        topi = sb("topi", TILES * 8, U32)
        topf = sb("topf", TILES * 8)
        hot = sb("hot", TILES * EXPERTS)
        hot2 = sb("hot2", TILES * EXPERTS)
        logit = sb("logit", TILES * EXPERTS)
        gateT = sb("gateT", TOKENS)
        ones = sb("ones", P)
        wb = sb("wb", DC * D)
        cg = sb("cg", DC * D)
        lam = sb("lam", 8)
        tabR = sb("tabR", 2 * SEQ)
        tabI = sb("tabI", 2 * SEQ)
        tabt = sb("tabt", SEQ)
        rowR = sb("rowR", P)
        rowI = sb("rowI", P)
        rot = sb("rot", 2 * D)
        rot2 = sb("rot2", 2 * D)
        comb = sb("comb", TILES * EXPERTS)
        combT = gateT
        wgt = sb("wgt", TILES * 4)
        wide = DC * 2 * FF
        w12 = [early[:, i * wide:(i + 1) * wide] for i in range(2)]
        w3 = [early[:, 2 * wide:2 * wide + FT * D], sb("w3_1", FT * D)[:, :]]
        gated = ctx_t
        hid = [probs[:, :].rearrange("p (f n) -> p f n", f=FT), pt[:, :].rearrange("p (f n) -> p f n", f=FT)]

        ps = ctx.enter_context(nc.psum_tensor("ps", [P, 8 * 512], F32))
        S = ps[:, 0:2048]
        AB = ps[:, 2048:3072]
        M = ps[:, 3072:3584]
        C = ps[:, 3584:4096]
        sums = [ps[:, o:o + D] for o in (2048, 2560, 3072, 3584)]

        credited = []

        def group(prefix, names):
            g = {n: sem(f"{prefix}_{n}") for n in names.split()}
            credited.extend(g.values())
            return g

        tail_names = " o_turned o_copied projected biased resid stats rstd normed turned xt"
        x_names = "k_projected v_projected q_projected k_copied v_copied q_copied scored masked exped weighted " \
                  "p_turned pt_a pt_b pv_done o_normed" + tail_names
        s_names = "x_copied qk_projected v_projected qk_copied v_copied scored shifted exped p_turned pt_copied " \
                  "pv_done o_normed" + tail_names
        G = {
            "ln": group("ln", "stats rstd normed turned xt"),
            "xa0": group("xa0", x_names),
            "sa": group("sa", s_names),
            "ffn": group("ffn", "expert relued added projected resid stats rstd normed turned xt"),
            "xa1": group("xa1", x_names.replace(" masked", "") + " kept"),
            "ssm": group("ssm", "x_copied v_projected rotated summed modulated projected biased resid stats rstd normed"),
            "rope": group("rope", "squared rms roped turned xt"),
            "la": group("la", s_names.replace(" stats", "").replace(" biased", "") + " squared added"),
            "moe": group("moe", "hidden silued gated expert out"),
        }
        loads = {"first": ["x", "const"], "xa0": ["xa0"], "sa": ["sa"], "ffn": ["ffn"], "ssm": ["four", "ssm"],
                 "late": ["xa1", "la", "moe"]}
        load_sems = {name: sem(f"loaded_{name}") for name in loads}
        loaded = {a: (load_sems[name], 16 * len(of)) for name, of in loads.items() for a in of}
        ctx_loaded = [sem(f"ctx_loaded{s}") for s in range(2)]

        def ctx_count(st, h):
            return 80 * (h + 1) if st == "xa0" else 80 * (SEQS // 2) + 16 * (h + 1)

        neg_ready = sem("neg_ready")
        credited.append(neg_ready)
        w_loaded = [sem(f"w_loaded{s}") for s in range(2)]
        dve_chain, pool_chain = sem("dve_chain"), sem("pool_chain")
        dve_passed, pool_passed, act_passed = sem("dve_passed"), sem("pool_passed"), sem("act_passed")
        made = sem("made")
        prep_mm, prep_dve, prep_act = sem("prep_mm"), sem("prep_dve"), sem("prep_act")
        final_ready = G["moe"]["out"]
        stored = sem("stored")

        block = ctx.enter_context(nc.Block())

        def tile(ap, h):
            return ap[:, bass.ts(h, D)]

        XA = ["xa0", "xa1"]
        PREV = {"xa0": "ln", "sa": "xa0", "ffn": "sa", "xa1": "ffn", "ssm": "xa1", "rope": "ssm", "la": "rope"}
        ORDER = ["ln", "xa0", "sa", "ffn", "xa1", "ssm", "rope", "la", "moe"]
        RUN = ORDER[:upto]

        @block.sync
        def _(sp):
            for s_ in credited:
                sp.sem_inc(s_, CREDIT)
            sp.dma_start(x[:, :], t["x"]).then_inc(loaded["x"][0], 16)
            for name in ("const", "xa0", "sa", "ffn", "four", "ssm"):
                sp.dma_start(W[name]["whole"], t[name]).then_inc(loaded[name][0], 16)

            def load_context(st, b, s, h):
                g = G[st]
                if not isinstance(b, int) or b >= 2:
                    hold(sp, g["v_projected"], b - 1)
                    if st == "xa0":
                        hold(sp, g["masked"], 8 * (b - 1))
                        hold(sp, g["weighted"], 4 * (b - 1))
                        hold(sp, neg_ready, b - 1)
                c = ctx_t[:, s * DC * KEYS:(s + 1) * DC * KEYS]
                done = ctx_loaded[s]
                src = t["ctx"][bass.ds(b, 1), :, :].rearrange("b p n -> (b p) n")
                sp.dma_start(c, src).then_inc(done, 16)
                if st == "xa0":
                    for r in range(2):
                        gsrc = t["gp"][bass.ds(b, 1), :, :].rearrange("b p n -> (b p) n")
                        msrc = t["mask"][bass.ds(b, 1), :, :].rearrange("b p n -> (b p) n")
                        sp.dma_start(gp[r * SEQ:(r + 1) * SEQ, s * KEYS:(s + 1) * KEYS], gsrc).then_inc(done, 16)
                        sp.dma_start(mask_i[r * SEQ:(r + 1) * SEQ, s * KEYS:(s + 1) * KEYS], msrc).then_inc(done, 16)

            if "xa0" in RUN:
                skewed(sp, SEQS, 0, lambda k, s, h: load_context("xa0", k, s, h))
            for name in ("xa1", "la", "moe"):
                sp.dma_start(W[name]["whole"], t[name]).then_inc(loaded[name][0], 16)
            if "xa1" in RUN:
                hold(sp, G["xa0"]["v_projected"], SEQS)
                skewed(sp, SEQS, 0, lambda k, s, h: load_context("xa1", k, s, h))
            if "moe" in RUN:
                def load_expert(e, s, h):
                    if not isinstance(e, int) or e >= 2:
                        hold(sp, G["moe"]["expert"], 8 * (e - 1))
                    a = t["w12"][bass.ds(e, 1), :, :].rearrange("b p n -> (b p) n")
                    b = t["w3"][bass.ds(e, 1), :, :].rearrange("b p n -> (b p) n")
                    sp.dma_start(w12[s], a).then_inc(w_loaded[s], 16)
                    sp.dma_start(w3[s], b).then_inc(w_loaded[s], 16)
                hold(sp, G["ffn"]["xt"], TILES)
                skewed(sp, EXPERTS, 0, load_expert)
                hold(sp, final_ready, 4 * CHUNKS * EXPERTS)
            else:
                last = {"ln": ("ln", "xt"), "rope": ("rope", "xt"), "ssm": ("ssm", "normed"), "la": ("la", "xt")}
                a, b = last.get(RUN[-1], (RUN[-1], "xt"))
                hold(sp, G[a][b], TILES)
                if RUN[-1] == "la":
                    hold(sp, G["la"]["added"], TILES)
            sp.dma_start(t["out"], x[:, :]).then_inc(stored, 16)
            sp.wait_ge(stored, 16)

        @block.tensor
        def _(pe):
            pe.wait_ge(*loaded["const"])

            def turn_rows(g, h):
                hold(pe, g["normed"], h + 1)
                for c in range(DC):
                    last = pe.transpose(C[:, c * P:(c + 1) * P], xn[:, c * P:(c + 1) * P], ident)
                last.then_inc(g["turned"], 1)

            def turn_outputs(g, h, per_tile, base):
                hold(pe, g["o_normed"], per_tile * (h + 1))
                hold(pe, g["xt"], h)
                for b in range(2):
                    last = pe.transpose(C[:, b * P:(b + 1) * P], obuf[:, base + b * P:base + (b + 1) * P], ident)
                last.then_inc(g["o_turned"], 1)

            def out_project(g, h, wo, dst):
                hold(pe, g["o_copied"], h + 1)
                hold(pe, g["resid"], h)
                for par in range(2):
                    last = pe.matmul(dst, ot[:, par * P:(par + 1) * P], kc(wo, D)[:, par, :],
                                     start=par == 0, stop=par == 1)
                last.then_inc(g["projected"], 1)

            def ln_step(k, s, h):
                hold(pe, G["ln"]["xt"], k)
                turn_rows(G["ln"], k)
            skewed(pe, TILES, 0, ln_step)

            def cross(st):
                g, w = G[st], W[st]
                wq, wk, wv = kc(w["wq"], D), kc(w["wk"], D), kc(w["wv"], D)
                prev = G[PREV[st]]
                pe.wait_ge(*loaded[st])

                def project(b, s, h):
                    c = ctx_t[:, s * DC * KEYS:(s + 1) * DC * KEYS].rearrange("p (c n) -> p c n", c=DC)
                    pe.wait_ge(ctx_loaded[s], ctx_count(st, h))
                    hold(pe, g["pt_a"], 2 * b - 2)
                    if isinstance(b, int) and b == 1:
                        hold(pe, g["k_copied"], 1)
                    for hf in range(2):
                        for k in range(DC):
                            last = pe.matmul(AB[:, hf * KEYS:(hf + 1) * KEYS], wk[:, k, hf * P:(hf + 1) * P],
                                             c[:, k, :], start=k == 0, stop=k == DC - 1)
                    last.then_inc(g["k_projected"], 1)
                    hold(pe, g["pt_b"], 2 * b - 2)
                    if isinstance(b, int) and b == 1:
                        hold(pe, g["v_copied"], 1)
                    for kt in range(2):
                        for k in range(DC):
                            last = pe.matmul(AB[:, 512 + kt * D:512 + (kt + 1) * D], c[:, k, kt * P:(kt + 1) * P],
                                             wv[:, k, :], start=k == 0, stop=k == DC - 1)
                    last.then_inc(g["v_projected"], 1)
                    hold(pe, prev["xt"], h + 1)
                    hold(pe, g["q_copied"], b)
                    hold(pe, g["o_normed"], b - 1)
                    for hf in range(2):
                        for k in range(DC):
                            last = pe.matmul(M[:, 256 + hf * SEQ:256 + (hf + 1) * SEQ], wq[:, k, hf * P:(hf + 1) * P],
                                             XT[:, k, bass.ts(b, SEQ)], start=k == 0, stop=k == DC - 1)
                    last.then_inc(g["q_projected"], 1)

                def turn_probs(b, s):
                    pr = probs[:, s * 2048:(s + 1) * 2048].rearrange("p (n k) -> p n k", n=PAIRS)
                    for c in range(4):
                        hold(pe, g["weighted"], 4 * b + c + 1)
                        if c == 0:
                            hold(pe, g["k_copied"], at_most(b + 2, SEQS))
                        elif c == 1:
                            hold(pe, g["v_copied"], at_most(b + 2, SEQS))
                        else:
                            hold(pe, g["pt_a" if c == 2 else "pt_b"], 2 * b + 1)
                        for n in range(2):
                            for kt in range(2):
                                o = (c % 2) * 512 + (n * 2 + kt) * P
                                last = pe.transpose(AB[:, o:o + P], pr[:, 2 * c + n, kt * P:(kt + 1) * P], ident)
                        last.then_inc(g["p_turned"], 1)

                def score(b, s):
                    hold(pe, g["q_copied"], b + 1)
                    hold(pe, g["k_copied"], b + 1)
                    if st == "xa0":
                        hold(pe, g["masked"], 8 * b)
                    else:
                        hold(pe, g["weighted"], 4 * b)
                    for hf in range(2):
                        q = qbuf[:, s * 2048 + hf * P:s * 2048 + (hf + 1) * P]
                        kk = kbuf[:, s * 1024 + hf * KEYS:s * 1024 + (hf + 1) * KEYS]
                        for j in range(4):
                            r = slice(32 * j, 32 * j + 32)
                            o = j * 512 + hf * KEYS
                            last = pe.matmul(S[:, o:o + KEYS], q[r, :], kk[r, :], start=True, stop=True)
                    last.then_inc(g["scored"], 1)

                def mix_values(b, s):
                    turned = pt[:, s * 2048:(s + 1) * 2048].rearrange("p (n k q) -> p n k q", n=PAIRS, k=2)
                    v = vbuf[:, s * 512:(s + 1) * 512].rearrange("p (k n) -> p k n", k=2)
                    hold(pe, g["pt_a"], 2 * b + 2)
                    hold(pe, g["pt_b"], 2 * b + 2)
                    hold(pe, g["v_copied"], b + 1)
                    hold(pe, g["o_normed"], b)
                    for n in range(PAIRS):
                        for kt in range(2):
                            last = pe.matmul(M[:, n * 32:(n + 1) * 32], turned[:, n, kt, :],
                                             v[:, kt, n * 32:(n + 1) * 32], start=kt == 0, stop=kt == 1)
                    last.then_inc(g["pv_done"], 1)

                def step(k, s, h):
                    odd_tile = s == 1
                    if live(k, 2, SEQS) and odd_tile:
                        turn_outputs(g, h - 1, 2, 0)
                    if live(k, 0, SEQS):
                        project(k, s, h)
                    if live(k, 1, SEQS):
                        turn_probs(k - 1, 1 - s)
                    if live(k, 2, SEQS) and odd_tile:
                        out_project(g, h - 1, w["wo"], C[:, 256:512])
                    if live(k, 0, SEQS):
                        score(k, s)
                    if live(k, 1, SEQS):
                        mix_values(k - 1, 1 - s)
                    if live(k, 2, SEQS) and odd_tile:
                        turn_rows(g, h - 1)
                skewed(pe, SEQS, 2, step)

            def inner(st, rows):
                g, w = G[st], W[st]
                width = w["w"].shape[1] // (DC * PAIRS)
                wqk = w["w"].rearrange("p (c n m) -> p c n m", c=DC, n=PAIRS)
                wv = kc(w["wv"], D)
                pe.wait_ge(*loaded[st])

                def project(i, s):
                    xt = xs[:, s * D:(s + 1) * D].rearrange("p (c n) -> p c n", c=DC)
                    hold(pe, g["x_copied"], i + 1)
                    hold(pe, g["qk_copied"], i)
                    for n in range(PAIRS):
                        for k in range(DC):
                            last = pe.matmul(S[0:width, 1024 + n * P:1024 + (n + 1) * P], wqk[:, k, n, :], xt[:, k, :],
                                             start=k == 0, stop=k == DC - 1)
                    last.then_inc(g["qk_projected"], 1)
                    hold(pe, g["pt_copied"], i - 1)
                    if isinstance(i, int) and i == 1:
                        hold(pe, g["v_copied"], 1)
                    for k in range(DC):
                        last = pe.matmul(AB[:, 0:D], xt[:, k, :], wv[:, k, :], start=k == 0, stop=k == DC - 1)
                    last.then_inc(g["v_projected"], 1)

                def turn_probs(i, s):
                    pr = probs[:, s * 2048:s * 2048 + 1024]
                    hold(pe, g["exped"], i + 1)
                    hold(pe, g["v_copied"], at_most(i + 2, TILES))
                    hold(pe, g["pt_copied"], i)
                    for n in range(PAIRS):
                        last = pe.transpose(AB[:, n * P:(n + 1) * P], pr[:, n * P:(n + 1) * P], ident)
                    last.then_inc(g["p_turned"], 1)

                def score(i, s):
                    hold(pe, g["qk_copied"], i + 1)
                    hold(pe, g["shifted"], i)
                    for n in range(PAIRS):
                        for b in range(2):
                            q = qbuf[0:rows, s * 2048 + (n * 2 + b) * P:s * 2048 + (n * 2 + b + 1) * P]
                            o = n * P + b * SEQ
                            kk = kbuf[0:rows, s * 1024 + o:s * 1024 + o + SEQ]
                            last = pe.matmul(S[:, o:o + SEQ], q, kk, start=True, stop=True)
                    last.then_inc(g["scored"], 1)

                def mix_values(i, s):
                    hold(pe, g["pt_copied"], i + 1)
                    hold(pe, g["o_normed"], i)
                    hold(pe, g["resid"], i)
                    for b in range(2):
                        dst = M if b == 0 else C[:, 256:512]
                        r = slice(b * SEQ, (b + 1) * SEQ)
                        for n in range(PAIRS):
                            last = pe.matmul(dst[:, n * 32:(n + 1) * 32], pt[r, s * 2048 + n * P:s * 2048 + (n + 1) * P],
                                             vbuf[r, s * 512 + n * 32:s * 512 + (n + 1) * 32], start=True, stop=True)
                    last.then_inc(g["pv_done"], 1)

                def step(k, s, h):
                    if live(k, 2, TILES):
                        turn_outputs(g, k - 2, 1, s * D)
                    if live(k, 0, TILES):
                        project(k, s)
                    if live(k, 1, TILES):
                        turn_probs(k - 1, 1 - s)
                    if live(k, 2, TILES):
                        out_project(g, k - 2, w["wo"], M[:, 256:512])
                    if live(k, 0, TILES):
                        score(k, s)
                    if live(k, 1, TILES):
                        mix_values(k - 1, 1 - s)
                    if live(k, 2, TILES):
                        turn_rows(g, k - 2)
                skewed(pe, TILES, 2, step)

            def choose(w, base):
                for c in range(CHUNKS):
                    for k in range(DC):
                        last = pe.matmul(S[0:EXPERTS, c * 512:(c + 1) * 512], kc(w, 8)[:, k, :],
                                         XT[:, k, c * 512:(c + 1) * 512], start=k == 0, stop=k == DC - 1)
                last.then_inc(prep_mm, 1)
                pe.wait_ge(prep_dve, base)
                for i in range(TILES):
                    last = pe.transpose(S[:, 1024 + i * 8:1024 + (i + 1) * 8], gateT[0:8, i * P:(i + 1) * P],
                                        ident[0:8, 0:8])
                last.then_inc(prep_mm, 1)

            if "xa0" in RUN:
                cross("xa0")
            if "sa" in RUN:
                inner("sa", SA_ROWS)
            if "ffn" in RUN:
                g, w = G["ffn"], W["ffn"]
                pe.wait_ge(*loaded["ffn"])
                hold(pe, G["sa"]["xt"], TILES)
                choose(w["gate_w"], 1)
                pe.wait_ge(prep_dve, 2)
                pe.matmul(S[:, 1280:1288], ones[:, :], hot2[:, 0:8], start=True, stop=True).then_inc(prep_mm, 1)
                we = w["we"].rearrange("p (c e h) -> p c e h", c=DC, e=EXPERTS)

                def experts(i, s):
                    for n in range(2 * EXPERTS):
                        e, hh = n // 2, n % 2
                        hold(pe, g["relued"], 16 * i + n - 3)
                        o = (n % 4) * 512
                        for k in range(DC):
                            last = pe.matmul(S[:, o:o + P], we[:, k, e, hh * P:(hh + 1) * P],
                                             XT[:, k, bass.ts(i, P)], start=k == 0, stop=k == DC - 1)
                        last.then_inc(g["expert"], 1)

                def back(i, s):
                    hold(pe, g["added"], 14 * (i + 1))
                    hold(pe, g["relued"], 16 * (i + 1))
                    hold(pe, g["resid"], i)
                    for hh in range(DC):
                        last = pe.transpose(M[:, 256 + hh * P:256 + (hh + 1) * P],
                                            acc[:, s * D + hh * P:s * D + (hh + 1) * P], ident)
                    last.then_inc(g["projected"], 1)

                pe.wait_ge(prep_dve, 3)

                def step(k, s, h):
                    if live(k, 1, TILES):
                        back(k - 1, 1 - s)
                    if live(k, 0, TILES):
                        experts(k, s)
                    if live(k, 1, TILES):
                        hold(pe, g["xt"], k - 1)
                        turn_rows(g, k - 1)
                skewed(pe, TILES, 1, step)
            if "xa1" in RUN:
                cross("xa1")
            if "ssm" in RUN:
                g, w = G["ssm"], W["ssm"]
                pe.wait_ge(*loaded["ssm"])
                pe.wait_ge(*loaded["four"])
                bw, ct = kc(w["bw"], D), kc(w["ct"], D)
                fwd, inv = kc(W["four"]["fwd"], D), kc(W["four"]["inv"], D)
                hold(pe, G["xa1"]["weighted"], 4 * SEQS)
                for m in range(DC):
                    for k in range(DC):
                        pe.matmul(S[:, m * D:(m + 1) * D], bw[:, k, m * P:(m + 1) * P], fwd[:, k, :],
                                  start=k == 0, stop=k == DC - 1)
                for m in range(DC):
                    for k in range(DC):
                        pe.matmul(S[:, 512 + m * D:512 + (m + 1) * D], inv[:, k, m * P:(m + 1) * P], ct[:, k, :],
                                  start=k == 0, stop=k == DC - 1)
                pe.matmul(S[:, 1024:1025], W["four"]["sines"], w["a"], start=True, stop=True).then_inc(prep_mm, 1)
                pe.wait_ge(prep_dve, 4)
                pe.transpose(S[:, 1024:1024 + P], tabR[:, :], ident)
                pe.transpose(S[:, 1024 + P:1024 + 2 * P], tabI[:, :], ident).then_inc(prep_mm, 1)
                pe.wait_ge(prep_dve, 5)

                def project(i, s):
                    hold(pe, g["x_copied"], i + 1)
                    hold(pe, g["rotated"], i)
                    for k in range(DC):
                        last = pe.matmul(AB[:, 0:D], xs[:, s * D + k * P:s * D + (k + 1) * P], kc(wb[:, :], D)[:, k, :],
                                         start=k == 0, stop=k == DC - 1)
                    last.then_inc(g["v_projected"], 1)

                def sum_over_time(i, s):
                    hold(pe, g["rotated"], i + 1)
                    hold(pe, g["modulated"], i)
                    for c in range(DC):
                        last = pe.matmul(S[:, c * P:(c + 1) * P], rot[:, s * D + c * P:s * D + (c + 1) * P],
                                         W["const"]["tri"], start=True, stop=True)
                    last.then_inc(g["summed"], 1)

                def out(i, s):
                    hold(pe, g["modulated"], i + 1)
                    hold(pe, g["resid"], i)
                    for c in range(DC):
                        last = pe.matmul(M[:, 256:512], rot2[:, s * D + c * P:s * D + (c + 1) * P],
                                         kc(cg[:, :], D)[:, c, :], start=c == 0, stop=c == DC - 1)
                    last.then_inc(g["projected"], 1)

                def step(k, s, h):
                    if live(k, 2, TILES):
                        out(k - 2, s)
                    if live(k, 0, TILES):
                        project(k, s)
                    if live(k, 1, TILES):
                        sum_over_time(k - 1, 1 - s)
                skewed(pe, TILES, 2, step)
            if "rope" in RUN:
                g = G["rope"]

                def step(k, s, h):
                    hold(pe, g["roped"], k + 1)
                    hold(pe, g["xt"], k)
                    for c in range(DC):
                        last = pe.transpose(C[:, c * P:(c + 1) * P], rot[:, c * P:(c + 1) * P], ident)
                    last.then_inc(g["turned"], 1)
                skewed(pe, TILES, 0, step)
            if "la" in RUN:
                inner("la", LA_ROWS)
            if "moe" in RUN:
                g, w = G["moe"], W["moe"]
                pe.wait_ge(*loaded["moe"])
                hold(pe, G["la"]["xt"], TILES)
                choose(w["router_w"], 6)
                pe.wait_ge(prep_dve, 7)
                for i in range(TILES):
                    pe.transpose(S[0:8, i * P:(i + 1) * P], comb[:, i * 8:(i + 1) * 8], ident).then_inc(prep_mm, 1)
                pe.wait_ge(prep_dve, 8)
                for i in range(TILES):
                    if i >= 2:
                        pe.wait_ge(prep_dve, 9 + i - 2)
                    o = (i % 2) * 512
                    pe.matmul(AB[:, o:o + D], combT[0:8, i * P:(i + 1) * P], w["b3"][0:8, :],
                              start=True, stop=True).then_inc(prep_mm, 1)
                pe.wait_ge(prep_dve, 8 + TILES)

                def hidden(m, u, h):
                    c, s = u % 2, (u // 2) % 2
                    w1 = w12[s].rearrange("p (c n) -> p c n", c=DC)
                    if c == 0:
                        pe.wait_ge(w_loaded[s], 32 * (h + 1))
                    for f in range(FT):
                        hold(pe, g["gated"], 8 * m + f - 1)
                        for half_ in range(2):
                            o = (f % 2) * 1024 + half_ * 512
                            for k in range(DC):
                                last = pe.matmul(S[:, o:o + 512], w1[:, k, half_ * FF + f * P:half_ * FF + (f + 1) * P],
                                                 XT[:, k, c * CHUNK:(c + 1) * CHUNK], start=k == 0, stop=k == DC - 1)
                        last.then_inc(g["hidden"], 1)

                def down(m, u):
                    s = (u // 2) % 2
                    wd = w3[s].rearrange("p (f n) -> p f n", f=FT)
                    hold(pe, g["gated"], 8 * (m + 1))
                    for i in range(4):
                        hold(pe, g["out"], 4 * m + i - 3)
                        for f in range(FT):
                            last = pe.matmul(sums[i], hid[u % 2][:, f, i * P:(i + 1) * P],
                                             wd[:, f, :], start=f == 0, stop=f == FT - 1)
                        last.then_inc(g["expert"], 1)

                def step(k, u, h):
                    if live(k, 0, CHUNKS * EXPERTS):
                        hidden(k, u, h)
                    if live(k, 1, CHUNKS * EXPERTS):
                        down(k - 1, (u - 1) % 4)
                skewed(pe, CHUNKS * EXPERTS, 1, step, unroll=4)

        @block.scalar
        def _(act):
            def copy_outputs(g, h):
                hold(act, g["o_turned"], h + 1)
                act.activation(ot[:, :].rearrange("p (a b q) -> p b a q", a=2, b=2),
                               C[:, 0:256].rearrange("p (b a q) -> p b a q", b=2, a=2), ACT.Copy)\
                   .then_inc(g["o_copied"], 1)

            def copy_turned(g, h):
                hold(act, g["turned"], h + 1)
                act.activation(XT[:, :, bass.ts(h, P)], C[:, 0:256].rearrange("p (c n) -> p c n", c=DC), ACT.Copy)\
                   .then_inc(g["xt"], 1)

            skewed(act, TILES, 0, lambda k, s, h: copy_turned(G["ln"], k))

            def cross(st):
                g, w = G[st], W[st]
                act.wait_ge(*loaded[st])

                def copy_keys(b, s):
                    hold(act, g["k_projected"], b + 1)
                    for hf in range(2):
                        last = act.activation(kbuf[:, s * 1024 + hf * KEYS:s * 1024 + (hf + 1) * KEYS],
                                              AB[:, hf * KEYS:(hf + 1) * KEYS], ACT.Identity,
                                              bias=w["bk"][:, hf:hf + 1])
                    last.then_inc(g["k_copied"], 1)

                def copy_probs(b, s):
                    for c in (0, 2):
                        hold(act, g["p_turned"], 4 * b + c + 1)
                        act.activation(pt[:, s * 2048 + c * 512:s * 2048 + (c + 1) * 512], AB[:, 0:512], ACT.Copy)\
                           .then_inc(g["pt_a"], 1)

                def exps(b, s):
                    for n in range(PAIRS):
                        hold(act, g["masked"], 8 * b + n + 1)
                        p = probs[:, s * 2048 + n * KEYS:s * 2048 + (n + 1) * KEYS]
                        act.activation(p, p, ACT.Exp, bias=mx[:, s * HEADS + n:s * HEADS + n + 1], scale=-1.0,
                                       accum_out=ssum[:, s * HEADS + n:s * HEADS + n + 1])\
                           .then_inc(g["exped"], 1)

                def plain_exps(b, s):
                    hold(act, g["exped"], 2 * b + 2)
                    for n in range(PAIRS):
                        o = (n % 4) * 512 + (n // 4) * KEYS
                        last = act.activation(probs[:, s * 2048 + n * KEYS:s * 2048 + (n + 1) * KEYS], S[:, o:o + KEYS],
                                              ACT.Exp, bias=mx[:, s * HEADS + n:s * HEADS + n + 1],
                                              accum_out=ssum[:, s * HEADS + n:s * HEADS + n + 1])
                        if n % 2 == 1:
                            last.then_inc(g["weighted"], 1)

                def step(k, s, h):
                    if live(k, 2, SEQS) and s == 1:
                        copy_outputs(g, h - 1)
                    if live(k, 0, SEQS):
                        copy_keys(k, s)
                    if live(k, 1, SEQS):
                        copy_probs(k - 1, 1 - s)
                    if live(k, 0, SEQS):
                        (exps if st == "xa0" else plain_exps)(k, s)
                    if live(k, 2, SEQS) and s == 1:
                        copy_turned(g, h - 1)
                skewed(act, SEQS, 2, step)

            def inner(st):
                g = G[st]

                def step(k, s, h):
                    if live(k, 2, TILES):
                        copy_outputs(g, k - 2)
                    if live(k, 1, TILES):
                        hold(act, g["p_turned"], k)
                        b = 1 - s
                        act.activation(pt[:, b * 2048:b * 2048 + 1024], AB[:, :], ACT.Copy).then_inc(g["pt_copied"], 1)
                    if live(k, 0, TILES):
                        hold(act, g["shifted"], k + 1)
                        p = probs[:, s * 2048:s * 2048 + 1024]
                        act.activation(p, p, ACT.Exp).then_inc(g["exped"], 1)
                    if live(k, 2, TILES):
                        if st == "la":
                            hold(act, g["resid"], k - 1)
                            hold(act, g["rstd"], k - 2)
                            act.activation(junk[:, :], tile(xn_all, k - 2), ACT.Square, scale=D ** -0.5,
                                           accum_out=mv[:, 0:1])\
                               .then_inc(g["squared"], 1)
                        copy_turned(g, k - 2)
                skewed(act, TILES, 2, step)

            if "xa0" in RUN:
                cross("xa0")
            if "sa" in RUN:
                inner("sa")
            if "ffn" in RUN:
                g = G["ffn"]
                act.wait_ge(prep_dve, 3)

                def relus(i, s):
                    for n in range(2 * EXPERTS):
                        hold(act, g["expert"], 16 * i + n + 1)
                        if n < 2:
                            out = acc[:, s * D + n * P:s * D + (n + 1) * P]
                        else:
                            hold(act, g["added"], 14 * i + max(n - 5, 0))
                            out = relu[:, (n % 4) * P:(n % 4 + 1) * P]
                        act.activation(out, S[:, (n % 4) * 512:(n % 4) * 512 + P], ACT.Relu, bias=bec[:, n:n + 1],
                                       scale=counts[:, n // 2:n // 2 + 1]).then_inc(g["relued"], 1)

                def step(k, s, h):
                    if live(k, 0, TILES):
                        relus(k, s)
                    if live(k, 1, TILES):
                        copy_turned(g, k - 1)
                skewed(act, TILES, 1, step)
            if "xa1" in RUN:
                cross("xa1")
            if "rope" in RUN:
                g = G["rope"]

                def step(k, s, h):
                    hold(act, G["ssm"]["normed"], k + 1)
                    hold(act, g["rms"], k)
                    act.activation(junk[:, :], tile(xn_all, k), ACT.Square, scale=D ** -0.5,
                                           accum_out=mv[:, 0:1])\
                       .then_inc(g["squared"], 1)
                    copy_turned(g, k)
                hold(act, G["ssm"]["normed"], TILES)
                skewed(act, TILES, 0, step)
            if "la" in RUN:
                inner("la")
            if "moe" in RUN:
                g, w = G["moe"], W["moe"]
                act.wait_ge(prep_dve, 6)
                act.wait_ge(made, 5)
                act.activation(wgt[:, 8:16], wgt[:, 0:8], ACT.Exp).then_inc(prep_act, 1)

                def step(m, u, h):
                    e = 2 * h + u // 2
                    for f in range(FT):
                        hold(act, g["hidden"], 8 * m + f + 1)
                        hold(act, g["gated"], 8 * m + f - 1)
                        act.sem_inc(act_passed, 1)
                        act.activation(gated[:, (f % 2) * CHUNK:(f % 2 + 1) * CHUNK],
                                       S[:, (f % 2) * 1024:(f % 2) * 1024 + 512], ACT.Silu,
                                       bias=w["b1"][:, bass.ds(e * FT + f, 1)]).then_inc(g["silued"], 1)
                skewed(act, CHUNKS * EXPERTS, 0, step, unroll=4)

        @block.gpsimd
        def _(pool):
            chain = Chain(pool, pool_chain)
            for i, value in enumerate((-0.5, LN_EPS, RMS_EPS)):
                pool.memset(half[:, i:i + 1], value).then_inc(made, 1)
            pool.memset(ones[:, :], 1.0).then_inc(made, 1)
            pool.wait_ge(made, 4)

            def inverse_root(g, h, eps, source, waited, signal):
                hold(pool, g[waited], h + 1)
                chain.link(pool.tensor_tensor(var[:, :], source, half[:, eps:eps + 1], ALU.add))
                pool.tensor_tensor(rstd[:, :], var[:, :], half[:, 0:1], ALU.pow).then_inc(g[signal], 1)

            def settle():
                pool.sem_inc(pool_passed, 1)

            def root_of_variance(g, h):
                inverse_root(g, h, 1, mv[:, 1:2], "stats", "rstd")

            def add_bias(g, h, bias, ready):
                hold(pool, ready, h + 1)
                pool.tensor_tensor(tile(x, h), tile(x, h), bias, ALU.add).then_inc(g["biased"], 1)

            def ln_step(k, s, h):
                root_of_variance(G["ln"], k)
                chain.restart()
            skewed(pool, TILES, 0, ln_step)

            def cross(st):
                g, w, prev = G[st], W[st], G[PREV[st]]
                pool.wait_ge(*loaded[st])

                def negate_mask(b, s, h):
                    pool.wait_ge(ctx_loaded[s], ctx_count(st, h))
                    hold(pool, g["masked"], 8 * (b - 1))
                    settle()
                    pool.tensor_scalar(neg[:, s * KEYS:(s + 1) * KEYS], mask_i[:, s * KEYS:(s + 1) * KEYS],
                                       1.0e9, -1.0e9, ALU.mult, ALU.add).then_inc(neg_ready, 1)

                def weigh(b, s):
                    for c in range(4):
                        hold(pool, g["exped"], 8 * b + 2 * c + 2)
                        p = probs[:, s * 2048 + c * 512:s * 2048 + (c + 1) * 512].rearrange("p (n k) -> p n k", n=2)
                        gw = gp[:, s * KEYS:(s + 1) * KEYS].unsqueeze(1).broadcast_to([P, 2, KEYS])
                        pool.tensor_tensor(p, p, gw, ALU.mult).then_inc(g["weighted"], 1)

                def step(k, s, h):
                    if live(k, 0, SEQS):
                        if st == "xa0":
                            negate_mask(k, s, h)
                        if s == 0:
                            hold(pool, prev["normed"], h + 1)
                            add_bias(g, h, w["bo"], prev["resid"] if st == "xa1" else prev["normed"])
                    if live(k, 2, SEQS) and s == 1:
                        root_of_variance(g, h - 1)
                    if live(k, 0, SEQS) and st == "xa0":
                        weigh(k, s)
                    if st == "xa1" and live(k, 2, SEQS) and s == 1:
                        hold(pool, g["normed"], h)
                        settle()
                        pool.tensor_copy(tile(xn_all, h - 1), xn[:, :]).then_inc(g["kept"], 1)
                    chain.restart()
                skewed(pool, SEQS, 2, step)

            def copy_tile(g, prev_xt, k, s, readers):
                hold(pool, prev_xt, k + 1)
                hold(pool, g[readers], k - 1)
                settle()
                pool.tensor_copy(xs[:, s * D:(s + 1) * D].rearrange("p (c n) -> p c n", c=DC),
                                 XT[:, :, bass.ts(k, P)]).then_inc(g["x_copied"], 1)

            def inner(st):
                g, w, prev = G[st], W[st], G[PREV[st]]
                pool.wait_ge(*loaded[st])

                def step(k, s, h):
                    if live(k, 0, TILES):
                        copy_tile(g, prev["xt"], k, s, "v_projected")
                        if st == "sa":
                            hold(pool, prev["normed"], k + 1)
                            add_bias(g, k, w["bo"], prev["resid"])
                    if live(k, 2, TILES):
                        if st == "sa":
                            root_of_variance(g, k - 2)
                        else:
                            inverse_root(g, k - 2, 2, mv[:, 0:1], "squared", "rstd")
                            pool.tensor_tensor(tile(x, k - 2), tile(x, k - 2), tile(xn_all, k - 2), ALU.add)\
                                .then_inc(g["added"], 1)
                    chain.restart()
                skewed(pool, TILES, 2, step)

            if "xa0" in RUN:
                cross("xa0")
            if "sa" in RUN:
                inner("sa")
            if "ffn" in RUN:
                def ffn_step(k, s, h):
                    if live(k, 1, TILES):
                        root_of_variance(G["ffn"], k - 1)
                    chain.restart()
                skewed(pool, TILES, 1, ffn_step)
            if "xa1" in RUN:
                cross("xa1")
            if "ssm" in RUN:
                g, w = G["ssm"], W["ssm"]
                pool.wait_ge(*loaded["ssm"])

                def ssm_step(k, s, h):
                    if live(k, 0, TILES):
                        copy_tile(g, G["xa1"]["xt"], k, s, "v_projected")
                        hold(pool, G["xa1"]["kept"], k + 1)
                        hold(pool, g["biased"], k)
                        chain.link(pool.tensor_tensor(junk[:, :], tile(xn_all, k), w["d"], ALU.mult))
                        pool.tensor_tensor(tile(x, k), tile(x, k), junk[:, :], ALU.add).then_inc(g["biased"], 1)
                    if live(k, 2, TILES):
                        root_of_variance(g, k - 2)
                    chain.restart()
                skewed(pool, TILES, 2, ssm_step)
            if "rope" in RUN:
                def rope_step(k, s, h):
                    inverse_root(G["rope"], k, 2, mv[:, 0:1], "squared", "rms")
                    chain.restart()
                skewed(pool, TILES, 0, rope_step)
            if "la" in RUN:
                inner("la")

        @block.vector
        def _(dve):
            chain = Chain(dve, dve_chain)
            dve.wait_ge(*loaded["x"])
            dve.wait_ge(*loaded["const"])
            K = W["const"]

            def settle():
                dve.sem_inc(dve_passed, 1)

            def tile_stats(g, h):
                chain.link(dve.bn_stats(stat6[:, :], tile(x, h)))
                dve.bn_aggr(mv[:, :], stat6[:, :]).then_inc(g["stats"], 1)

            def normalise(g, h, out):
                hold(dve, g["rstd"], h + 1)
                dve.tensor_scalar(out, tile(x, h), mv[:, 0:1], rstd[:, :], ALU.subtract, ALU.mult)\
                   .then_inc(g["normed"], 1)

            def add_output(g, h, src):
                hold(dve, g["projected"], h + 1)
                if "biased" in g:
                    hold(dve, g["biased"], h + 1)
                dve.tensor_tensor(tile(x, h), src, tile(x, h), ALU.add).then_inc(g["resid"], 1)
                hold(dve, g["resid"], h + 1)
                settle()

            def ln_step(k, s, h):
                tile_stats(G["ln"], k)
                hold(dve, G["ln"]["turned"], k)
                normalise(G["ln"], k, xn[:, :])
                chain.restart()
            skewed(dve, TILES, 0, ln_step)

            def cross(st):
                g, w = G[st], W[st]
                dve.wait_ge(*loaded[st])

                def copy_queries(b, s):
                    hold(dve, g["q_projected"], b + 1)
                    for hf in range(2):
                        for par in range(2):
                            o = s * 2048 + hf * P + par * SEQ
                            last = dve.tensor_scalar(qbuf[:, o:o + SEQ], M[:, 256 + hf * SEQ:256 + (hf + 1) * SEQ],
                                                     w["bq"][:, hf:hf + 1], K["par_x"][:, par:par + 1],
                                                     ALU.add, ALU.mult)
                    last.then_inc(g["q_copied"], 1)

                def copy_values(b, s):
                    hold(dve, g["v_projected"], b + 1)
                    dve.tensor_tensor(vbuf[:, s * 512:(s + 1) * 512].rearrange("p (k n) -> p k n", k=2),
                                      AB[:, 512:1024].rearrange("p (k n) -> p k n", k=2),
                                      w["bv"].unsqueeze(1).broadcast_to([P, 2, D]), ALU.add).then_inc(g["v_copied"], 1)

                def copy_probs(b, s):
                    for c in (1, 3):
                        hold(dve, g["p_turned"], 4 * b + c + 1)
                        dve.tensor_copy(pt[:, s * 2048 + c * 512:s * 2048 + (c + 1) * 512], AB[:, 512:1024])\
                           .then_inc(g["pt_b"], 1)

                def mask_scores(b, s):
                    hold(dve, neg_ready, b + 1)
                    hold(dve, g["scored"], b + 1)
                    settle()
                    for n in range(PAIRS):
                        o = (n % 4) * 512 + (n // 4) * KEYS
                        dve.tensor_tensor_reduce(out=probs[:, s * 2048 + n * KEYS:s * 2048 + (n + 1) * KEYS],
                                                 in0=S[:, o:o + KEYS], in1=neg[:, s * KEYS:(s + 1) * KEYS],
                                                 scale=-1.0, scalar=BIG, op0=ALU.add, op1=ALU.min,
                                                 accum_out=mx[:, s * HEADS + n:s * HEADS + n + 1])\
                           .then_inc(g["masked"], 1)

                def row_maxima(b, s):
                    banks = S.rearrange("p (j f k) -> p f j k", j=4, f=2)
                    hold(dve, g["scored"], b + 1)
                    for hf in range(2):
                        dve.tensor_reduce(mx[:, s * HEADS + 4 * hf:s * HEADS + 4 * hf + 4], banks[:, hf, :, :],
                                          AX.X, ALU.max, negate=True).then_inc(g["exped"], 1)

                def normalise_outputs(b, s):
                    hold(dve, g["pv_done"], b + 1)
                    r = rsum[:, s * HEADS:s * HEADS + PAIRS]
                    chain.link(dve.reciprocal(r, ssum[:, s * HEADS:s * HEADS + PAIRS]))
                    for par in range(2):
                        rows = slice(par * SEQ, (par + 1) * SEQ)
                        last = dve.tensor_tensor(
                            obuf[rows, s * P:(s + 1) * P].rearrange("p (n d) -> p n d", n=PAIRS),
                            M[rows, 0:256].rearrange("p (n a d) -> p n a d", n=PAIRS, a=2)[:, :, par, :],
                            r[rows, :].unsqueeze(2).broadcast_to([SEQ, PAIRS, DH]), ALU.mult)
                    last.then_inc(g["o_normed"], 1)

                def step(k, s, h):
                    closes = live(k, 2, SEQS) and s == 1
                    if live(k, 0, SEQS):
                        copy_queries(k, s)
                        copy_values(k, s)
                    if live(k, 1, SEQS):
                        copy_probs(k - 1, 1 - s)
                    if closes:
                        add_output(g, h - 1, C[:, 256:512])
                        tile_stats(g, h - 1)
                    if live(k, 0, SEQS):
                        (mask_scores if st == "xa0" else row_maxima)(k, s)
                    if live(k, 1, SEQS):
                        normalise_outputs(k - 1, 1 - s)
                    if closes:
                        if st == "xa1":
                            hold(dve, g["kept"], h - 1)
                        normalise(g, h - 1, xn[:, :])
                    chain.restart()
                skewed(dve, SEQS, 2, step)

            def inner(st, rows):
                g, w = G[st], W[st]
                dve.wait_ge(*loaded[st])
                scale = K["par_s" if st == "sa" else "par_x"]
                if st == "sa":
                    for par in range(2):
                        chain.mark(dve.tensor_scalar(bqm[0:rows, par * PAIRS:(par + 1) * PAIRS], w["b"][0:rows, :],
                                                     scale[0:rows, par:par + 1], None, ALU.mult))
                    chain.restart()

                def copy_queries_and_keys(i, s):
                    hold(dve, g["qk_projected"], i + 1)
                    src = S[:, 1024:2048].rearrange("p (n b q) -> p (n b) q", n=PAIRS, b=2)
                    for par in range(2):
                        out = qbuf[0:rows, s * 2048:(s + 1) * 2048].rearrange("p (n a q) -> p n a q", n=HEADS, a=2)
                        if st == "sa":
                            out4 = out[:, :, par, :].rearrange("p (n b) q -> p n b q", b=2)
                            for b in range(2):
                                dve.scalar_tensor_tensor(
                                    out=out4[:, :, b, :],
                                    in0=S[0:rows, 1024:2048].rearrange("p (n b q) -> p n b q", n=PAIRS, b=2)[:, :, b, :],
                                    scalar=scale[0:rows, par:par + 1],
                                    in1=bqm[0:rows, par * PAIRS:(par + 1) * PAIRS].unsqueeze(2)
                                    .broadcast_to([rows, PAIRS, SEQ]),
                                    op0=ALU.mult, op1=ALU.add)
                        else:
                            dve.tensor_scalar(out[:, :, par, :], src[0:rows, :, :], scale[0:rows, par:par + 1], None,
                                              ALU.mult)
                    kk = kbuf[:, s * 1024:(s + 1) * 1024].rearrange("p (n q) -> p n q", n=PAIRS)
                    src = S[:, 1024:2048].rearrange("p (n q) -> p n q", n=PAIRS)
                    if st == "sa":
                        for a, b in ((32, 64), (64, 96)):
                            dve.tensor_tensor(kk[a:b], src[a:b], w["b"][a:b, :].unsqueeze(2).broadcast_to([32, PAIRS, P]),
                                              ALU.add)
                        last = dve.tensor_tensor(kk[0:32], src[96:128],
                                                 w["b"][96:128, :].unsqueeze(2).broadcast_to([32, PAIRS, P]), ALU.add)
                    else:
                        last = dve.tensor_copy(kk[0:32], src[32:64])
                    last.then_inc(g["qk_copied"], 1)

                def copy_values(i, s):
                    hold(dve, g["v_projected"], i + 1)
                    v = vbuf[:, s * 512:s * 512 + D]
                    if st == "sa":
                        dve.tensor_tensor(v, AB[:, 0:D], w["bv"], ALU.add).then_inc(g["v_copied"], 1)
                    else:
                        dve.tensor_copy(v, AB[:, 0:D]).then_inc(g["v_copied"], 1)

                def shift_scores(i, s):
                    hold(dve, g["scored"], i + 1)
                    p = probs[:, s * 2048:s * 2048 + 1024].rearrange("p (n k) -> p n k", n=HEADS)
                    src = S[:, 0:1024].rearrange("p (n k) -> p n k", n=HEADS)
                    if st == "la":
                        chain.link(dve.tensor_tensor(p, src, K["causal"].unsqueeze(1).broadcast_to([P, HEADS, SEQ]),
                                                     ALU.add))
                        src = p
                    m = mx[:, s * HEADS:(s + 1) * HEADS]
                    chain.link(dve.tensor_reduce(m, src, AX.X, ALU.max, negate=True))
                    dve.tensor_tensor(p, src, m.unsqueeze(2).broadcast_to([P, HEADS, SEQ]), ALU.add)\
                       .then_inc(g["shifted"], 1)

                def normalise_outputs(i, s):
                    p = probs[:, s * 2048:s * 2048 + 1024].rearrange("p (n k) -> p n k", n=HEADS)
                    hold(dve, g["exped"], i + 1)
                    z = ssum[:, s * HEADS:(s + 1) * HEADS]
                    r = rsum[:, s * HEADS:(s + 1) * HEADS]
                    chain.link(dve.tensor_reduce(z, p, AX.X, ALU.add))
                    chain.link(dve.reciprocal(r, z))
                    hold(dve, g["pv_done"], i + 1)
                    for b in range(2):
                        src = M[:, 0:256] if b == 0 else C[:, 256:512]
                        for par in range(2):
                            q = slice(par * SEQ, (par + 1) * SEQ)
                            last = dve.tensor_tensor(
                                obuf[q, s * D + b * P:s * D + (b + 1) * P].rearrange("p (n d) -> p n d", n=PAIRS),
                                src[q].rearrange("p (n a d) -> p n a d", n=PAIRS, a=2)[:, :, par, :],
                                r[q].rearrange("p (n b) -> p n b", b=2)[:, :, b:b + 1].broadcast_to([SEQ, PAIRS, DH]),
                                ALU.mult)
                    last.then_inc(g["o_normed"], 1)

                def step(k, s, h):
                    if live(k, 0, TILES):
                        copy_queries_and_keys(k, s)
                        copy_values(k, s)
                    if live(k, 2, TILES):
                        if st == "sa":
                            add_output(g, k - 2, M[:, 256:512])
                            tile_stats(g, k - 2)
                        else:
                            hold(dve, g["projected"], k - 1)
                            dve.tensor_tensor(tile(xn_all, k - 2), M[:, 256:512], tile(xn_all, k - 2), ALU.add)\
                               .then_inc(g["resid"], 1)
                    if live(k, 0, TILES):
                        shift_scores(k, s)
                    if live(k, 1, TILES):
                        normalise_outputs(k - 1, 1 - s)
                    if live(k, 2, TILES):
                        if st == "sa":
                            normalise(g, k - 2, xn[:, :])
                        else:
                            hold(dve, g["rstd"], k - 1)
                            dve.scalar_tensor_tensor(out=xn[:, :], in0=tile(xn_all, k - 2), scalar=rstd[:, :],
                                                     in1=w["norm2"], op0=ALU.mult, op1=ALU.mult)\
                               .then_inc(g["normed"], 1)
                    chain.restart()
                skewed(dve, TILES, 2, step)

            def choose(bias, mm):
                dve.wait_ge(prep_mm, mm)
                dve.tensor_scalar(gateT[0:8, :], S[0:8, 0:TOKENS], bias[0:8, :], None, ALU.add).then_inc(prep_dve, 1)
                dve.wait_ge(prep_mm, mm + 1)
                chain.link(dve.tensor_copy(logit[:, :], S[:, 1024:1024 + 64]))
                for i in range(TILES):
                    r = slice(i * 8, (i + 1) * 8)
                    chain.mark(dve.max(top[:, r], logit[:, r]))
                chain.join()
                for i in range(TILES):
                    r = slice(i * 8, (i + 1) * 8)
                    chain.mark(dve.max_index(topi[:, r], top[:, r], logit[:, r]))
                chain.join()
                chain.link(dve.tensor_copy(topf[:, :], topi[:, :]))
                for i in range(TILES):
                    for rank, dst in ((0, hot), (1, hot2)):
                        chain.mark(dve.tensor_scalar(dst[:, i * 8:(i + 1) * 8], K["iota"],
                                                     topf[:, i * 8 + rank:i * 8 + rank + 1], None, ALU.is_equal))
                chain.join()

            if "xa0" in RUN:
                cross("xa0")
            if "sa" in RUN:
                inner("sa", SA_ROWS)
            if "ffn" in RUN:
                g, w = G["ffn"], W["ffn"]
                dve.wait_ge(*loaded["ffn"])
                choose(w["gate_b"], 1)
                chain.link(dve.tensor_tensor(hot[:, :], hot[:, :], hot2[:, :], ALU.add))
                dve.tensor_reduce(hot2[:, 0:8], hot[:, :].rearrange("p (t e) -> p e t", e=8), AX.X, ALU.add)\
                   .then_inc(prep_dve, 1)
                dve.wait_ge(prep_mm, 3)
                chain.link(dve.tensor_scalar(counts[:, :], S[:, 1280:1288], 1.0 / (2 * TOKENS), None, ALU.mult))
                dve.tensor_tensor(bec[:, :].rearrange("p (e f) -> p e f", e=8), w["be"].rearrange("p (e f) -> p e f", e=8),
                                  counts[:, :].unsqueeze(2).broadcast_to([P, 8, 2]), ALU.mult).then_inc(prep_dve, 1)
                chain.restart()

                def add_experts(i, s):
                    for n in range(2, 2 * EXPERTS):
                        hold(dve, g["relued"], 16 * i + n + 1)
                        if n >= 4:
                            hold(dve, g["added"], 14 * i + n - 3)
                        a = acc[:, s * D + (n % 2) * P:s * D + (n % 2 + 1) * P]
                        dve.tensor_tensor(a, a, relu[:, (n % 4) * P:(n % 4 + 1) * P], ALU.add).then_inc(g["added"], 1)

                def step(k, s, h):
                    if live(k, 1, TILES):
                        add_output(g, k - 1, M[:, 256:512])
                        tile_stats(g, k - 1)
                    if live(k, 0, TILES):
                        add_experts(k, s)
                    if live(k, 1, TILES):
                        normalise(g, k - 1, xn[:, :])
                    chain.restart()
                skewed(dve, TILES, 1, step)
            if "xa1" in RUN:
                cross("xa1")
            if "ssm" in RUN:
                g = G["ssm"]
                dve.wait_ge(prep_mm, 4)
                chain.mark(dve.tensor_copy(wb[:, :], S[:, 0:512]))
                chain.mark(dve.tensor_copy(cg[:, :], S[:, 512:1024]))
                col = [lam[:, i:i + 1] for i in range(8)]
                omega, sq, den, lr, li, sq2, lr2, li2 = col
                chain.link(dve.tensor_copy(omega, S[:, 1024:1025]))
                chain.link(dve.tensor_tensor(sq, omega, omega, ALU.mult))
                chain.link(dve.tensor_scalar(den, sq, 1.0, None, ALU.add))
                chain.link(dve.reciprocal(sq2, den))
                chain.link(dve.tensor_scalar(sq, sq, -1.0, 1.0, ALU.mult, ALU.add))
                chain.mark(dve.tensor_tensor(lr, sq, sq2, ALU.mult))
                chain.link(dve.tensor_scalar(li, omega, sq2, -2.0, ALU.mult, ALU.mult))
                chain.mark(dve.memset(tabR[:, 0:1], 1.0))
                chain.link(dve.memset(tabI[:, 0:1], 0.0))
                m = 1
                while m < SEQ:
                    chain.link(dve.tensor_scalar(tabt[:, 0:m], tabI[:, 0:m], li, None, ALU.mult))
                    chain.link(dve.scalar_tensor_tensor(out=tabR[:, m:2 * m], in0=tabR[:, 0:m], scalar=lr,
                                                        in1=tabt[:, 0:m], op0=ALU.mult, op1=ALU.subtract))
                    chain.link(dve.tensor_scalar(tabt[:, 0:m], tabR[:, 0:m], li, None, ALU.mult))
                    chain.link(dve.scalar_tensor_tensor(out=tabI[:, m:2 * m], in0=tabI[:, 0:m], scalar=lr,
                                                        in1=tabt[:, 0:m], op0=ALU.mult, op1=ALU.add))
                    chain.mark(dve.tensor_tensor(sq, li, li, ALU.mult))
                    chain.link(dve.tensor_tensor(sq2, lr, lr, ALU.mult))
                    chain.mark(dve.tensor_tensor(lr2, sq2, sq, ALU.subtract))
                    chain.link(dve.tensor_scalar(li2, lr, li, 2.0, ALU.mult, ALU.mult))
                    lr, lr2, li, li2 = lr2, lr, li2, li
                    m *= 2
                dve.tensor_copy(tabR[:, SEQ:], tabR[:, 0:SEQ])
                dve.tensor_copy(tabI[:, SEQ:], tabI[:, 0:SEQ]).then_inc(prep_dve, 1)
                dve.wait_ge(prep_dve, 4)
                dve.wait_ge(prep_mm, 5)
                dve.tensor_copy(rowR[:, :], S[:, 1024:1024 + P])
                dve.tensor_copy(rowI[:, :], S[:, 1024 + P:1024 + 2 * P]).then_inc(prep_dve, 1)
                dve.wait_ge(prep_dve, 5)
                chain.restart()

                def turn_phase(src, real, imag, forward, out, s):
                    a = acc[:, 0:D].rearrange("p (c n) -> p c n", c=DC)
                    v = src.rearrange("p (c n) -> p c n", c=DC)
                    chain.mark(dve.tensor_tensor(a, v, real.unsqueeze(1).broadcast_to([P, DC, P]), ALU.mult))
                    b = acc[:, D:2 * D]
                    chain.mark(dve.tensor_tensor(b[:, 0:P], src[:, P:2 * P], imag, ALU.mult))
                    chain.link(dve.tensor_tensor(b[:, P:2 * P], src[:, 0:P], imag, ALU.mult))
                    chain.mark(dve.tensor_tensor(out[:, s * D:s * D + P], acc[:, 0:P], b[:, 0:P],
                                                 ALU.subtract if forward else ALU.add))
                    return dve.tensor_tensor(out[:, s * D + P:(s + 1) * D], acc[:, P:2 * P], b[:, P:2 * P],
                                             ALU.add if forward else ALU.subtract)

                def step(k, s, h):
                    if live(k, 2, TILES):
                        add_output(g, k - 2, M[:, 256:512])
                        tile_stats(g, k - 2)
                    if live(k, 0, TILES):
                        hold(dve, g["v_projected"], k + 1)
                        turn_phase(AB[:, 0:D], rowR[:, :], rowI[:, :], False, rot, s).then_inc(g["rotated"], 1)
                        hold(dve, g["rotated"], k + 1)
                    if live(k, 1, TILES):
                        hold(dve, g["summed"], k)
                        turn_phase(S[:, 0:D], tabR[:, :], tabI[:, :], True, rot2, 1 - s).then_inc(g["modulated"], 1)
                        hold(dve, g["modulated"], k)
                    if live(k, 2, TILES):
                        normalise(g, k - 2, tile(xn_all, k - 2))
                    chain.restart()
                skewed(dve, TILES, 2, step)
            if "rope" in RUN:
                g = G["rope"]
                dve.wait_ge(*loaded["la"])

                def step(k, s, h):
                    hold(dve, g["rms"], k + 1)
                    hold(dve, g["roped"], k)
                    xr = rot2[:, 0:D]
                    chain.link(dve.scalar_tensor_tensor(out=xr, in0=tile(xn_all, k), scalar=rstd[:, :],
                                                        in1=W["la"]["norm1"], op0=ALU.mult, op1=ALU.mult))
                    xe, xo = (xr.rearrange("p (n a) -> p n a", a=2)[:, :, a] for a in range(2))
                    for j, (v, tab) in enumerate(((xe, "cos"), (xo, "sin"), (xe, "sin"), (xo, "cos"))):
                        chain.mark(dve.tensor_tensor(acc[:, j * P:(j + 1) * P], v, K[tab], ALU.mult))
                    chain.join()
                    hold(dve, g["turned"], k)
                    dve.tensor_tensor(rot[:, 0:P], acc[:, 0:P], acc[:, P:2 * P], ALU.subtract)
                    dve.tensor_tensor(rot[:, P:2 * P], acc[:, 2 * P:3 * P], acc[:, 3 * P:4 * P], ALU.add)\
                       .then_inc(g["roped"], 1)
                    chain.restart()
                skewed(dve, TILES, 0, step)
            if "la" in RUN:
                inner("la", LA_ROWS)
            if "moe" in RUN:
                g, w = G["moe"], W["moe"]
                dve.wait_ge(*loaded["moe"])
                choose(w["router_b"], 6)
                tops = top[:, :].rearrange("p (t r) -> p t r", r=8)
                dve.tensor_tensor(wgt[:, 0:8], tops[:, :, 1], tops[:, :, 0], ALU.subtract).then_inc(made, 1)
                dve.wait_ge(prep_act, 1)
                chain.link(dve.tensor_scalar(wgt[:, 16:24], wgt[:, 8:16], 1.0, None, ALU.add))
                chain.link(dve.reciprocal(wgt[:, 24:32], wgt[:, 16:24]))
                chain.link(dve.tensor_tensor(wgt[:, 16:24], wgt[:, 8:16], wgt[:, 24:32], ALU.mult))
                for dst, wi in ((hot, 24), (hot2, 16)):
                    v = dst[:, :].rearrange("p (t e) -> p t e", e=8)
                    chain.mark(dve.tensor_tensor(v, v, wgt[:, wi:wi + 8].unsqueeze(2).broadcast_to([P, 8, 8]), ALU.mult))
                chain.join()
                dve.tensor_tensor(comb[:, :], hot[:, :], hot2[:, :], ALU.add).then_inc(prep_dve, 1)
                dve.wait_ge(prep_mm, 15)
                dve.tensor_copy(combT[0:8, :], S[0:8, 0:TOKENS]).then_inc(prep_dve, 1)
                hold(dve, G["la"]["added"], TILES)
                for i in range(TILES):
                    dve.wait_ge(prep_mm, 16 + i)
                    o = (i % 2) * 512
                    dve.tensor_tensor(tile(x, i), AB[:, o:o + D], tile(x, i), ALU.add).then_inc(prep_dve, 1)
                dve.wait_ge(prep_dve, 8 + TILES)
                chain.restart()

                def gate(m, u, h):
                    c = u % 2
                    e = 2 * h + u // 2
                    for f in range(FT):
                        hold(dve, g["silued"], 8 * m + f + 1)
                        dve.scalar_tensor_tensor(out=hid[c][:, f, :], in0=S[:, (f % 2) * 1024 + 512:(f % 2 + 1) * 1024],
                                                 scalar=w["b2"][:, bass.ds(e * FT + f, 1)],
                                                 in1=gated[:, (f % 2) * CHUNK:(f % 2 + 1) * CHUNK],
                                                 op0=ALU.add, op1=ALU.mult).then_inc(g["gated"], 1)

                def combine(m, u, e):
                    c = u % 2
                    for i in range(4):
                        tok = c * 4 + i
                        hold(dve, g["expert"], 4 * m + i + 1)
                        hold(dve, g["out"], 4 * m - 4)
                        xt = x[:, tok * D:(tok + 1) * D]
                        dve.scalar_tensor_tensor(out=xt, in0=sums[i],
                                                 scalar=comb[:, bass.ds(e + tok * 8, 1)], in1=xt,
                                                 op0=ALU.mult, op1=ALU.add).then_inc(g["out"], 1)

                def step(m, u, h):
                    if live(m, 0, CHUNKS * EXPERTS):
                        gate(m, u, h)
                    if live(m, 1, CHUNKS * EXPERTS):
                        combine(m - 1, (u - 1) % 4, 2 * h + u // 2 if u % 2 else 2 * h + u // 2 - 1)
                skewed(dve, CHUNKS * EXPERTS, 1, step, unroll=4)



def channels_first(w):
    return w.reshape(DC, P, -1).transpose(1, 0, 2)


def column(b):
    return b.reshape(DC, P).T


def rows(b):
    return np.broadcast_to(b, (P, b.shape[-1]))


def padded(a):
    out = np.zeros((P, a.shape[1]), a.dtype)
    out[:a.shape[0]] = a
    return out


def by_parity(wo):
    return wo.reshape(PAIRS, 2, DH, D).transpose(0, 2, 1, 3).reshape(P, 2, D)


def constants():
    p = np.arange(P)
    c = {"ident": np.eye(P)}
    par = (p[:, None] // DH) % 2 == np.arange(2)[None, :]
    c["par_x"] = par / np.sqrt(DH)
    rot_par = ((p[:, None] - 2 * DH) // ROT) % 2 == np.arange(2)[None, :]
    c["par_s"] = np.where(p[:, None] < 2 * DH, par, rot_par) / np.sqrt(DH + ROT)
    c["iota"] = np.tile(np.arange(8), (P, 1))
    c["causal"] = np.where(np.arange(SEQ)[None, :] > (p % SEQ)[:, None], -1.0e9, 0.0)
    same = p[:, None] // SEQ == p[None, :] // SEQ
    c["tri"] = same & (p[:, None] <= p[None, :])
    half = D // 2
    theta = (1.0 / np.float32(10000.0) ** (np.arange(half, dtype=np.float32) / np.float32(half))).astype(np.float32)
    ang = ((p % SEQ).astype(np.float32)[:, None] * theta[None, :]).astype(np.float32).astype(np.float64)
    c["cos"], c["sin"] = np.cos(ang), np.sin(ang)
    return c


def fourier():
    n, k = np.arange(D), np.arange(P)
    ang = 2 * np.pi * ((n[:, None] * k[None, :]) % D) / D
    alternate = 1.0 - 2.0 * (n % 2)
    fwd = np.concatenate([np.cos(ang), -np.sin(ang)], axis=1)
    fwd[:, P] = alternate
    inv = np.concatenate([np.cos(ang), -np.sin(ang)], axis=1) * 2.0 / D
    inv[:, 0] = 1.0 / D
    inv[:, P] = alternate / D
    j = np.arange(1, P + 1)
    turns = (j[:, None] * k[None, :]) % D
    sines = -2.0 * np.sin(2 * np.pi * turns / D)
    sines[turns % P == 0] = 0.0
    return {"fwd": channels_first(fwd), "inv": channels_first(inv), "sines": sines}


def pack(name, parts):
    fields = PACKS[name]
    return np.ascontiguousarray(np.concatenate(
        [np.asarray(parts[f]).reshape(P, fields[f]).astype(np.float32, copy=False) for f in fields], axis=1))


def lay_out(v):
    out = {}
    out["x"] = v["x"].reshape(TILES, P, D).transpose(1, 0, 2).reshape(P, TILES * D)
    out["ctx"] = v["ctx_1024"].transpose(0, 2, 1).reshape(SEQS, DC, P, KEYS).transpose(0, 2, 1, 3)\
        .reshape(SEQS, P, DC * KEYS)
    out["gp"] = v["fside_BxSxS2_0"]
    out["mask"] = v["mask_BxSxS2_ik1"]
    out["const"] = pack("const", constants())
    out["four"] = pack("four", fourier())

    def cross(q, k, vv, o, bq, bk, bv, bo):
        return {"wq": channels_first(q), "wk": channels_first(k), "wv": channels_first(vv), "wo": by_parity(o),
                "bq": column(bq), "bk": column(bk), "bv": rows(bv), "bo": rows(bo)}
    out["xa0"] = pack("xa0", cross(*(v["L0_xattn_w" + n] for n in ("q_k", "k_k", "v_k", "o_k", "q_b", "k_b", "v_b", "o_b"))))
    out["xa1"] = pack("xa1", cross(*(v["L1_xattn_" + n] for n in ("W_q", "W_k", "W_v", "W_o", "b_q", "b_k", "b_v", "b_o"))))
    a = {n: v["L0_attn_" + n] for n in ("Wq", "bq", "Wk", "bk", "Wv", "bv", "Wr", "br", "Wo", "bo")}
    w = np.concatenate([a["Wq"].reshape(D, PAIRS, 2 * DH), a["Wr"].reshape(D, PAIRS, 2 * ROT),
                        a["Wk"].reshape(D, PAIRS, 2 * DH)], axis=2)
    b = np.concatenate([a["bq"].reshape(PAIRS, 2 * DH), a["br"].reshape(PAIRS, 2 * ROT),
                        a["bk"].reshape(PAIRS, 2 * DH)], axis=1)
    out["sa"] = pack("sa", {"w": channels_first(w.reshape(D, -1)), "wv": channels_first(a["Wv"]),
                            "wo": by_parity(a["Wo"]), "b": b.T, "bv": rows(a["bv"]), "bo": rows(a["bo"])})
    out["ffn"] = pack("ffn", {
        "gate_w": channels_first(v["L0_ffn_gate_w"].T), "gate_b": padded(v["L0_ffn_gate_b"][:, None]),
        "we": channels_first(v["L0_ffn_expert_w"].transpose(2, 0, 1).reshape(D, -1)),
        "be": v["L0_ffn_expert_b"].reshape(EXPERTS, DC, P).transpose(2, 0, 1)})
    out["ssm"] = pack("ssm", {"bw": channels_first(v["L1_attn_B_w"]), "ct": channels_first(v["L1_attn_C_w"].T),
                              "a": v["L1_attn_a_params"][:, None], "d": rows(v["L1_attn_D"])})
    f = {n: v["L1_ffn_" + n] for n in ("norm1_w", "Wq", "Wk", "Wv", "Wo", "norm2_w", "router_w", "router_b",
                                       "W1", "b1", "W2", "b2", "W3", "b3")}
    groups = np.arange(HEADS) // (HEADS // 4)
    wk = f["Wk"].reshape(D, 4, DH)[:, groups].reshape(D, PAIRS, 2 * DH)
    wv = f["Wv"].reshape(D, 4, DH)[:, groups].reshape(D, D)
    w = np.concatenate([f["Wq"].reshape(D, PAIRS, 2 * DH), wk], axis=2)
    out["la"] = pack("la", {"w": channels_first(w.reshape(D, -1)), "wv": channels_first(wv), "wo": by_parity(f["Wo"]),
                            "norm1": rows(f["norm1_w"]), "norm2": rows(f["norm2_w"])})

    def feature_columns(b):
        return b.reshape(EXPERTS, FT, P).transpose(2, 0, 1)
    out["moe"] = pack("moe", {"router_w": channels_first(f["router_w"]), "router_b": padded(f["router_b"][:, None]),
                              "b1": feature_columns(f["b1"]), "b2": feature_columns(f["b2"]), "b3": padded(f["b3"])})
    both = np.concatenate([f["W1"], f["W2"]], axis=2)
    out["w12"] = both.reshape(EXPERTS, DC, P, 2 * FF).transpose(0, 2, 1, 3).reshape(EXPERTS, P, DC * 2 * FF)
    out["w3"] = f["W3"].reshape(EXPERTS, FT, P, D).transpose(0, 2, 1, 3).reshape(EXPERTS, P, FT * D)
    return {n: np.ascontiguousarray(a) for n, a in out.items()}


def program(nc, arrays, upto=9):
    t = {}
    for name, a in arrays.items():
        t[name] = nc.dram_tensor(f"in_{name}", a.shape, mybir.dt.from_np(a.dtype), kind="ExternalInput").ap()
    t["out"] = nc.dram_tensor("out_x", (P, TILES * D), F32, kind="ExternalOutput").ap()
    build(nc, t, upto)


def kernel(**inputs):
    import concourse.bacc as bacc
    from concourse.bass_utils import run_bass_kernel_spmd as run

    nc = bacc.Bacc("TRN2", target_bir_lowering=False, num_devices=1)
    arrays = lay_out({n: np.asarray(a) for n, a in inputs.items()})
    program(nc, arrays)
    r = run(nc, [{f"in_{n}": a for n, a in arrays.items()}], core_ids=[0])
    return np.ascontiguousarray(
        r.results[0]["out_x"].reshape(P, TILES, D).transpose(1, 0, 2).reshape(SEQS, SEQ, D))
```

```python
from contextlib import ExitStack

import numpy as np

import concourse.bass as bass
from concourse import mybir

F32 = mybir.dt.float32
F16 = mybir.dt.float16
I32 = mybir.dt.int32
U32 = mybir.dt.uint32
ALU = mybir.AluOpType
ACT = mybir.ActivationFunctionType
AX = mybir.AxisListType

P = 128
SEQS, SEQ, D = 16, 64, 256
KEYS = 256
TOKENS = SEQS * SEQ
TILES = TOKENS // P
DC = D // P
HEADS, DH = 16, 16
PAIRS = HEADS // 2
ROT = 32
EXPERTS = 8
FF = 1024
FT = FF // P
CHUNK = 512
CHUNKS = TOKENS // CHUNK
LN_EPS, RMS_EPS = 1e-5, 1e-6
CREDIT = 1
BIG = 3.0e38

SA_ROWS = 2 * DH + 2 * ROT
LA_ROWS = 2 * DH

PACKS = {
    "const": {"ident": P, "par_x": 2, "par_s": 2, "iota": 8, "causal": SEQ, "tri": P, "cos": P, "sin": P},
    "xa0": {"wq": 512, "wk": 512, "wv": 512, "wo": 512, "bq": 2, "bk": 2, "bv": D, "bo": D},
    "sa": {"w": 2048, "wv": 512, "wo": 512, "b": 8, "bv": D, "bo": D},
    "ffn": {"gate_w": 16, "gate_b": 1, "we": 4096, "be": 16},
    "xa1": {"wq": 512, "wk": 512, "wv": 512, "wo": 512, "bq": 2, "bk": 2, "bv": D, "bo": D},
    "ssm": {"bw": 512, "ct": 512, "a": 1, "d": D},
    "four": {"fwd": 512, "inv": 512, "sines": P},
    "la": {"w": 1024, "wv": 512, "wo": 512, "norm1": D, "norm2": D},
    "moe": {"router_w": 16, "router_b": 1, "b1": 64, "b2": 64, "b3": D},
}


EARLY = ("xa0", "sa", "ffn")


class Signal:

    def __init__(self, sem, base):
        self.sem, self.base = sem, base


def hold(eng, signal, n):
    if isinstance(n, int) and n <= 0:
        return
    eng.wait_ge(signal.sem, n + (signal.base + CREDIT))


def at_most(n, top):
    return min(n, top) if isinstance(n, int) else n


def skewed(eng, n, lag, step, unroll=2):
    for k in range(unroll):
        step(k, k % unroll, k // unroll)
    with eng.Fori(1, n // unroll) as h:
        for s in range(unroll):
            step(unroll * h + s, s, h)
    for k in range(n, n + lag):
        step(k, k % unroll, k // unroll)


def live(k, lag, n):
    return 0 <= k - lag < n if isinstance(k, int) else True


class Chain:

    def __init__(self, eng, sem):
        self.eng, self.sem, self.n = eng, sem, 0

    def link(self, ins):
        ins.then_inc(self.sem, 1)
        self.n += 1
        self.eng.wait_ge(self.sem, self.n)

    def mark(self, ins):
        ins.then_inc(self.sem, 1)
        self.n += 1

    def join(self):
        self.eng.wait_ge(self.sem, self.n)

    def restart(self):
        if self.n:
            self.join()
            self.eng.sem_clear(self.sem)
            self.n = 0


def build(nc, t, upto=9):
    ctx = ExitStack()
    with ctx:
        def sb(name, cols, dt=F32):
            return ctx.enter_context(nc.sbuf_tensor(name, [P, cols], dt))

        def sem(name):
            return ctx.enter_context(nc.semaphore(name))

        W = {}
        early = sb("early", sum(sum(PACKS[pack].values()) for pack in EARLY))
        taken = 0
        for pack, fields in PACKS.items():
            cols = sum(fields.values())
            if pack in EARLY:
                whole = early[:, taken:taken + cols]
                taken += cols
            else:
                whole = sb("pack_" + pack, cols)[:, :]
            W[pack] = {"whole": whole}
            at = 0
            for name, cols in fields.items():
                W[pack][name] = whole[:, at:at + cols]
                at += cols

        def kc(ap, n):
            return ap.rearrange("p (c n) -> p c n", n=n)

        ident = W["const"]["ident"]
        x = sb("x", TILES * D)
        xn_all = sb("xn_all", TILES * D)
        xt_all = sb("xt_all", DC * TOKENS)
        XT = xt_all[:, :].rearrange("p (c n) -> p c n", c=DC)
        xn = sb("xn", D)
        stat6 = sb("stat6", 6)
        mv = sb("mv", 2)
        var = sb("var", 1)
        rstd = sb("rstd", 1)
        half = sb("half", 3)
        junk = sb("junk", D)
        probs = sb("probs", 2 * PAIRS * KEYS)
        pt = sb("pt", 2 * PAIRS * 2 * P)
        ctx_t = sb("ctx_t", 2 * DC * KEYS)
        gp = sb("gp", 2 * KEYS)
        mask_i = sb("mask_i", 2 * KEYS, I32)
        neg = sb("neg", 2 * KEYS)
        kbuf = sb("kbuf", 4 * 1024, F16)
        vbuf = sb("vbuf", 4 * 512, F16)
        qbuf = sb("qbuf", 4 * 2048, F16)

        def k_part(part, s):
            return kbuf[:, (2 * part + s) * 1024:(2 * part + s + 1) * 1024]

        def v_part(part, s):
            return vbuf[:, (2 * part + s) * 512:(2 * part + s + 1) * 512]

        def q_part(part, s):
            return qbuf[:, (2 * part + s) * 2048:(2 * part + s + 1) * 2048]

        def p_part(part, s):
            return pt[:, :].bitcast(F16)[:, (2 * part + s) * 2048:(2 * part + s + 1) * 2048]

        mx = sb("mx", 2 * HEADS)
        ssum = sb("ssum", 2 * HEADS)
        rsum = sb("rsum", 2 * HEADS)
        obuf = sb("obuf", 2 * 2 * P)
        ot = sb("ot", 2 * P)
        xs = sb("xs", 2 * DC * P)
        scratch = sb("scratch", 1024)
        acc = scratch[:, 0:2 * DC * P]
        relu = scratch[:, 512:1024]
        qsplit = sb("qsplit", 512, F16)
        counts = sb("counts", EXPERTS)
        bec = sb("bec", 2 * EXPERTS)
        top = sb("top", TILES * 8)
        topi = sb("topi", TILES * 8, U32)
        topf = sb("topf", TILES * 8)
        hot = sb("hot", TILES * EXPERTS)
        hot2 = sb("hot2", TILES * EXPERTS)
        logit = sb("logit", TILES * EXPERTS)
        gateT = sb("gateT", TOKENS)
        ones = sb("ones", P)
        wb = sb("wb", DC * D)
        cg = sb("cg", DC * D)
        lam = sb("lam", 8)
        tabR = sb("tabR", 2 * SEQ)
        tabI = sb("tabI", 2 * SEQ)
        tabt = sb("tabt", SEQ)
        rowR = sb("rowR", P)
        rowI = sb("rowI", P)
        rot = sb("rot", 2 * D)
        rot2 = sb("rot2", 2 * D)
        vsum = rot
        comb = sb("comb", TILES * EXPERTS)
        combT = gateT
        wgt = sb("wgt", TILES * 4)
        wide = DC * 2 * FF
        w12 = [early[:, i * wide:(i + 1) * wide] for i in range(2)]
        w3 = [early[:, 2 * wide:2 * wide + FT * D], sb("w3_1", FT * D)[:, :]]
        gated = ctx_t
        hid = [probs[:, :].rearrange("p (f n) -> p f n", f=FT), pt[:, :].rearrange("p (f n) -> p f n", f=FT)]

        ps = ctx.enter_context(nc.psum_tensor("ps", [P, 8 * 512], F32))
        S = ps[:, 0:2048]
        AB = ps[:, 2048:3072]
        M = ps[:, 3072:3584]
        C = ps[:, 3584:4096]
        sums = [ps[:, o:o + D] for o in (2048, 2560, 3072, 3584)]

        shared = {}

        def signals(counts):
            out = {}
            for name, count in counts.items():
                if name not in shared:
                    shared[name] = [sem(name), 0]
                out[name] = Signal(*shared[name])
                shared[name][1] += count
            return out

        def each(count, names):
            return {name: count for name in names.split()}

        rows_turned = each(TILES, "stats rstd normed turned xt")
        tail = {**rows_turned, **each(TILES, "o_turned o_copied projected resid")}
        cross_counts = {
            **each(SEQS, "k_projected k_hi k_copied v_projected v_summed v_hi v_lo scored pv_done o_normed"),
            **each(TILES, "q_projected q_copied biased"), **each(4 * SEQS, "weighted p_turned pt_hi pt_lo"), **tail}
        inner_counts = {
            **each(TILES, "x_copied qk_projected qk_summed qk_hi qk_copied v_projected v_summed v_hi v_lo scored "
                          "shifted exped p_turned pt_hi pt_lo pv_done o_normed"), **tail}
        G = {
            "ln": signals(rows_turned),
            "xa0": signals({**cross_counts, **each(8 * SEQS, "masked powered"), "negated": SEQS}),
            "sa": signals({**inner_counts, "biased": TILES}),
            "ffn": signals({**rows_turned, **each(TILES, "projected resid"), "expert": 16 * TILES,
                            "relued": 16 * TILES, "added": 14 * TILES}),
            "xa1": signals({**cross_counts, "maxima": 2 * SEQS, "kept": TILES}),
            "ssm": signals(each(TILES, "x_copied v_projected rotated summed modulated projected biased resid stats "
                                       "rstd normed")),
            "rope": signals(each(TILES, "squared rstd roped turned xt")),
            "la": signals({**inner_counts, **each(TILES, "squared summed_up")}),
            "moe": signals({"hidden": 0, "silued": 0, "gated": 0, "chunk_out": 0, "out": 0}),
        }
        loads = {"first": ["x", "const"], "xa0": ["xa0"], "sa": ["sa"], "ffn": ["ffn"], "ssm": ["four", "ssm"],
                 "late": ["xa1", "la", "moe"]}
        load_sems = {name: sem(f"loaded_{name}") for name in loads}
        loaded = {a: (load_sems[name], 16 * len(of)) for name, of in loads.items() for a in of}
        ctx_loaded = [sem(f"ctx_loaded{s}") for s in range(2)]

        def ctx_count(st, h):
            return 80 * (h + 1) if st == "xa0" else 80 * (SEQS // 2) + 16 * (h + 1)

        w_loaded = [sem(f"w_loaded{s}") for s in range(2)]
        dve_chain, pool_chain = sem("dve_chain"), sem("pool_chain")
        dve_passed, pool_passed, act_passed = sem("dve_passed"), sem("pool_passed"), sem("act_passed")
        made = sem("made")
        prep_mm, prep_dve, prep_act = sem("prep_mm"), sem("prep_dve"), sem("prep_act")
        final_ready = G["moe"]["out"]
        stored = sem("stored")

        block = ctx.enter_context(nc.Block())

        def tile(ap, h):
            return ap[:, bass.ts(h, D)]

        XA = ["xa0", "xa1"]
        PREV = {"xa0": "ln", "sa": "xa0", "ffn": "sa", "xa1": "ffn", "ssm": "xa1", "rope": "ssm", "la": "rope"}
        ORDER = ["ln", "xa0", "sa", "ffn", "xa1", "ssm", "rope", "la", "moe"]
        RUN = ORDER[:upto]

        @block.sync
        def _(sp):
            for counter, _ in shared.values():
                sp.sem_inc(counter, CREDIT)
            sp.dma_start(x[:, :], t["x"]).then_inc(loaded["x"][0], 16)
            for name in ("const", "xa0", "sa", "ffn", "four", "ssm"):
                sp.dma_start(W[name]["whole"], t[name]).then_inc(loaded[name][0], 16)

            def load_context(st, b, s, h):
                g = G[st]
                if not isinstance(b, int) or b >= 2:
                    hold(sp, g["v_projected"], b - 1)
                    if st == "xa0":
                        hold(sp, g["masked"], 8 * (b - 1))
                        hold(sp, g["weighted"], 4 * (b - 1))
                        hold(sp, G["xa0"]["negated"], b - 1)
                c = ctx_t[:, s * DC * KEYS:(s + 1) * DC * KEYS]
                done = ctx_loaded[s]
                src = t["ctx"][bass.ds(b, 1), :, :].rearrange("b p n -> (b p) n")
                sp.dma_start(c, src).then_inc(done, 16)
                if st == "xa0":
                    for r in range(2):
                        gsrc = t["gp"][bass.ds(b, 1), :, :].rearrange("b p n -> (b p) n")
                        msrc = t["mask"][bass.ds(b, 1), :, :].rearrange("b p n -> (b p) n")
                        sp.dma_start(gp[r * SEQ:(r + 1) * SEQ, s * KEYS:(s + 1) * KEYS], gsrc).then_inc(done, 16)
                        sp.dma_start(mask_i[r * SEQ:(r + 1) * SEQ, s * KEYS:(s + 1) * KEYS], msrc).then_inc(done, 16)

            if "xa0" in RUN:
                skewed(sp, SEQS, 0, lambda k, s, h: load_context("xa0", k, s, h))
            for name in ("xa1", "la", "moe"):
                sp.dma_start(W[name]["whole"], t[name]).then_inc(loaded[name][0], 16)
            if "xa1" in RUN:
                hold(sp, G["xa0"]["v_projected"], SEQS)
                skewed(sp, SEQS, 0, lambda k, s, h: load_context("xa1", k, s, h))
            if "moe" in RUN:
                def load_expert(e, s, h):
                    if not isinstance(e, int) or e >= 2:
                        hold(sp, G["moe"]["chunk_out"], 8 * (e - 1))
                    a = t["w12"][bass.ds(e, 1), :, :].rearrange("b p n -> (b p) n")
                    b = t["w3"][bass.ds(e, 1), :, :].rearrange("b p n -> (b p) n")
                    sp.dma_start(w12[s], a).then_inc(w_loaded[s], 16)
                    sp.dma_start(w3[s], b).then_inc(w_loaded[s], 16)
                hold(sp, G["ffn"]["xt"], TILES)
                skewed(sp, EXPERTS, 0, load_expert)
                hold(sp, final_ready, 4 * CHUNKS * EXPERTS)
            else:
                last = {"ln": ("ln", "xt"), "rope": ("rope", "xt"), "ssm": ("ssm", "normed"), "la": ("la", "xt")}
                a, b = last.get(RUN[-1], (RUN[-1], "xt"))
                hold(sp, G[a][b], TILES)
                if RUN[-1] == "la":
                    hold(sp, G["la"]["summed_up"], TILES)
            sp.dma_start(t["out"], x[:, :]).then_inc(stored, 16)
            sp.wait_ge(stored, 16)

        @block.tensor
        def _(pe):
            pe.wait_ge(*loaded["const"])

            def turn_rows(g, h):
                hold(pe, g["normed"], h + 1)
                for c in range(DC):
                    last = pe.transpose(C[:, c * P:(c + 1) * P], xn[:, c * P:(c + 1) * P], ident)
                last.then_inc(g["turned"].sem, 1)

            def turn_outputs(g, h, per_tile, base):
                hold(pe, g["o_normed"], per_tile * (h + 1))
                hold(pe, g["xt"], h)
                for b in range(2):
                    last = pe.transpose(C[:, b * P:(b + 1) * P], obuf[:, base + b * P:base + (b + 1) * P], ident)
                last.then_inc(g["o_turned"].sem, 1)

            def split_product(dst, a, b, first=True, final=True):
                pe.matmul(dst, a[0], b[0], start=first, stop=False)
                pe.matmul(dst, a[0], b[1], start=False, stop=False)
                return pe.matmul(dst, a[1], b[0], start=False, stop=final)

            def out_project(g, h, wo, dst):
                hold(pe, g["o_copied"], h + 1)
                hold(pe, g["resid"], h)
                for par in range(2):
                    last = pe.matmul(dst, ot[:, par * P:(par + 1) * P], kc(wo, D)[:, par, :],
                                     start=par == 0, stop=par == 1)
                last.then_inc(g["projected"].sem, 1)

            def ln_step(k, s, h):
                hold(pe, G["ln"]["xt"], k)
                turn_rows(G["ln"], k)
            skewed(pe, TILES, 0, ln_step)

            def cross(st):
                g, w = G[st], W[st]
                wq, wk, wv = kc(w["wq"], D), kc(w["wk"], D), kc(w["wv"], D)
                prev = G[PREV[st]]
                pe.wait_ge(*loaded[st])

                def project(b, s, h):
                    c = ctx_t[:, s * DC * KEYS:(s + 1) * DC * KEYS].rearrange("p (c n) -> p c n", c=DC)
                    pe.wait_ge(ctx_loaded[s], ctx_count(st, h))
                    hold(pe, g["pt_lo"], 4 * b - 5)
                    if isinstance(b, int) and b == 1:
                        hold(pe, g["k_copied"], 1)
                    for hf in range(2):
                        for k in range(DC):
                            last = pe.matmul(AB[:, hf * KEYS:(hf + 1) * KEYS], wk[:, k, hf * P:(hf + 1) * P],
                                             c[:, k, :], start=k == 0, stop=k == DC - 1)
                    last.then_inc(g["k_projected"].sem, 1)
                    hold(pe, g["pt_lo"], 4 * b - 4)
                    if isinstance(b, int) and b == 1:
                        hold(pe, g["v_summed"], 1)
                    for kt in range(2):
                        for k in range(DC):
                            last = pe.matmul(AB[:, 512 + kt * D:512 + (kt + 1) * D], c[:, k, kt * P:(kt + 1) * P],
                                             wv[:, k, :], start=k == 0, stop=k == DC - 1)
                    last.then_inc(g["v_projected"].sem, 1)
                    if s == 0:
                        hold(pe, prev["xt"], h + 1)
                        hold(pe, g["o_normed"], b - 1)
                        for hf in range(2):
                            for k in range(DC):
                                last = pe.matmul(M[:, 256 + hf * P:256 + (hf + 1) * P], wq[:, k, hf * P:(hf + 1) * P],
                                                 XT[:, k, bass.ts(h, P)], start=k == 0, stop=k == DC - 1)
                        last.then_inc(g["q_projected"].sem, 1)

                def turn_probs(b, s):
                    pr = probs[:, s * 2048:(s + 1) * 2048].rearrange("p (n k) -> p n k", n=PAIRS)
                    for c in range(4):
                        hold(pe, g["weighted"], 4 * b + c + 1)
                        if c == 0:
                            hold(pe, g["k_copied"], at_most(b + 2, SEQS))
                        elif c == 1:
                            hold(pe, g["v_summed"], at_most(b + 2, SEQS))
                        else:
                            hold(pe, g["pt_lo"], 4 * b + c - 1)
                        for n in range(2):
                            for kt in range(2):
                                o = (c % 2) * 512 + (n * 2 + kt) * P
                                last = pe.transpose(AB[:, o:o + P], pr[:, 2 * c + n, kt * P:(kt + 1) * P], ident)
                        last.then_inc(g["p_turned"].sem, 1)

                def score(b, s, h):
                    hold(pe, g["q_copied"], h + 1)
                    hold(pe, g["k_copied"], b + 1)
                    if st == "xa0":
                        hold(pe, g["masked"], 8 * b)
                    else:
                        hold(pe, g["weighted"], 4 * b)
                    for hf in range(2):
                        q = [q_part(part, s)[:, hf * P:(hf + 1) * P] for part in range(2)]
                        kk = [k_part(part, s)[:, hf * KEYS:(hf + 1) * KEYS] for part in range(2)]
                        for j in range(4):
                            r = slice(32 * j, 32 * j + 32)
                            o = j * 512 + hf * KEYS
                            last = split_product(S[:, o:o + KEYS], [a[r, :] for a in q], [a[r, :] for a in kk])
                    last.then_inc(g["scored"].sem, 1)

                def mix_values(b, s):
                    turned = [p_part(part, s).rearrange("p (n k q) -> p n k q", n=PAIRS, k=2) for part in range(2)]
                    v = [v_part(part, s).rearrange("p (k n) -> p k n", k=2) for part in range(2)]
                    hold(pe, g["pt_lo"], 4 * b + 4)
                    hold(pe, g["v_lo"], b + 1)
                    hold(pe, g["o_normed"], b)
                    for n in range(PAIRS):
                        for kt in range(2):
                            last = split_product(M[:, n * 32:(n + 1) * 32], [a[:, n, kt, :] for a in turned],
                                                 [a[:, kt, n * 32:(n + 1) * 32] for a in v], kt == 0, kt == 1)
                    last.then_inc(g["pv_done"].sem, 1)

                def step(k, s, h):
                    odd_tile = s == 1
                    if live(k, 2, SEQS) and odd_tile:
                        turn_outputs(g, h - 1, 2, 0)
                    if live(k, 0, SEQS):
                        project(k, s, h)
                    if live(k, 1, SEQS):
                        turn_probs(k - 1, 1 - s)
                    if live(k, 2, SEQS) and odd_tile:
                        out_project(g, h - 1, w["wo"], C[:, 256:512])
                    if live(k, 0, SEQS):
                        score(k, s, h)
                    if live(k, 1, SEQS):
                        mix_values(k - 1, 1 - s)
                    if live(k, 2, SEQS) and odd_tile:
                        turn_rows(g, h - 1)
                skewed(pe, SEQS, 2, step)

            def inner(st, rows):
                g, w = G[st], W[st]
                width = w["w"].shape[1] // (DC * PAIRS)
                wqk = w["w"].rearrange("p (c n m) -> p c n m", c=DC, n=PAIRS)
                wv = kc(w["wv"], D)
                pe.wait_ge(*loaded[st])

                def project(i, s):
                    xt = xs[:, s * D:(s + 1) * D].rearrange("p (c n) -> p c n", c=DC)
                    hold(pe, g["x_copied"], i + 1)
                    hold(pe, g["qk_summed"], i)
                    for n in range(PAIRS):
                        for k in range(DC):
                            last = pe.matmul(S[0:width, 1024 + n * P:1024 + (n + 1) * P], wqk[:, k, n, :], xt[:, k, :],
                                             start=k == 0, stop=k == DC - 1)
                    last.then_inc(g["qk_projected"].sem, 1)
                    hold(pe, g["pt_lo"], i - 1)
                    if isinstance(i, int) and i == 1:
                        hold(pe, g["v_summed"], 1)
                    for k in range(DC):
                        last = pe.matmul(AB[:, 0:D], xt[:, k, :], wv[:, k, :], start=k == 0, stop=k == DC - 1)
                    last.then_inc(g["v_projected"].sem, 1)

                def turn_probs(i, s):
                    pr = probs[:, s * 2048:s * 2048 + 1024]
                    hold(pe, g["exped"], i + 1)
                    hold(pe, g["v_summed"], at_most(i + 2, TILES))
                    hold(pe, g["pt_lo"], i)
                    for n in range(PAIRS):
                        last = pe.transpose(AB[:, n * P:(n + 1) * P], pr[:, n * P:(n + 1) * P], ident)
                    last.then_inc(g["p_turned"].sem, 1)

                def score(i, s):
                    hold(pe, g["qk_copied"], i + 1)
                    hold(pe, g["shifted"], i)
                    for n in range(PAIRS):
                        for b in range(2):
                            o = n * P + b * SEQ
                            q = [q_part(part, s)[0:rows, (n * 2 + b) * P:(n * 2 + b + 1) * P] for part in range(2)]
                            kk = [k_part(part, s)[0:rows, o:o + SEQ] for part in range(2)]
                            last = split_product(S[:, o:o + SEQ], q, kk)
                    last.then_inc(g["scored"].sem, 1)

                def mix_values(i, s):
                    hold(pe, g["pt_lo"], i + 1)
                    hold(pe, g["v_lo"], i + 1)
                    hold(pe, g["o_normed"], i)
                    hold(pe, g["resid"], i)
                    for b in range(2):
                        dst = M if b == 0 else C[:, 256:512]
                        r = slice(b * SEQ, (b + 1) * SEQ)
                        for n in range(PAIRS):
                            turned = [p_part(part, s)[r, n * P:(n + 1) * P] for part in range(2)]
                            v = [v_part(part, s)[r, n * 32:(n + 1) * 32] for part in range(2)]
                            last = split_product(dst[:, n * 32:(n + 1) * 32], turned, v)
                    last.then_inc(g["pv_done"].sem, 1)

                def step(k, s, h):
                    if live(k, 2, TILES):
                        turn_outputs(g, k - 2, 1, s * D)
                    if live(k, 0, TILES):
                        project(k, s)
                    if live(k, 1, TILES):
                        turn_probs(k - 1, 1 - s)
                    if live(k, 2, TILES):
                        out_project(g, k - 2, w["wo"], M[:, 256:512])
                    if live(k, 1, TILES):
                        mix_values(k - 1, 1 - s)
                    if live(k, 0, TILES):
                        score(k, s)
                    if live(k, 2, TILES):
                        turn_rows(g, k - 2)
                skewed(pe, TILES, 2, step)

            def choose(w, base):
                for c in range(CHUNKS):
                    for k in range(DC):
                        last = pe.matmul(S[0:EXPERTS, c * 512:(c + 1) * 512], kc(w, 8)[:, k, :],
                                         XT[:, k, c * 512:(c + 1) * 512], start=k == 0, stop=k == DC - 1)
                last.then_inc(prep_mm, 1)
                pe.wait_ge(prep_dve, base)
                for i in range(TILES):
                    last = pe.transpose(S[:, 1024 + i * 8:1024 + (i + 1) * 8], gateT[0:8, i * P:(i + 1) * P],
                                        ident[0:8, 0:8])
                last.then_inc(prep_mm, 1)

            if "xa0" in RUN:
                cross("xa0")
            if "sa" in RUN:
                inner("sa", SA_ROWS)
            if "ffn" in RUN:
                g, w = G["ffn"], W["ffn"]
                pe.wait_ge(*loaded["ffn"])
                hold(pe, G["sa"]["xt"], TILES)
                choose(w["gate_w"], 1)
                pe.wait_ge(prep_dve, 2)
                pe.matmul(S[:, 1280:1288], ones[:, :], hot2[:, 0:8], start=True, stop=True).then_inc(prep_mm, 1)
                we = w["we"].rearrange("p (c e h) -> p c e h", c=DC, e=EXPERTS)

                def experts(i, s):
                    for n in range(2 * EXPERTS):
                        e, hh = n // 2, n % 2
                        hold(pe, g["relued"], 16 * i + n - 3)
                        o = (n % 4) * 512
                        for k in range(DC):
                            last = pe.matmul(S[:, o:o + P], we[:, k, e, hh * P:(hh + 1) * P],
                                             XT[:, k, bass.ts(i, P)], start=k == 0, stop=k == DC - 1)
                        last.then_inc(g["expert"].sem, 1)

                def back(i, s):
                    hold(pe, g["added"], 14 * (i + 1))
                    hold(pe, g["relued"], 16 * (i + 1))
                    hold(pe, g["resid"], i)
                    for hh in range(DC):
                        last = pe.transpose(M[:, 256 + hh * P:256 + (hh + 1) * P],
                                            acc[:, s * D + hh * P:s * D + (hh + 1) * P], ident)
                    last.then_inc(g["projected"].sem, 1)

                pe.wait_ge(prep_dve, 3)

                def step(k, s, h):
                    if live(k, 1, TILES):
                        back(k - 1, 1 - s)
                    if live(k, 0, TILES):
                        experts(k, s)
                    if live(k, 1, TILES):
                        hold(pe, g["xt"], k - 1)
                        turn_rows(g, k - 1)
                skewed(pe, TILES, 1, step)
            if "xa1" in RUN:
                cross("xa1")
            if "ssm" in RUN:
                g, w = G["ssm"], W["ssm"]
                pe.wait_ge(*loaded["ssm"])
                pe.wait_ge(*loaded["four"])
                bw, ct = kc(w["bw"], D), kc(w["ct"], D)
                fwd, inv = kc(W["four"]["fwd"], D), kc(W["four"]["inv"], D)
                hold(pe, G["xa1"]["weighted"], 4 * SEQS)
                for m in range(DC):
                    for k in range(DC):
                        pe.matmul(S[:, m * D:(m + 1) * D], bw[:, k, m * P:(m + 1) * P], fwd[:, k, :],
                                  start=k == 0, stop=k == DC - 1)
                for m in range(DC):
                    for k in range(DC):
                        pe.matmul(S[:, 512 + m * D:512 + (m + 1) * D], inv[:, k, m * P:(m + 1) * P], ct[:, k, :],
                                  start=k == 0, stop=k == DC - 1)
                pe.matmul(S[:, 1024:1025], W["four"]["sines"], w["a"], start=True, stop=True).then_inc(prep_mm, 1)
                pe.wait_ge(prep_dve, 4)
                pe.transpose(S[:, 1024:1024 + P], tabR[:, :], ident)
                pe.transpose(S[:, 1024 + P:1024 + 2 * P], tabI[:, :], ident).then_inc(prep_mm, 1)
                pe.wait_ge(prep_dve, 5)

                def project(i, s):
                    hold(pe, g["x_copied"], i + 1)
                    hold(pe, g["rotated"], i)
                    for k in range(DC):
                        last = pe.matmul(AB[:, 0:D], xs[:, s * D + k * P:s * D + (k + 1) * P], kc(wb[:, :], D)[:, k, :],
                                         start=k == 0, stop=k == DC - 1)
                    last.then_inc(g["v_projected"].sem, 1)

                def sum_over_time(i, s):
                    hold(pe, g["rotated"], i + 1)
                    hold(pe, g["modulated"], i)
                    for c in range(DC):
                        last = pe.matmul(S[:, c * P:(c + 1) * P], rot[:, s * D + c * P:s * D + (c + 1) * P],
                                         W["const"]["tri"], start=True, stop=True)
                    last.then_inc(g["summed"].sem, 1)

                def out(i, s):
                    hold(pe, g["modulated"], i + 1)
                    hold(pe, g["resid"], i)
                    for c in range(DC):
                        last = pe.matmul(M[:, 256:512], rot2[:, s * D + c * P:s * D + (c + 1) * P],
                                         kc(cg[:, :], D)[:, c, :], start=c == 0, stop=c == DC - 1)
                    last.then_inc(g["projected"].sem, 1)

                def step(k, s, h):
                    if live(k, 2, TILES):
                        out(k - 2, s)
                    if live(k, 0, TILES):
                        project(k, s)
                    if live(k, 1, TILES):
                        sum_over_time(k - 1, 1 - s)
                skewed(pe, TILES, 2, step)
            if "rope" in RUN:
                g = G["rope"]

                def step(k, s, h):
                    hold(pe, g["roped"], k + 1)
                    hold(pe, g["xt"], k)
                    for c in range(DC):
                        last = pe.transpose(C[:, c * P:(c + 1) * P], rot[:, c * P:(c + 1) * P], ident)
                    last.then_inc(g["turned"].sem, 1)
                skewed(pe, TILES, 0, step)
            if "la" in RUN:
                inner("la", LA_ROWS)
            if "moe" in RUN:
                g, w = G["moe"], W["moe"]
                pe.wait_ge(*loaded["moe"])
                hold(pe, G["la"]["xt"], TILES)
                choose(w["router_w"], 6)
                pe.wait_ge(prep_dve, 7)
                for i in range(TILES):
                    pe.transpose(S[0:8, i * P:(i + 1) * P], comb[:, i * 8:(i + 1) * 8], ident).then_inc(prep_mm, 1)
                pe.wait_ge(prep_dve, 8)
                for i in range(TILES):
                    if i >= 2:
                        pe.wait_ge(prep_dve, 9 + i - 2)
                    o = (i % 2) * 512
                    pe.matmul(AB[:, o:o + D], combT[0:8, i * P:(i + 1) * P], w["b3"][0:8, :],
                              start=True, stop=True).then_inc(prep_mm, 1)
                pe.wait_ge(prep_dve, 8 + TILES)

                def hidden(m, u, h):
                    c, s = u % 2, (u // 2) % 2
                    w1 = w12[s].rearrange("p (c n) -> p c n", c=DC)
                    if c == 0:
                        pe.wait_ge(w_loaded[s], 32 * (h + 1))
                    for f in range(FT):
                        hold(pe, g["gated"], 8 * m + f - 1)
                        for half_ in range(2):
                            o = (f % 2) * 1024 + half_ * 512
                            for k in range(DC):
                                last = pe.matmul(S[:, o:o + 512], w1[:, k, half_ * FF + f * P:half_ * FF + (f + 1) * P],
                                                 XT[:, k, c * CHUNK:(c + 1) * CHUNK], start=k == 0, stop=k == DC - 1)
                        last.then_inc(g["hidden"].sem, 1)

                def down(m, u):
                    s = (u // 2) % 2
                    wd = w3[s].rearrange("p (f n) -> p f n", f=FT)
                    hold(pe, g["gated"], 8 * (m + 1))
                    for i in range(4):
                        hold(pe, g["out"], 4 * m + i - 3)
                        for f in range(FT):
                            last = pe.matmul(sums[i], hid[u % 2][:, f, i * P:(i + 1) * P],
                                             wd[:, f, :], start=f == 0, stop=f == FT - 1)
                        last.then_inc(g["chunk_out"].sem, 1)

                def step(k, u, h):
                    if live(k, 0, CHUNKS * EXPERTS):
                        hidden(k, u, h)
                    if live(k, 1, CHUNKS * EXPERTS):
                        down(k - 1, (u - 1) % 4)
                skewed(pe, CHUNKS * EXPERTS, 1, step, unroll=4)

        @block.scalar
        def _(act):
            def copy_outputs(g, h):
                hold(act, g["o_turned"], h + 1)
                act.activation(ot[:, :].rearrange("p (a b q) -> p b a q", a=2, b=2),
                               C[:, 0:256].rearrange("p (b a q) -> p b a q", b=2, a=2), ACT.Copy)\
                   .then_inc(g["o_copied"].sem, 1)

            def copy_turned(g, h):
                hold(act, g["turned"], h + 1)
                act.activation(XT[:, :, bass.ts(h, P)], C[:, 0:256].rearrange("p (c n) -> p c n", c=DC), ACT.Copy)\
                   .then_inc(g["xt"].sem, 1)

            skewed(act, TILES, 0, lambda k, s, h: copy_turned(G["ln"], k))

            def cross(st):
                g, w = G[st], W[st]
                act.wait_ge(*loaded[st])

                def copy_keys(b, s):
                    hold(act, g["k_projected"], b + 1)
                    for hf in range(2):
                        last = act.activation(k_part(0, s)[:, hf * KEYS:(hf + 1) * KEYS],
                                              AB[:, hf * KEYS:(hf + 1) * KEYS], ACT.Identity,
                                              bias=w["bk"][:, hf:hf + 1])
                    last.then_inc(g["k_hi"].sem, 1)
                    hold(act, g["v_summed"], b + 1)
                    act.activation(v_part(0, s), vsum[:, :], ACT.Copy).then_inc(g["v_hi"].sem, 1)

                def copy_probs(b, s):
                    for c in range(4):
                        hold(act, g["p_turned"], 4 * b + c + 1)
                        act.activation(p_part(0, s)[:, c * 512:(c + 1) * 512],
                                       AB[:, (c % 2) * 512:(c % 2 + 1) * 512], ACT.Copy).then_inc(g["pt_hi"].sem, 1)

                def exps(b, s):
                    for n in range(PAIRS):
                        hold(act, g["masked"], 8 * b + n + 1)
                        p = probs[:, s * 2048 + n * KEYS:s * 2048 + (n + 1) * KEYS]
                        act.activation(p, p, ACT.Exp, bias=mx[:, s * HEADS + n:s * HEADS + n + 1], scale=-1.0,
                                       accum_out=ssum[:, s * HEADS + n:s * HEADS + n + 1])\
                           .then_inc(g["powered"].sem, 1)

                def plain_exps(b, s):
                    hold(act, g["maxima"], 2 * b + 2)
                    for n in range(PAIRS):
                        o = (n % 4) * 512 + (n // 4) * KEYS
                        last = act.activation(probs[:, s * 2048 + n * KEYS:s * 2048 + (n + 1) * KEYS], S[:, o:o + KEYS],
                                              ACT.Exp, bias=mx[:, s * HEADS + n:s * HEADS + n + 1],
                                              accum_out=ssum[:, s * HEADS + n:s * HEADS + n + 1])
                        if n % 2 == 1:
                            last.then_inc(g["weighted"].sem, 1)

                def step(k, s, h):
                    if live(k, 2, SEQS) and s == 1:
                        copy_outputs(g, h - 1)
                    if live(k, 0, SEQS):
                        copy_keys(k, s)
                    if live(k, 1, SEQS):
                        copy_probs(k - 1, 1 - s)
                    if live(k, 0, SEQS):
                        (exps if st == "xa0" else plain_exps)(k, s)
                    if live(k, 2, SEQS) and s == 1:
                        copy_turned(g, h - 1)
                skewed(act, SEQS, 2, step)

            def inner(st, width, scale):
                g = G[st]

                def step(k, s, h):
                    if live(k, 2, TILES):
                        copy_outputs(g, k - 2)
                    if live(k, 0, TILES):
                        hold(act, g["qk_summed"], k + 1)
                        act.activation(k_part(0, s)[0:width], scratch[0:width, :], ACT.Copy)\
                           .then_inc(g["qk_hi"].sem, 1)
                        hold(act, g["v_summed"], k + 1)
                        act.activation(v_part(0, s)[:, 0:D], vsum[:, 0:D], ACT.Copy).then_inc(g["v_hi"].sem, 1)
                    if live(k, 1, TILES):
                        hold(act, g["p_turned"], k)
                        act.activation(p_part(0, 1 - s)[:, 0:1024], AB[:, :], ACT.Copy).then_inc(g["pt_hi"].sem, 1)
                    if live(k, 0, TILES):
                        hold(act, g["shifted"], k + 1)
                        p = probs[:, s * 2048:s * 2048 + 1024]
                        act.activation(p, p, ACT.Exp, scale=scale).then_inc(g["exped"].sem, 1)
                    if live(k, 2, TILES):
                        if st == "la":
                            hold(act, g["resid"], k - 1)
                            hold(act, g["rstd"], k - 2)
                            act.activation(junk[:, :], tile(xn_all, k - 2), ACT.Square, scale=D ** -0.5,
                                           accum_out=mv[:, 0:1])\
                               .then_inc(g["squared"].sem, 1)
                        copy_turned(g, k - 2)
                skewed(act, TILES, 2, step)

            if "xa0" in RUN:
                cross("xa0")
            if "sa" in RUN:
                inner("sa", P, (DH + ROT) ** -0.5)
            if "ffn" in RUN:
                g = G["ffn"]
                act.wait_ge(prep_dve, 3)

                def relus(i, s):
                    for n in range(2 * EXPERTS):
                        hold(act, g["expert"], 16 * i + n + 1)
                        if n < 2:
                            out = acc[:, s * D + n * P:s * D + (n + 1) * P]
                        else:
                            hold(act, g["added"], 14 * i + max(n - 5, 0))
                            out = relu[:, (n % 4) * P:(n % 4 + 1) * P]
                        act.activation(out, S[:, (n % 4) * 512:(n % 4) * 512 + P], ACT.Relu, bias=bec[:, n:n + 1],
                                       scale=counts[:, n // 2:n // 2 + 1]).then_inc(g["relued"].sem, 1)

                def step(k, s, h):
                    if live(k, 0, TILES):
                        relus(k, s)
                    if live(k, 1, TILES):
                        copy_turned(g, k - 1)
                skewed(act, TILES, 1, step)
            if "xa1" in RUN:
                cross("xa1")
            if "rope" in RUN:
                g = G["rope"]

                def step(k, s, h):
                    hold(act, G["ssm"]["normed"], k + 1)
                    hold(act, g["rstd"], k)
                    act.activation(junk[:, :], tile(xn_all, k), ACT.Square, scale=D ** -0.5,
                                           accum_out=mv[:, 0:1])\
                       .then_inc(g["squared"].sem, 1)
                    copy_turned(g, k)
                hold(act, G["ssm"]["normed"], TILES)
                skewed(act, TILES, 0, step)
            if "la" in RUN:
                inner("la", 4 * DH, DH ** -0.5)
            if "moe" in RUN:
                g, w = G["moe"], W["moe"]
                act.wait_ge(prep_dve, 6)
                act.wait_ge(made, 5)
                act.activation(wgt[:, 8:16], wgt[:, 0:8], ACT.Exp).then_inc(prep_act, 1)

                def step(m, u, h):
                    e = 2 * h + u // 2
                    for f in range(FT):
                        hold(act, g["hidden"], 8 * m + f + 1)
                        hold(act, g["gated"], 8 * m + f - 1)
                        act.sem_inc(act_passed, 1)
                        act.activation(gated[:, (f % 2) * CHUNK:(f % 2 + 1) * CHUNK],
                                       S[:, (f % 2) * 1024:(f % 2) * 1024 + 512], ACT.Silu,
                                       bias=w["b1"][:, bass.ds(e * FT + f, 1)]).then_inc(g["silued"].sem, 1)
                skewed(act, CHUNKS * EXPERTS, 0, step, unroll=4)

        @block.gpsimd
        def _(pool):
            chain = Chain(pool, pool_chain)
            for i, value in enumerate((-0.5, LN_EPS, RMS_EPS)):
                pool.memset(half[:, i:i + 1], value).then_inc(made, 1)
            pool.memset(ones[:, :], 1.0).then_inc(made, 1)
            pool.wait_ge(made, 4)

            def inverse_root(g, h, eps, source, waited, signal):
                hold(pool, g[waited], h + 1)
                chain.link(pool.tensor_tensor(var[:, :], source, half[:, eps:eps + 1], ALU.add))
                pool.tensor_tensor(rstd[:, :], var[:, :], half[:, 0:1], ALU.pow).then_inc(g[signal].sem, 1)

            def settle():
                pool.sem_inc(pool_passed, 1)

            def root_of_variance(g, h):
                inverse_root(g, h, 1, mv[:, 1:2], "stats", "rstd")

            def add_bias(g, h, bias, ready):
                hold(pool, ready, h + 1)
                pool.tensor_tensor(tile(x, h), tile(x, h), bias, ALU.add).then_inc(g["biased"].sem, 1)

            def ln_step(k, s, h):
                root_of_variance(G["ln"], k)
                chain.restart()
            skewed(pool, TILES, 0, ln_step)

            def split_values(g, i, s, cols):
                hold(pool, g["v_hi"], i + 1)
                pool.tensor_tensor(v_part(1, s)[:, 0:cols], vsum[:, 0:cols], v_part(0, s)[:, 0:cols], ALU.subtract)\
                    .then_inc(g["v_lo"].sem, 1)

            def cross(st):
                g, w, prev = G[st], W[st], G[PREV[st]]
                pool.wait_ge(*loaded[st])

                def negate_mask(b, s, h):
                    pool.wait_ge(ctx_loaded[s], ctx_count(st, h))
                    hold(pool, g["masked"], 8 * (b - 1))
                    settle()
                    pool.tensor_scalar(neg[:, s * KEYS:(s + 1) * KEYS], mask_i[:, s * KEYS:(s + 1) * KEYS],
                                       1.0e9, -1.0e9, ALU.mult, ALU.add).then_inc(G["xa0"]["negated"].sem, 1)

                def weigh(b, s):
                    for c in range(4):
                        hold(pool, g["powered"], 8 * b + 2 * c + 2)
                        p = probs[:, s * 2048 + c * 512:s * 2048 + (c + 1) * 512].rearrange("p (n k) -> p n k", n=2)
                        gw = gp[:, s * KEYS:(s + 1) * KEYS].unsqueeze(1).broadcast_to([P, 2, KEYS])
                        pool.tensor_tensor(p, p, gw, ALU.mult).then_inc(g["weighted"].sem, 1)

                def step(k, s, h):
                    if live(k, 0, SEQS):
                        if st == "xa0":
                            negate_mask(k, s, h)
                        if s == 0:
                            hold(pool, prev["normed"], h + 1)
                            add_bias(g, h, w["bo"], prev["resid"] if st == "xa1" else prev["normed"])
                    if live(k, 0, SEQS):
                        split_values(g, k, s, 2 * D)
                    if live(k, 2, SEQS) and s == 1:
                        root_of_variance(g, h - 1)
                    if live(k, 0, SEQS) and st == "xa0":
                        weigh(k, s)
                    if st == "xa1" and live(k, 2, SEQS) and s == 1:
                        hold(pool, g["normed"], h)
                        settle()
                        pool.tensor_copy(tile(xn_all, h - 1), xn[:, :]).then_inc(g["kept"].sem, 1)
                    chain.restart()
                skewed(pool, SEQS, 2, step)

            def copy_tile(g, prev_xt, k, s, readers):
                hold(pool, prev_xt, k + 1)
                hold(pool, g[readers], k - 1)
                settle()
                pool.tensor_copy(xs[:, s * D:(s + 1) * D].rearrange("p (c n) -> p c n", c=DC),
                                 XT[:, :, bass.ts(k, P)]).then_inc(g["x_copied"].sem, 1)

            def inner(st):
                g, w, prev = G[st], W[st], G[PREV[st]]
                pool.wait_ge(*loaded[st])

                def step(k, s, h):
                    if live(k, 0, TILES):
                        copy_tile(g, prev["xt"], k, s, "v_projected")
                        if st == "sa":
                            hold(pool, prev["normed"], k + 1)
                            add_bias(g, k, w["bo"], prev["resid"])
                        split_values(g, k, s, D)
                    if live(k, 2, TILES):
                        if st == "sa":
                            root_of_variance(g, k - 2)
                        else:
                            inverse_root(g, k - 2, 2, mv[:, 0:1], "squared", "rstd")
                            pool.tensor_tensor(tile(x, k - 2), tile(x, k - 2), tile(xn_all, k - 2), ALU.add)\
                                .then_inc(g["summed_up"].sem, 1)
                    chain.restart()
                skewed(pool, TILES, 2, step)

            if "xa0" in RUN:
                cross("xa0")
            if "sa" in RUN:
                inner("sa")
            if "ffn" in RUN:
                def ffn_step(k, s, h):
                    if live(k, 1, TILES):
                        root_of_variance(G["ffn"], k - 1)
                    chain.restart()
                skewed(pool, TILES, 1, ffn_step)
            if "xa1" in RUN:
                cross("xa1")
            if "ssm" in RUN:
                g, w = G["ssm"], W["ssm"]
                pool.wait_ge(*loaded["ssm"])

                def ssm_step(k, s, h):
                    if live(k, 0, TILES):
                        copy_tile(g, G["xa1"]["xt"], k, s, "v_projected")
                        hold(pool, G["xa1"]["kept"], k + 1)
                        hold(pool, g["biased"], k)
                        chain.link(pool.tensor_tensor(junk[:, :], tile(xn_all, k), w["d"], ALU.mult))
                        pool.tensor_tensor(tile(x, k), tile(x, k), junk[:, :], ALU.add).then_inc(g["biased"].sem, 1)
                    if live(k, 2, TILES):
                        root_of_variance(g, k - 2)
                    chain.restart()
                skewed(pool, TILES, 2, ssm_step)
            if "rope" in RUN:
                def rope_step(k, s, h):
                    inverse_root(G["rope"], k, 2, mv[:, 0:1], "squared", "rstd")
                    chain.restart()
                skewed(pool, TILES, 0, rope_step)
            if "la" in RUN:
                inner("la")

        @block.vector
        def _(dve):
            chain = Chain(dve, dve_chain)
            dve.wait_ge(*loaded["x"])
            dve.wait_ge(*loaded["const"])
            K = W["const"]

            def settle():
                dve.sem_inc(dve_passed, 1)

            def tile_stats(g, h):
                chain.link(dve.bn_stats(stat6[:, :], tile(x, h)))
                dve.bn_aggr(mv[:, :], stat6[:, :]).then_inc(g["stats"].sem, 1)

            def normalise(g, h, out):
                hold(dve, g["rstd"], h + 1)
                dve.tensor_scalar(out, tile(x, h), mv[:, 0:1], rstd[:, :], ALU.subtract, ALU.mult)\
                   .then_inc(g["normed"].sem, 1)

            def add_output(g, h, src):
                hold(dve, g["projected"], h + 1)
                if "biased" in g:
                    hold(dve, g["biased"], h + 1)
                dve.tensor_tensor(tile(x, h), src, tile(x, h), ALU.add).then_inc(g["resid"].sem, 1)
                hold(dve, g["resid"], h + 1)
                settle()

            def ln_step(k, s, h):
                tile_stats(G["ln"], k)
                hold(dve, G["ln"]["turned"], k)
                normalise(G["ln"], k, xn[:, :])
                chain.restart()
            skewed(dve, TILES, 0, ln_step)

            def cross(st):
                g, w = G[st], W[st]
                dve.wait_ge(*loaded[st])

                def copy_queries(h):
                    hold(dve, g["q_projected"], h + 1)
                    q = scratch[:, 0:256]
                    for hf in range(2):
                        chain.mark(dve.tensor_scalar(q[:, hf * P:(hf + 1) * P], M[:, 256 + hf * P:256 + (hf + 1) * P],
                                                     w["bq"][:, hf:hf + 1], DH ** -0.5, ALU.add, ALU.mult))
                    chain.join()
                    chain.link(dve.tensor_copy(qsplit[:, 0:256], q))
                    chain.link(dve.tensor_tensor(qsplit[:, 256:512], q, qsplit[:, 0:256], ALU.subtract))
                    for part in range(2):
                        src = qsplit[:, part * 256:(part + 1) * 256].rearrange("p (f b q) -> p b f q", f=2, b=2)
                        both = qbuf[:, part * 4096:(part + 1) * 4096].rearrange("p (b r) -> p b r", b=2)[:, :, 0:256]
                        blocks = both.rearrange("p b (f a q) -> p b f a q", f=2, a=2)
                        for par in range(2):
                            last = dve.tensor_scalar(blocks[:, :, :, par, :], src, K["par_x"][:, par:par + 1], None,
                                                     ALU.mult)
                            if part == 0 or par == 0:
                                chain.mark(last)
                    last.then_inc(g["q_copied"].sem, 1)
                    hold(dve, g["q_copied"], h + 1)

                def sum_values(b, s):
                    hold(dve, g["v_projected"], b + 1)
                    hold(dve, g["v_lo"], b)
                    dve.tensor_tensor(vsum[:, :].rearrange("p (k n) -> p k n", k=2),
                                      AB[:, 512:1024].rearrange("p (k n) -> p k n", k=2),
                                      w["bv"].unsqueeze(1).broadcast_to([P, 2, D]), ALU.add)\
                       .then_inc(g["v_summed"].sem, 1)

                def split_keys(b, s):
                    hold(dve, g["k_hi"], b + 1)
                    for hf in range(2):
                        r = slice(hf * KEYS, (hf + 1) * KEYS)
                        last = dve.scalar_tensor_tensor(out=k_part(1, s)[:, r], in0=AB[:, r],
                                                        scalar=w["bk"][:, hf:hf + 1], in1=k_part(0, s)[:, r],
                                                        op0=ALU.add, op1=ALU.subtract)
                    last.then_inc(g["k_copied"].sem, 1)

                def split_probs(b, s):
                    for c in range(4):
                        hold(dve, g["pt_hi"], 4 * b + c + 1)
                        r = slice(c * 512, (c + 1) * 512)
                        dve.tensor_tensor(p_part(1, s)[:, r], AB[:, (c % 2) * 512:(c % 2 + 1) * 512],
                                          p_part(0, s)[:, r], ALU.subtract).then_inc(g["pt_lo"].sem, 1)

                def mask_scores(b, s):
                    hold(dve, G["xa0"]["negated"], b + 1)
                    hold(dve, g["scored"], b + 1)
                    settle()
                    for n in range(PAIRS):
                        o = (n % 4) * 512 + (n // 4) * KEYS
                        dve.tensor_tensor_reduce(out=probs[:, s * 2048 + n * KEYS:s * 2048 + (n + 1) * KEYS],
                                                 in0=S[:, o:o + KEYS], in1=neg[:, s * KEYS:(s + 1) * KEYS],
                                                 scale=-1.0, scalar=BIG, op0=ALU.add, op1=ALU.min,
                                                 accum_out=mx[:, s * HEADS + n:s * HEADS + n + 1])\
                           .then_inc(g["masked"].sem, 1)

                def row_maxima(b, s):
                    banks = S.rearrange("p (j f k) -> p f j k", j=4, f=2)
                    hold(dve, g["scored"], b + 1)
                    for hf in range(2):
                        dve.tensor_reduce(mx[:, s * HEADS + 4 * hf:s * HEADS + 4 * hf + 4], banks[:, hf, :, :],
                                          AX.X, ALU.max, negate=True).then_inc(g["maxima"].sem, 1)

                def normalise_outputs(b, s):
                    hold(dve, g["pv_done"], b + 1)
                    r = rsum[:, s * HEADS:s * HEADS + PAIRS]
                    chain.link(dve.reciprocal(r, ssum[:, s * HEADS:s * HEADS + PAIRS]))
                    for par in range(2):
                        rows = slice(par * SEQ, (par + 1) * SEQ)
                        last = dve.tensor_tensor(
                            obuf[rows, s * P:(s + 1) * P].rearrange("p (n d) -> p n d", n=PAIRS),
                            M[rows, 0:256].rearrange("p (n a d) -> p n a d", n=PAIRS, a=2)[:, :, par, :],
                            r[rows, :].unsqueeze(2).broadcast_to([SEQ, PAIRS, DH]), ALU.mult)
                    last.then_inc(g["o_normed"].sem, 1)

                def step(k, s, h):
                    closes = live(k, 2, SEQS) and s == 1
                    if live(k, 0, SEQS):
                        split_keys(k, s)
                        sum_values(k, s)
                        if s == 0:
                            copy_queries(h)
                    if live(k, 1, SEQS):
                        split_probs(k - 1, 1 - s)
                    if closes:
                        add_output(g, h - 1, C[:, 256:512])
                        tile_stats(g, h - 1)
                    if live(k, 0, SEQS):
                        (mask_scores if st == "xa0" else row_maxima)(k, s)
                    if live(k, 1, SEQS):
                        normalise_outputs(k - 1, 1 - s)
                    if closes:
                        if st == "xa1":
                            hold(dve, g["kept"], h - 1)
                        normalise(g, h - 1, xn[:, :])
                    chain.restart()
                skewed(dve, SEQS, 2, step)

            def inner(st, rows):
                g, w = G[st], W[st]
                dve.wait_ge(*loaded[st])
                blocks_of = K["par_s" if st == "sa" else "par_x"]
                width = rows + 2 * DH

                def sum_projections(i, s):
                    hold(dve, g["qk_projected"], i + 1)
                    hold(dve, g["qk_copied"], i)
                    full = scratch[0:width, :].rearrange("p (n q) -> p n q", n=PAIRS)
                    src = S[0:width, 1024:2048].rearrange("p (n q) -> p n q", n=PAIRS)
                    if st == "sa":
                        sums = dve.tensor_tensor(full, src, w["b"].unsqueeze(2).broadcast_to([P, PAIRS, P]), ALU.add)
                    else:
                        sums = dve.tensor_copy(full, src)
                    sums.then_inc(g["qk_summed"].sem, 1)
                    hold(dve, g["v_projected"], i + 1)
                    hold(dve, g["v_lo"], i)
                    if st == "sa":
                        sums = dve.tensor_tensor(vsum[:, 0:D], AB[:, 0:D], w["bv"], ALU.add)
                    else:
                        sums = dve.tensor_copy(vsum[:, 0:D], AB[:, 0:D])
                    sums.then_inc(g["v_summed"].sem, 1)

                def split_queries_and_keys(i, s):
                    hold(dve, g["qk_hi"], i + 1)
                    chain.link(dve.tensor_tensor(k_part(1, s)[0:width], scratch[0:width, :], k_part(0, s)[0:width],
                                                 ALU.subtract))
                    for part in range(2):
                        src = k_part(part, s)[0:rows].rearrange("p (n q) -> p n q", q=SEQ)
                        out = q_part(part, s)[0:rows].rearrange("p (n a q) -> p n a q", n=HEADS, a=2)
                        for par in range(2):
                            chain.mark(dve.tensor_scalar(out[:, :, par, :], src, blocks_of[0:rows, par:par + 1], None,
                                                         ALU.mult))
                    chain.join()
                    for part in range(2):
                        last = dve.tensor_copy(k_part(part, s)[0:2 * DH], k_part(part, s)[rows:width])
                    last.then_inc(g["qk_copied"].sem, 1)

                def split_probs(i, s):
                    hold(dve, g["pt_hi"], i + 1)
                    dve.tensor_tensor(p_part(1, s)[:, 0:1024], AB[:, :], p_part(0, s)[:, 0:1024], ALU.subtract)\
                       .then_inc(g["pt_lo"].sem, 1)

                def shift_scores(i, s):
                    hold(dve, g["scored"], i + 1)
                    p = probs[:, s * 2048:s * 2048 + 1024].rearrange("p (n k) -> p n k", n=HEADS)
                    src = S[:, 0:1024].rearrange("p (n k) -> p n k", n=HEADS)
                    if st == "la":
                        chain.link(dve.tensor_tensor(p, src, K["causal"].unsqueeze(1).broadcast_to([P, HEADS, SEQ]),
                                                     ALU.add))
                        src = p
                    m = mx[:, s * HEADS:(s + 1) * HEADS]
                    chain.link(dve.tensor_reduce(m, src, AX.X, ALU.max, negate=True))
                    dve.tensor_tensor(p, src, m.unsqueeze(2).broadcast_to([P, HEADS, SEQ]), ALU.add)\
                       .then_inc(g["shifted"].sem, 1)

                def normalise_outputs(i, s):
                    p = probs[:, s * 2048:s * 2048 + 1024].rearrange("p (n k) -> p n k", n=HEADS)
                    hold(dve, g["exped"], i + 1)
                    z = ssum[:, s * HEADS:(s + 1) * HEADS]
                    r = rsum[:, s * HEADS:(s + 1) * HEADS]
                    chain.link(dve.tensor_reduce(z, p, AX.X, ALU.add))
                    chain.link(dve.reciprocal(r, z))
                    hold(dve, g["pv_done"], i + 1)
                    for b in range(2):
                        src = M[:, 0:256] if b == 0 else C[:, 256:512]
                        for par in range(2):
                            q = slice(par * SEQ, (par + 1) * SEQ)
                            last = dve.tensor_tensor(
                                obuf[q, s * D + b * P:s * D + (b + 1) * P].rearrange("p (n d) -> p n d", n=PAIRS),
                                src[q].rearrange("p (n a d) -> p n a d", n=PAIRS, a=2)[:, :, par, :],
                                r[q].rearrange("p (n b) -> p n b", b=2)[:, :, b:b + 1].broadcast_to([SEQ, PAIRS, DH]),
                                ALU.mult)
                    last.then_inc(g["o_normed"].sem, 1)

                def step(k, s, h):
                    if live(k, 0, TILES):
                        sum_projections(k, s)
                    if live(k, 1, TILES):
                        split_probs(k - 1, 1 - s)
                    if live(k, 0, TILES):
                        split_queries_and_keys(k, s)
                    if live(k, 2, TILES):
                        if st == "sa":
                            add_output(g, k - 2, M[:, 256:512])
                            tile_stats(g, k - 2)
                        else:
                            hold(dve, g["projected"], k - 1)
                            dve.tensor_tensor(tile(xn_all, k - 2), M[:, 256:512], tile(xn_all, k - 2), ALU.add)\
                               .then_inc(g["resid"].sem, 1)
                    if live(k, 1, TILES):
                        normalise_outputs(k - 1, 1 - s)
                    if live(k, 0, TILES):
                        shift_scores(k, s)
                    if live(k, 2, TILES):
                        if st == "sa":
                            normalise(g, k - 2, xn[:, :])
                        else:
                            hold(dve, g["rstd"], k - 1)
                            dve.scalar_tensor_tensor(out=xn[:, :], in0=tile(xn_all, k - 2), scalar=rstd[:, :],
                                                     in1=w["norm2"], op0=ALU.mult, op1=ALU.mult)\
                               .then_inc(g["normed"].sem, 1)
                    chain.restart()
                skewed(dve, TILES, 2, step)

            def choose(bias, mm):
                dve.wait_ge(prep_mm, mm)
                dve.tensor_scalar(gateT[0:8, :], S[0:8, 0:TOKENS], bias[0:8, :], None, ALU.add).then_inc(prep_dve, 1)
                dve.wait_ge(prep_mm, mm + 1)
                chain.link(dve.tensor_copy(logit[:, :], S[:, 1024:1024 + 64]))
                for i in range(TILES):
                    r = slice(i * 8, (i + 1) * 8)
                    chain.mark(dve.max(top[:, r], logit[:, r]))
                chain.join()
                for i in range(TILES):
                    r = slice(i * 8, (i + 1) * 8)
                    chain.mark(dve.max_index(topi[:, r], top[:, r], logit[:, r]))
                chain.join()
                chain.link(dve.tensor_copy(topf[:, :], topi[:, :]))
                for i in range(TILES):
                    for rank, dst in ((0, hot), (1, hot2)):
                        chain.mark(dve.tensor_scalar(dst[:, i * 8:(i + 1) * 8], K["iota"],
                                                     topf[:, i * 8 + rank:i * 8 + rank + 1], None, ALU.is_equal))
                chain.join()

            if "xa0" in RUN:
                cross("xa0")
            if "sa" in RUN:
                inner("sa", SA_ROWS)
            if "ffn" in RUN:
                g, w = G["ffn"], W["ffn"]
                dve.wait_ge(*loaded["ffn"])
                choose(w["gate_b"], 1)
                chain.link(dve.tensor_tensor(hot[:, :], hot[:, :], hot2[:, :], ALU.add))
                dve.tensor_reduce(hot2[:, 0:8], hot[:, :].rearrange("p (t e) -> p e t", e=8), AX.X, ALU.add)\
                   .then_inc(prep_dve, 1)
                dve.wait_ge(prep_mm, 3)
                chain.link(dve.tensor_scalar(counts[:, :], S[:, 1280:1288], 1.0 / (2 * TOKENS), None, ALU.mult))
                dve.tensor_tensor(bec[:, :].rearrange("p (e f) -> p e f", e=8), w["be"].rearrange("p (e f) -> p e f", e=8),
                                  counts[:, :].unsqueeze(2).broadcast_to([P, 8, 2]), ALU.mult).then_inc(prep_dve, 1)
                chain.restart()

                def add_experts(i, s):
                    for n in range(2, 2 * EXPERTS):
                        hold(dve, g["relued"], 16 * i + n + 1)
                        if n >= 4:
                            hold(dve, g["added"], 14 * i + n - 3)
                        a = acc[:, s * D + (n % 2) * P:s * D + (n % 2 + 1) * P]
                        dve.tensor_tensor(a, a, relu[:, (n % 4) * P:(n % 4 + 1) * P], ALU.add).then_inc(g["added"].sem, 1)

                def step(k, s, h):
                    if live(k, 1, TILES):
                        add_output(g, k - 1, M[:, 256:512])
                        tile_stats(g, k - 1)
                    if live(k, 0, TILES):
                        add_experts(k, s)
                    if live(k, 1, TILES):
                        normalise(g, k - 1, xn[:, :])
                    chain.restart()
                skewed(dve, TILES, 1, step)
            if "xa1" in RUN:
                cross("xa1")
            if "ssm" in RUN:
                g = G["ssm"]
                dve.wait_ge(prep_mm, 4)
                chain.mark(dve.tensor_copy(wb[:, :], S[:, 0:512]))
                chain.mark(dve.tensor_copy(cg[:, :], S[:, 512:1024]))
                col = [lam[:, i:i + 1] for i in range(8)]
                omega, sq, den, lr, li, sq2, lr2, li2 = col
                chain.link(dve.tensor_copy(omega, S[:, 1024:1025]))
                chain.link(dve.tensor_tensor(sq, omega, omega, ALU.mult))
                chain.link(dve.tensor_scalar(den, sq, 1.0, None, ALU.add))
                chain.link(dve.reciprocal(sq2, den))
                chain.link(dve.tensor_scalar(sq, sq, -1.0, 1.0, ALU.mult, ALU.add))
                chain.mark(dve.tensor_tensor(lr, sq, sq2, ALU.mult))
                chain.link(dve.tensor_scalar(li, omega, sq2, -2.0, ALU.mult, ALU.mult))
                chain.mark(dve.memset(tabR[:, 0:1], 1.0))
                chain.link(dve.memset(tabI[:, 0:1], 0.0))
                m = 1
                while m < SEQ:
                    chain.link(dve.tensor_scalar(tabt[:, 0:m], tabI[:, 0:m], li, None, ALU.mult))
                    chain.link(dve.scalar_tensor_tensor(out=tabR[:, m:2 * m], in0=tabR[:, 0:m], scalar=lr,
                                                        in1=tabt[:, 0:m], op0=ALU.mult, op1=ALU.subtract))
                    chain.link(dve.tensor_scalar(tabt[:, 0:m], tabR[:, 0:m], li, None, ALU.mult))
                    chain.link(dve.scalar_tensor_tensor(out=tabI[:, m:2 * m], in0=tabI[:, 0:m], scalar=lr,
                                                        in1=tabt[:, 0:m], op0=ALU.mult, op1=ALU.add))
                    chain.mark(dve.tensor_tensor(sq, li, li, ALU.mult))
                    chain.link(dve.tensor_tensor(sq2, lr, lr, ALU.mult))
                    chain.mark(dve.tensor_tensor(lr2, sq2, sq, ALU.subtract))
                    chain.link(dve.tensor_scalar(li2, lr, li, 2.0, ALU.mult, ALU.mult))
                    lr, lr2, li, li2 = lr2, lr, li2, li
                    m *= 2
                dve.tensor_copy(tabR[:, SEQ:], tabR[:, 0:SEQ])
                dve.tensor_copy(tabI[:, SEQ:], tabI[:, 0:SEQ]).then_inc(prep_dve, 1)
                dve.wait_ge(prep_dve, 4)
                dve.wait_ge(prep_mm, 5)
                dve.tensor_copy(rowR[:, :], S[:, 1024:1024 + P])
                dve.tensor_copy(rowI[:, :], S[:, 1024 + P:1024 + 2 * P]).then_inc(prep_dve, 1)
                dve.wait_ge(prep_dve, 5)
                chain.restart()

                def turn_phase(src, real, imag, forward, out, s):
                    a = acc[:, 0:D].rearrange("p (c n) -> p c n", c=DC)
                    v = src.rearrange("p (c n) -> p c n", c=DC)
                    chain.mark(dve.tensor_tensor(a, v, real.unsqueeze(1).broadcast_to([P, DC, P]), ALU.mult))
                    b = acc[:, D:2 * D]
                    chain.mark(dve.tensor_tensor(b[:, 0:P], src[:, P:2 * P], imag, ALU.mult))
                    chain.link(dve.tensor_tensor(b[:, P:2 * P], src[:, 0:P], imag, ALU.mult))
                    chain.mark(dve.tensor_tensor(out[:, s * D:s * D + P], acc[:, 0:P], b[:, 0:P],
                                                 ALU.subtract if forward else ALU.add))
                    return dve.tensor_tensor(out[:, s * D + P:(s + 1) * D], acc[:, P:2 * P], b[:, P:2 * P],
                                             ALU.add if forward else ALU.subtract)

                def step(k, s, h):
                    if live(k, 2, TILES):
                        add_output(g, k - 2, M[:, 256:512])
                        tile_stats(g, k - 2)
                    if live(k, 0, TILES):
                        hold(dve, g["v_projected"], k + 1)
                        turn_phase(AB[:, 0:D], rowR[:, :], rowI[:, :], False, rot, s).then_inc(g["rotated"].sem, 1)
                        hold(dve, g["rotated"], k + 1)
                    if live(k, 1, TILES):
                        hold(dve, g["summed"], k)
                        turn_phase(S[:, 0:D], tabR[:, :], tabI[:, :], True, rot2, 1 - s).then_inc(g["modulated"].sem, 1)
                        hold(dve, g["modulated"], k)
                    if live(k, 2, TILES):
                        normalise(g, k - 2, tile(xn_all, k - 2))
                    chain.restart()
                skewed(dve, TILES, 2, step)
            if "rope" in RUN:
                g = G["rope"]
                dve.wait_ge(*loaded["la"])

                def step(k, s, h):
                    hold(dve, g["rstd"], k + 1)
                    hold(dve, g["roped"], k)
                    xr = rot2[:, 0:D]
                    chain.link(dve.scalar_tensor_tensor(out=xr, in0=tile(xn_all, k), scalar=rstd[:, :],
                                                        in1=W["la"]["norm1"], op0=ALU.mult, op1=ALU.mult))
                    xe, xo = (xr.rearrange("p (n a) -> p n a", a=2)[:, :, a] for a in range(2))
                    for j, (v, tab) in enumerate(((xe, "cos"), (xo, "sin"), (xe, "sin"), (xo, "cos"))):
                        chain.mark(dve.tensor_tensor(acc[:, j * P:(j + 1) * P], v, K[tab], ALU.mult))
                    chain.join()
                    hold(dve, g["turned"], k)
                    dve.tensor_tensor(rot[:, 0:P], acc[:, 0:P], acc[:, P:2 * P], ALU.subtract)
                    dve.tensor_tensor(rot[:, P:2 * P], acc[:, 2 * P:3 * P], acc[:, 3 * P:4 * P], ALU.add)\
                       .then_inc(g["roped"].sem, 1)
                    chain.restart()
                skewed(dve, TILES, 0, step)
            if "la" in RUN:
                inner("la", LA_ROWS)
            if "moe" in RUN:
                g, w = G["moe"], W["moe"]
                dve.wait_ge(*loaded["moe"])
                choose(w["router_b"], 6)
                tops = top[:, :].rearrange("p (t r) -> p t r", r=8)
                dve.tensor_tensor(wgt[:, 0:8], tops[:, :, 1], tops[:, :, 0], ALU.subtract).then_inc(made, 1)
                dve.wait_ge(prep_act, 1)
                chain.link(dve.tensor_scalar(wgt[:, 16:24], wgt[:, 8:16], 1.0, None, ALU.add))
                chain.link(dve.reciprocal(wgt[:, 24:32], wgt[:, 16:24]))
                chain.link(dve.tensor_tensor(wgt[:, 16:24], wgt[:, 8:16], wgt[:, 24:32], ALU.mult))
                for dst, wi in ((hot, 24), (hot2, 16)):
                    v = dst[:, :].rearrange("p (t e) -> p t e", e=8)
                    chain.mark(dve.tensor_tensor(v, v, wgt[:, wi:wi + 8].unsqueeze(2).broadcast_to([P, 8, 8]), ALU.mult))
                chain.join()
                dve.tensor_tensor(comb[:, :], hot[:, :], hot2[:, :], ALU.add).then_inc(prep_dve, 1)
                dve.wait_ge(prep_mm, 15)
                dve.tensor_copy(combT[0:8, :], S[0:8, 0:TOKENS]).then_inc(prep_dve, 1)
                hold(dve, G["la"]["summed_up"], TILES)
                for i in range(TILES):
                    dve.wait_ge(prep_mm, 16 + i)
                    o = (i % 2) * 512
                    dve.tensor_tensor(tile(x, i), AB[:, o:o + D], tile(x, i), ALU.add).then_inc(prep_dve, 1)
                dve.wait_ge(prep_dve, 8 + TILES)
                chain.restart()

                def gate(m, u, h):
                    c = u % 2
                    e = 2 * h + u // 2
                    for f in range(FT):
                        hold(dve, g["silued"], 8 * m + f + 1)
                        dve.scalar_tensor_tensor(out=hid[c][:, f, :], in0=S[:, (f % 2) * 1024 + 512:(f % 2 + 1) * 1024],
                                                 scalar=w["b2"][:, bass.ds(e * FT + f, 1)],
                                                 in1=gated[:, (f % 2) * CHUNK:(f % 2 + 1) * CHUNK],
                                                 op0=ALU.add, op1=ALU.mult).then_inc(g["gated"].sem, 1)

                def combine(m, u, e):
                    c = u % 2
                    for i in range(4):
                        tok = c * 4 + i
                        hold(dve, g["chunk_out"], 4 * m + i + 1)
                        hold(dve, g["out"], 4 * m - 4)
                        xt = x[:, tok * D:(tok + 1) * D]
                        dve.scalar_tensor_tensor(out=xt, in0=sums[i],
                                                 scalar=comb[:, bass.ds(e + tok * 8, 1)], in1=xt,
                                                 op0=ALU.mult, op1=ALU.add).then_inc(g["out"].sem, 1)

                def step(m, u, h):
                    if live(m, 0, CHUNKS * EXPERTS):
                        gate(m, u, h)
                    if live(m, 1, CHUNKS * EXPERTS):
                        combine(m - 1, (u - 1) % 4, 2 * h + u // 2 if u % 2 else 2 * h + u // 2 - 1)
                skewed(dve, CHUNKS * EXPERTS, 1, step, unroll=4)



def channels_first(w):
    return w.reshape(DC, P, -1).transpose(1, 0, 2)


def column(b):
    return b.reshape(DC, P).T


def rows(b):
    return np.broadcast_to(b, (P, b.shape[-1]))


def padded(a):
    out = np.zeros((P, a.shape[1]), a.dtype)
    out[:a.shape[0]] = a
    return out


def by_parity(wo):
    return wo.reshape(PAIRS, 2, DH, D).transpose(0, 2, 1, 3).reshape(P, 2, D)


def constants():
    p = np.arange(P)
    c = {"ident": np.eye(P)}
    par = (p[:, None] // DH) % 2 == np.arange(2)[None, :]
    c["par_x"] = par
    rot_par = ((p[:, None] - 2 * DH) // ROT) % 2 == np.arange(2)[None, :]
    c["par_s"] = np.where(p[:, None] < 2 * DH, par, rot_par)
    c["iota"] = np.tile(np.arange(8), (P, 1))
    c["causal"] = np.where(np.arange(SEQ)[None, :] > (p % SEQ)[:, None], -1.0e9, 0.0)
    same = p[:, None] // SEQ == p[None, :] // SEQ
    c["tri"] = same & (p[:, None] <= p[None, :])
    half = D // 2
    theta = (1.0 / np.float32(10000.0) ** (np.arange(half, dtype=np.float32) / np.float32(half))).astype(np.float32)
    ang = ((p % SEQ).astype(np.float32)[:, None] * theta[None, :]).astype(np.float32).astype(np.float64)
    c["cos"], c["sin"] = np.cos(ang), np.sin(ang)
    return c


def fourier():
    n, k = np.arange(D), np.arange(P)
    ang = 2 * np.pi * ((n[:, None] * k[None, :]) % D) / D
    alternate = 1.0 - 2.0 * (n % 2)
    fwd = np.concatenate([np.cos(ang), -np.sin(ang)], axis=1)
    fwd[:, P] = alternate
    inv = np.concatenate([np.cos(ang), -np.sin(ang)], axis=1) * 2.0 / D
    inv[:, 0] = 1.0 / D
    inv[:, P] = alternate / D
    j = np.arange(1, P + 1)
    turns = (j[:, None] * k[None, :]) % D
    sines = -2.0 * np.sin(2 * np.pi * turns / D)
    sines[turns % P == 0] = 0.0
    return {"fwd": channels_first(fwd), "inv": channels_first(inv), "sines": sines}


def pack(name, parts):
    fields = PACKS[name]
    return np.ascontiguousarray(np.concatenate(
        [np.asarray(parts[f]).reshape(P, fields[f]).astype(np.float32, copy=False) for f in fields], axis=1))


def lay_out(v):
    out = {}
    out["x"] = v["x"].reshape(TILES, P, D).transpose(1, 0, 2).reshape(P, TILES * D)
    out["ctx"] = v["ctx_1024"].transpose(0, 2, 1).reshape(SEQS, DC, P, KEYS).transpose(0, 2, 1, 3)\
        .reshape(SEQS, P, DC * KEYS)
    out["gp"] = v["fside_BxSxS2_0"]
    out["mask"] = v["mask_BxSxS2_ik1"]
    out["const"] = pack("const", constants())
    out["four"] = pack("four", fourier())

    def cross(q, k, vv, o, bq, bk, bv, bo):
        return {"wq": channels_first(q), "wk": channels_first(k), "wv": channels_first(vv), "wo": by_parity(o),
                "bq": column(bq), "bk": column(bk), "bv": rows(bv), "bo": rows(bo)}
    out["xa0"] = pack("xa0", cross(*(v["L0_xattn_w" + n] for n in ("q_k", "k_k", "v_k", "o_k", "q_b", "k_b", "v_b", "o_b"))))
    out["xa1"] = pack("xa1", cross(*(v["L1_xattn_" + n] for n in ("W_q", "W_k", "W_v", "W_o", "b_q", "b_k", "b_v", "b_o"))))
    a = {n: v["L0_attn_" + n] for n in ("Wq", "bq", "Wk", "bk", "Wv", "bv", "Wr", "br", "Wo", "bo")}
    w = np.concatenate([a["Wq"].reshape(D, PAIRS, 2 * DH), a["Wr"].reshape(D, PAIRS, 2 * ROT),
                        a["Wk"].reshape(D, PAIRS, 2 * DH)], axis=2)
    b = np.concatenate([a["bq"].reshape(PAIRS, 2 * DH), a["br"].reshape(PAIRS, 2 * ROT),
                        a["bk"].reshape(PAIRS, 2 * DH)], axis=1)
    out["sa"] = pack("sa", {"w": channels_first(w.reshape(D, -1)), "wv": channels_first(a["Wv"]),
                            "wo": by_parity(a["Wo"]), "b": b.T, "bv": rows(a["bv"]), "bo": rows(a["bo"])})
    out["ffn"] = pack("ffn", {
        "gate_w": channels_first(v["L0_ffn_gate_w"].T), "gate_b": padded(v["L0_ffn_gate_b"][:, None]),
        "we": channels_first(v["L0_ffn_expert_w"].transpose(2, 0, 1).reshape(D, -1)),
        "be": v["L0_ffn_expert_b"].reshape(EXPERTS, DC, P).transpose(2, 0, 1)})
    out["ssm"] = pack("ssm", {"bw": channels_first(v["L1_attn_B_w"]), "ct": channels_first(v["L1_attn_C_w"].T),
                              "a": v["L1_attn_a_params"][:, None], "d": rows(v["L1_attn_D"])})
    f = {n: v["L1_ffn_" + n] for n in ("norm1_w", "Wq", "Wk", "Wv", "Wo", "norm2_w", "router_w", "router_b",
                                       "W1", "b1", "W2", "b2", "W3", "b3")}
    groups = np.arange(HEADS) // (HEADS // 4)
    wk = f["Wk"].reshape(D, 4, DH)[:, groups].reshape(D, PAIRS, 2 * DH)
    wv = f["Wv"].reshape(D, 4, DH)[:, groups].reshape(D, D)
    w = np.concatenate([f["Wq"].reshape(D, PAIRS, 2 * DH), wk], axis=2)
    out["la"] = pack("la", {"w": channels_first(w.reshape(D, -1)), "wv": channels_first(wv), "wo": by_parity(f["Wo"]),
                            "norm1": rows(f["norm1_w"]), "norm2": rows(f["norm2_w"])})

    def feature_columns(b):
        return b.reshape(EXPERTS, FT, P).transpose(2, 0, 1)
    out["moe"] = pack("moe", {"router_w": channels_first(f["router_w"]), "router_b": padded(f["router_b"][:, None]),
                              "b1": feature_columns(f["b1"]), "b2": feature_columns(f["b2"]), "b3": padded(f["b3"])})
    both = np.concatenate([f["W1"], f["W2"]], axis=2)
    out["w12"] = both.reshape(EXPERTS, DC, P, 2 * FF).transpose(0, 2, 1, 3).reshape(EXPERTS, P, DC * 2 * FF)
    out["w3"] = f["W3"].reshape(EXPERTS, FT, P, D).transpose(0, 2, 1, 3).reshape(EXPERTS, P, FT * D)
    return {n: np.ascontiguousarray(a) for n, a in out.items()}


def program(nc, arrays, upto=9):
    t = {}
    for name, a in arrays.items():
        t[name] = nc.dram_tensor(f"in_{name}", a.shape, mybir.dt.from_np(a.dtype), kind="ExternalInput").ap()
    t["out"] = nc.dram_tensor("out_x", (P, TILES * D), F32, kind="ExternalOutput").ap()
    build(nc, t, upto)


def kernel(**inputs):
    import concourse.bacc as bacc
    from concourse.bass_utils import run_bass_kernel_spmd as run

    nc = bacc.Bacc("TRN2", target_bir_lowering=False, num_devices=1)
    arrays = lay_out({n: np.asarray(a) for n, a in inputs.items()})
    program(nc, arrays)
    r = run(nc, [{f"in_{n}": a for n, a in arrays.items()}], core_ids=[0])
    return np.ascontiguousarray(
        r.results[0]["out_x"].reshape(P, TILES, D).transpose(1, 0, 2).reshape(SEQS, SEQ, D))
```

```python
from contextlib import ExitStack

import numpy as np

import concourse.bass as bass
from concourse import mybir

F32 = mybir.dt.float32
F16 = mybir.dt.float16
I32 = mybir.dt.int32
U32 = mybir.dt.uint32
ALU = mybir.AluOpType
ACT = mybir.ActivationFunctionType
AX = mybir.AxisListType

P = 128
SEQS, SEQ, D = 16, 64, 256
KEYS = 256
TOKENS = SEQS * SEQ
TILES = TOKENS // P
DC = D // P
HEADS, DH = 16, 16
PAIRS = HEADS // 2
ROT = 32
EXPERTS = 8
FF = 1024
FT = FF // P
CHUNK = 512
CHUNKS = TOKENS // CHUNK
LN_EPS, RMS_EPS = 1e-5, 1e-6
CREDIT = 1
BIG = 3.0e38

SA_ROWS = 2 * DH + 2 * ROT
LA_ROWS = 2 * DH
SA_SCALE, LA_SCALE = (DH + ROT) ** -0.5, DH ** -0.5

PACKS = {
    "const": {"ident": P, "par_x": 2, "par_s": 2, "iota": 8, "causal": SEQ, "tri": P, "cos": P, "sin": P},
    "xa0": {"wq": 512, "wk": 512, "wv": 512, "wo": 512, "bq": 2, "bk": 2, "bv": D, "bo": D},
    "sa": {"w": 2048, "wv": 512, "wo": 512, "b": 8, "bv": D, "bo": D},
    "ffn": {"gate_w": 16, "gate_b": 1, "we": 4096, "be": 16},
    "xa1": {"wq": 512, "wk": 512, "wv": 512, "wo": 512, "bq": 2, "bk": 2, "bv": D, "bo": D},
    "ssm": {"bw": 512, "ct": 512, "a": 1, "d": D},
    "four": {"fwd": 512, "inv": 512, "sines": P},
    "la": {"w": 1024, "wv": 512, "wo": 512, "norm1": D, "norm2": D},
    "moe": {"router_w": 16, "router_b": 1, "b1": 64, "b2": 64, "b3": D},
}


EARLY = ("xa0", "sa", "ffn")


class Signal:

    def __init__(self, sem, base):
        self.sem, self.base = sem, base


def hold(eng, signal, n):
    if isinstance(n, int) and n <= 0:
        return
    eng.wait_ge(signal.sem, n + (signal.base + CREDIT))


def at_most(n, top):
    return min(n, top) if isinstance(n, int) else n


def skewed(eng, n, lag, step, unroll=2):
    peeled = max(-(-lag // unroll), 1)
    for k in range(peeled * unroll):
        step(k, k % unroll, k // unroll)
    with eng.Fori(peeled, n // unroll) as h:
        for s in range(unroll):
            step(unroll * h + s, s, h)
    for k in range(n, n + lag):
        step(k, k % unroll, k // unroll)


def live(k, lag, n):
    return 0 <= k - lag < n if isinstance(k, int) else True


class Chain:

    def __init__(self, eng, sem):
        self.eng, self.sem, self.n = eng, sem, 0

    def link(self, ins):
        ins.then_inc(self.sem, 1)
        self.n += 1
        self.eng.wait_ge(self.sem, self.n)

    def mark(self, ins):
        ins.then_inc(self.sem, 1)
        self.n += 1

    def join(self):
        self.eng.wait_ge(self.sem, self.n)

    def restart(self):
        if self.n:
            self.join()
            self.eng.sem_clear(self.sem)
            self.n = 0


def build(nc, t):
    ctx = ExitStack()
    with ctx:
        def sb(name, cols, dt=F32):
            return ctx.enter_context(nc.sbuf_tensor(name, [P, cols], dt))

        def sem(name):
            return ctx.enter_context(nc.semaphore(name))

        W = {}
        early = sb("early", sum(sum(PACKS[pack].values()) for pack in EARLY))
        taken = 0
        for pack, fields in PACKS.items():
            cols = sum(fields.values())
            if pack in EARLY:
                whole = early[:, taken:taken + cols]
                taken += cols
            else:
                whole = sb("pack_" + pack, cols)[:, :]
            W[pack] = {"whole": whole}
            at = 0
            for name, cols in fields.items():
                W[pack][name] = whole[:, at:at + cols]
                at += cols

        def kc(ap, n):
            return ap.rearrange("p (c n) -> p c n", n=n)

        ident = W["const"]["ident"]
        x = sb("x", TILES * D)
        xn_all = sb("xn_all", TILES * D)
        xt_all = sb("xt_all", DC * TOKENS)
        XT = xt_all[:, :].rearrange("p (c n) -> p c n", c=DC)
        xn = sb("xn", D)
        stat6 = sb("stat6", 6)
        mv = sb("mv", 2)
        var = sb("var", 1)
        rstd = sb("rstd", 1)
        rstd2 = sb("rstd2", 2)
        half = sb("half", 3)
        junk = sb("junk", D)
        probs = sb("probs", 2 * PAIRS * KEYS)
        pt = sb("pt", 2 * PAIRS * 2 * P)
        ctx_t = sb("ctx_t", 2 * DC * KEYS)
        gp = sb("gp", 2 * KEYS)
        mask_i = sb("mask_i", 2 * KEYS, I32)
        neg = sb("neg", 2 * KEYS)
        kbuf = sb("kbuf", 4 * 1024, F16)
        vbuf = sb("vbuf", 4 * 512, F16)
        qbuf = sb("qbuf", 4 * 2048, F16)

        def k_part(part, s):
            return kbuf[:, (2 * part + s) * 1024:(2 * part + s + 1) * 1024]

        def v_part(part, s):
            return vbuf[:, (2 * part + s) * 512:(2 * part + s + 1) * 512]

        def q_part(part, s):
            return qbuf[:, (2 * part + s) * 2048:(2 * part + s + 1) * 2048]

        def p_part(part, s):
            return pt[:, :].bitcast(F16)[:, (2 * part + s) * 2048:(2 * part + s + 1) * 2048]

        mx = sb("mx", 2 * HEADS)
        ssum = sb("ssum", 2 * HEADS)
        rsum = sb("rsum", 2 * HEADS)
        obuf = sb("obuf", 2 * 2 * P)
        ot = sb("ot", 2 * P)
        xs = sb("xs", 2 * DC * P)
        scratch = sb("scratch", 1024)
        acc = scratch[:, 0:2 * DC * P]
        relu = scratch[:, 512:1024]
        qsplit = sb("qsplit", 512, F16)
        counts = sb("counts", EXPERTS)
        bec = sb("bec", 2 * EXPERTS)
        top = sb("top", TILES * 8)
        topi = sb("topi", TILES * 8, U32)
        topf = sb("topf", TILES * 8)
        hot = sb("hot", TILES * EXPERTS)
        hot2 = sb("hot2", TILES * EXPERTS)
        logit = sb("logit", TILES * EXPERTS)
        gateT = sb("gateT", TOKENS)
        ones = sb("ones", P)
        two = sb("two", 1)
        wb = sb("wb", DC * D)
        cg = sb("cg", DC * D)
        lam = sb("lam", 8)
        omega, sq, den, lr, li, sq2, lr2, li2 = (lam[:, i:i + 1] for i in range(8))
        tabR = sb("tabR", 2 * SEQ)
        tabI = sb("tabI", 2 * SEQ)
        tabt = sb("tabt", SEQ)
        rowR = sb("rowR", P)
        rowI = sb("rowI", P)
        rot = sb("rot", 2 * D)
        rot2 = sb("rot2", 2 * D)
        vsum = rot
        comb = sb("comb", TILES * EXPERTS)
        combT = gateT
        wgt = sb("wgt", TILES * 4)
        wide = DC * 2 * FF
        w12_in, w3_in = qbuf[:, :].bitcast(F32), kbuf[:, :].bitcast(F32)
        w12 = [early[:, i * wide:(i + 1) * wide].bitcast(F16) for i in range(2)]
        w3 = [early[:, 2 * wide:2 * wide + FT * D].bitcast(F16), sb("w3_1", 2 * FT * D, F16)[:, :]]

        def part_of(both, part):
            n = both.shape[1] // 2
            return both[:, part * n:(part + 1) * n]

        xt_split = xn_all[:, :].bitcast(F16)
        gated = ctx_t
        hid = [probs[:, :].bitcast(F16), pt[:, :].bitcast(F16)]
        product = scratch[:, 0:CHUNK]

        ps = ctx.enter_context(nc.psum_tensor("ps", [P, 8 * 512], F32))
        S = ps[:, 0:2048]
        AB = ps[:, 2048:3072]
        M = ps[:, 3072:3584]
        C = ps[:, 3584:4096]
        sums = [ps[:, o:o + D] for o in (2048, 2560, 3072, 3584)]

        shared = {}

        def signals(counts):
            out = {}
            for name, count in counts.items():
                if name not in shared:
                    shared[name] = [sem(name), 0]
                out[name] = Signal(*shared[name])
                shared[name][1] += count
            return out

        def each(count, names):
            return {name: count for name in names.split()}

        rows_turned = each(TILES, "stats rstd normed turned xt")
        tail = {**rows_turned, **each(TILES, "o_turned o_copied projected resid")}
        cross_counts = {
            **each(SEQS, "k_projected k_hi k_copied v_projected v_summed v_hi v_lo scored pv_done o_normed"),
            **each(TILES, "q_projected q_taken q_copied biased"),
            **each(4 * SEQS, "weighted p_turned pt_hi pt_lo"), **tail}
        inner_counts = {
            **each(TILES, "x_copied qk_projected qk_summed qk_hi qk_copied v_projected v_summed v_hi v_lo scored "
                          "maxima exped p_turned pt_hi pt_lo pv_done o_normed"), **tail}
        G = {
            "ln": signals(rows_turned),
            "xa0": signals({**cross_counts, **each(8 * SEQS, "masked powered"), "negated": SEQS}),
            "sa": signals({**inner_counts, "biased": TILES}),
            "ffn": signals({**rows_turned, **each(TILES, "projected resid"), "expert": 16 * TILES,
                            "relued": 16 * TILES, "added": 14 * TILES}),
            "xa1": signals({**cross_counts, "maxima": 2 * SEQS, "kept": TILES}),
            "ssm": signals(each(TILES, "x_copied v_projected rotated summed modulated projected biased resid stats "
                                       "rstd normed")),
            "rope": signals(each(TILES, "squared rstd roped turned xt")),
            "la": signals({**inner_counts, **each(TILES, "squared summed_up")}),
            "moe": signals({"hidden": 0, "silued": 0, "gated": 0, "gated_hi": 0, "gated_lo": 0, "chunk_out": 0,
                            "out": 0, "w12_hi": 0, "w3_hi": 0, "w_split": 0}),
        }
        loads = {"first": ["x", "const"], "xa0": ["xa0"], "sa": ["sa"], "ffn": ["ffn"], "ssm": ["four", "ssm"],
                 "late": ["xa1", "la", "moe"]}
        load_sems = {name: sem(f"loaded_{name}") for name in loads}
        loaded = {a: (load_sems[name], 16 * len(of)) for name, of in loads.items() for a in of}
        ctx_loaded = [sem(f"ctx_loaded{s}") for s in range(2)]
        mask_loaded = [sem(f"mask_loaded{s}") for s in range(2)]

        def ctx_count(st, h):
            return 16 * (h + 1) + (16 * (SEQS // 2) if st == "xa1" else 0)

        w_loaded = [sem(f"w_loaded{s}") for s in range(2)]
        dve_chain, pool_chain = sem("dve_chain"), sem("pool_chain")
        dve_passed, pool_passed, act_passed, sp_passed = (sem(e + "_passed") for e in ("dve", "pool", "act", "sp"))
        made = sem("made")
        prep_mm, prep_dve, prep_act = sem("prep_mm"), sem("prep_dve"), sem("prep_act")
        tables, logits_taken = sem("tables"), sem("logits_taken")
        final_ready = G["moe"]["out"]
        stored = sem("stored")

        block = ctx.enter_context(nc.Block())

        def tile(ap, h):
            return ap[:, bass.ts(h, D)]

        PREV = {"xa0": "ln", "sa": "xa0", "ffn": "sa", "xa1": "ffn", "ssm": "xa1", "rope": "ssm", "la": "rope"}

        @block.sync
        def _(sp):
            for counter, _ in shared.values():
                sp.sem_inc(counter, CREDIT)
            sp.dma_start(x[:, :], t["x"]).then_inc(loaded["x"][0], 16)
            for name in ("const", "xa0", "sa", "ffn", "four", "ssm"):
                sp.dma_start(W[name]["whole"], t[name]).then_inc(loaded[name][0], 16)

            def load_context(st, b, s):
                hold(sp, G[st]["v_projected"], b - 1)
                sp.sem_inc(sp_passed, 1)
                c = ctx_t[:, s * DC * KEYS:(s + 1) * DC * KEYS]
                src = t["ctx"][bass.ds(b, 1), :, :].rearrange("b p n -> (b p) n")
                sp.dma_start(c, src).then_inc(ctx_loaded[s], 16)

            def load_mask(b, s):
                hold(sp, G["xa0"]["weighted"], 4 * (b - 1))
                sp.sem_inc(sp_passed, 1)
                hold(sp, G["xa0"]["negated"], b - 1)
                sp.sem_inc(sp_passed, 1)
                gsrc = t["gp"][bass.ds(b, 1), :, :].rearrange("b p n -> (b p) n")
                msrc = t["mask"][bass.ds(b, 1), :, :].rearrange("b p n -> (b p) n")
                for r in range(2):
                    q = slice(r * SEQ, (r + 1) * SEQ)
                    sp.dma_start(mask_i[q, s * KEYS:(s + 1) * KEYS], msrc).then_inc(mask_loaded[s], 16)
                    sp.dma_start(gp[q, s * KEYS:(s + 1) * KEYS], gsrc).then_inc(mask_loaded[s], 16)

            def load_step(k, s, h):
                if live(k, 0, SEQS):
                    load_context("xa0", k, s)
                if live(k, 1, SEQS):
                    load_mask(k - 1, 1 - s)
            skewed(sp, SEQS, 1, load_step)
            for name in ("xa1", "la", "moe"):
                sp.dma_start(W[name]["whole"], t[name]).then_inc(loaded[name][0], 16)
            hold(sp, G["xa0"]["v_projected"], SEQS)
            skewed(sp, SEQS, 0, lambda k, s, h: load_context("xa1", k, s))
            def load_expert(e, s, h):
                hold(sp, G["moe"]["w_split"], e)
                a = t["w12"][bass.ds(e, 1), :, :].rearrange("b p n -> (b p) n")
                b = t["w3"][bass.ds(e, 1), :, :].rearrange("b p n -> (b p) n")
                sp.dma_start(w12_in, a).then_inc(w_loaded[s], 16)
                sp.dma_start(w3_in, b).then_inc(w_loaded[s], 16)
            hold(sp, G["la"]["scored"], TILES)
            skewed(sp, EXPERTS, 0, load_expert)
            hold(sp, final_ready, 4 * CHUNKS * EXPERTS)
            sp.dma_start(t["out"], x[:, :]).then_inc(stored, 16)
            sp.wait_ge(stored, 16)

        @block.tensor
        def _(pe):
            pe.wait_ge(*loaded["const"])

            def turn_rows(g, h):
                hold(pe, g["normed"], h + 1)
                for c in range(DC):
                    last = pe.transpose(C[:, c * P:(c + 1) * P], xn[:, c * P:(c + 1) * P], ident)
                last.then_inc(g["turned"].sem, 1)

            def turn_outputs(g, h, per_tile, base):
                hold(pe, g["o_normed"], per_tile * (h + 1))
                hold(pe, g["xt"], h)
                for b in range(2):
                    last = pe.transpose(C[:, b * P:(b + 1) * P], obuf[:, base + b * P:base + (b + 1) * P], ident)
                last.then_inc(g["o_turned"].sem, 1)

            def split_product(dst, a, b, first=True, final=True):
                pe.matmul(dst, a[0], b[0], start=first, stop=False)
                pe.matmul(dst, a[0], b[1], start=False, stop=False)
                return pe.matmul(dst, a[1], b[0], start=False, stop=final)

            def out_project(g, h, wo, dst):
                hold(pe, g["o_copied"], h + 1)
                hold(pe, g["resid"], h)
                for par in range(2):
                    last = pe.matmul(dst, ot[:, par * P:(par + 1) * P], kc(wo, D)[:, par, :],
                                     start=par == 0, stop=par == 1)
                last.then_inc(g["projected"].sem, 1)

            def ln_step(k, s, h):
                hold(pe, G["ln"]["xt"], k)
                turn_rows(G["ln"], k)
            skewed(pe, TILES, 0, ln_step)

            def cross(st):
                g, w = G[st], W[st]
                wq, wk, wv = kc(w["wq"], D), kc(w["wk"], D), kc(w["wv"], D)
                prev = G[PREV[st]]
                pe.wait_ge(*loaded[st])

                def context(s):
                    return ctx_t[:, s * DC * KEYS:(s + 1) * DC * KEYS].rearrange("p (c n) -> p c n", c=DC)

                def project_keys(b, s, h):
                    c = context(s)
                    pe.wait_ge(ctx_loaded[s], ctx_count(st, h))
                    if isinstance(b, int) and b <= 2:
                        hold(pe, g["k_copied"], b)
                    else:
                        hold(pe, g["pt_lo"], 4 * b - 9)
                    for hf in range(2):
                        for k in range(DC):
                            last = pe.matmul(AB[:, hf * KEYS:(hf + 1) * KEYS], wk[:, k, hf * P:(hf + 1) * P],
                                             c[:, k, :], start=k == 0, stop=k == DC - 1)
                    last.then_inc(g["k_projected"].sem, 1)

                def project_values(b, s):
                    c = context(s)
                    if isinstance(b, int) and b <= 1:
                        hold(pe, g["v_summed"], b)
                    else:
                        hold(pe, g["pt_lo"], 4 * b - 4)
                    for kt in range(2):
                        for k in range(DC):
                            last = pe.matmul(AB[:, 512 + kt * D:512 + (kt + 1) * D], c[:, k, kt * P:(kt + 1) * P],
                                             wv[:, k, :], start=k == 0, stop=k == DC - 1)
                    last.then_inc(g["v_projected"].sem, 1)

                def project_queries(h):
                    if isinstance(h, int) and h == 0:
                        hold(pe, prev["xt"], TILES)
                    hold(pe, g["xt"], h - 2)
                    for hf in range(2):
                        for c in range(DC):
                            last = pe.matmul(C[:, 256 + hf * P:256 + (hf + 1) * P], wq[:, c, hf * P:(hf + 1) * P],
                                             XT[:, c, bass.ts(h, P)], start=c == 0, stop=c == DC - 1)
                    last.then_inc(g["q_projected"].sem, 1)

                def turn_probs(b, s, chunks):
                    pr = probs[:, s * 2048:(s + 1) * 2048].rearrange("p (n k) -> p n k", n=PAIRS)
                    for c in chunks:
                        hold(pe, g["weighted"], 4 * b + c + 1)
                        if c == 0:
                            hold(pe, g["k_copied"], at_most(b + 3, SEQS))
                        elif c == 1:
                            hold(pe, g["v_summed"], at_most(b + 2, SEQS))
                        else:
                            hold(pe, g["pt_lo"], 4 * b + c - 1)
                        for n in range(2):
                            for kt in range(2):
                                o = (c % 2) * 512 + (n * 2 + kt) * P
                                last = pe.transpose(AB[:, o:o + P], pr[:, 2 * c + n, kt * P:(kt + 1) * P], ident)
                        last.then_inc(g["p_turned"].sem, 1)

                def score(b, s, h, hf):
                    hold(pe, g["q_copied"], h + 1)
                    hold(pe, g["k_copied"], b + 1)
                    if st == "xa0":
                        hold(pe, g["masked"], 8 * b)
                    else:
                        hold(pe, g["weighted"], 4 * b)
                    q = [q_part(part, s)[:, hf * P:(hf + 1) * P] for part in range(2)]
                    kk = [k_part(part, s)[:, hf * KEYS:(hf + 1) * KEYS] for part in range(2)]
                    for j in range(4):
                        r = slice(32 * j, 32 * j + 32)
                        o = j * 512 + hf * KEYS
                        last = split_product(S[:, o:o + KEYS], [a[r, :] for a in q], [a[r, :] for a in kk])
                    if hf == 1:
                        last.then_inc(g["scored"].sem, 1)

                def mix_values(b, s):
                    turned = [p_part(part, s).rearrange("p (n k q) -> p n k q", n=PAIRS, k=2) for part in range(2)]
                    v = [v_part(part, s).rearrange("p (k n) -> p k n", k=2) for part in range(2)]
                    hold(pe, g["pt_lo"], 4 * b + 4)
                    hold(pe, g["v_lo"], b + 1)
                    hold(pe, g["o_normed"], b)
                    for n in range(PAIRS):
                        for kt in range(2):
                            last = split_product(M[:, n * 32:(n + 1) * 32], [a[:, n, kt, :] for a in turned],
                                                 [a[:, kt, n * 32:(n + 1) * 32] for a in v], kt == 0, kt == 1)
                    last.then_inc(g["pv_done"].sem, 1)

                def step(k, s, h):
                    if live(k, 0, SEQS):
                        if s == 0:
                            project_queries(h)
                        project_keys(k, s, h)
                    if live(k, 3, SEQS):
                        mix_values(k - 3, 1 - s)
                    if live(k, 1, SEQS):
                        project_values(k - 1, 1 - s)
                    if live(k, 3, SEQS) and s == 0:
                        hold(pe, g["q_taken"], at_most(h + 1, TILES))
                        turn_outputs(g, h - 2, 2, 0)
                    for hf in range(2):
                        if live(k, 2, SEQS):
                            turn_probs(k - 2, s, (2 * hf, 2 * hf + 1))
                        if hf == 1 and live(k, 3, SEQS) and s == 0:
                            out_project(g, h - 2, w["wo"], C[:, 256:512])
                        if hf == 0 and live(k, 4, SEQS) and s == 1:
                            turn_rows(g, h - 2)
                        if live(k, 1, SEQS):
                            score(k - 1, 1 - s, h - 1 if s == 0 else h, hf)
                skewed(pe, SEQS, 4, step)

            def inner(st, rows):
                g, w = G[st], W[st]
                width = w["w"].shape[1] // (DC * PAIRS)
                wqk = w["w"].rearrange("p (c n m) -> p c n m", c=DC, n=PAIRS)
                wv = kc(w["wv"], D)
                pe.wait_ge(*loaded[st])

                def project(i, s):
                    xt = xs[:, s * D:(s + 1) * D].rearrange("p (c n) -> p c n", c=DC)
                    hold(pe, g["x_copied"], i + 1)
                    hold(pe, g["qk_summed"], i)
                    for n in range(PAIRS):
                        for k in range(DC):
                            last = pe.matmul(S[0:width, 1024 + n * P:1024 + (n + 1) * P], wqk[:, k, n, :], xt[:, k, :],
                                             start=k == 0, stop=k == DC - 1)
                    last.then_inc(g["qk_projected"].sem, 1)

                def project_values(i, s):
                    xt = xs[:, s * D:(s + 1) * D].rearrange("p (c n) -> p c n", c=DC)
                    hold(pe, g["pt_lo"], i - 1)
                    if isinstance(i, int) and i == 1:
                        hold(pe, g["v_summed"], 1)
                    for k in range(DC):
                        last = pe.matmul(AB[:, 0:D], xt[:, k, :], wv[:, k, :], start=k == 0, stop=k == DC - 1)
                    last.then_inc(g["v_projected"].sem, 1)

                def turn_probs(i, s):
                    pr = probs[:, s * 2048:s * 2048 + 1024]
                    hold(pe, g["exped"], i + 1)
                    hold(pe, g["v_summed"], at_most(i + 2, TILES))
                    hold(pe, g["pt_lo"], i)
                    for n in range(PAIRS):
                        last = pe.transpose(AB[:, n * P:(n + 1) * P], pr[:, n * P:(n + 1) * P], ident)
                    last.then_inc(g["p_turned"].sem, 1)

                def score(i, s):
                    hold(pe, g["qk_copied"], i + 1)
                    hold(pe, g["exped"], i)
                    for n in range(PAIRS):
                        for b in range(2):
                            o = n * P + b * SEQ
                            q = [q_part(part, s)[0:rows, (n * 2 + b) * P:(n * 2 + b + 1) * P] for part in range(2)]
                            kk = [k_part(part, s)[0:rows, o:o + SEQ] for part in range(2)]
                            last = split_product(S[:, o:o + SEQ], q, kk)
                    last.then_inc(g["scored"].sem, 1)

                def mix_values(i, s):
                    hold(pe, g["pt_lo"], i + 1)
                    hold(pe, g["v_lo"], i + 1)
                    hold(pe, g["o_normed"], i)
                    hold(pe, g["resid"], i)
                    for b in range(2):
                        dst = M if b == 0 else C[:, 256:512]
                        r = slice(b * SEQ, (b + 1) * SEQ)
                        for n in range(PAIRS):
                            turned = [p_part(part, s)[r, n * P:(n + 1) * P] for part in range(2)]
                            v = [v_part(part, s)[r, n * 32:(n + 1) * 32] for part in range(2)]
                            last = split_product(dst[:, n * 32:(n + 1) * 32], turned, v)
                    last.then_inc(g["pv_done"].sem, 1)

                def step(k, s, h):
                    if live(k, 2, TILES):
                        project_values(k - 2, s)
                        score(k - 2, s)
                    if live(k, 3, TILES):
                        turn_probs(k - 3, 1 - s)
                    if live(k, 0, TILES):
                        project(k, s)
                    if live(k, 5, TILES):
                        turn_rows(g, k - 5)
                    if live(k, 4, TILES):
                        turn_outputs(g, k - 4, 1, s * D)
                        out_project(g, k - 4, w["wo"], M[:, 256:512])
                    if live(k, 3, TILES):
                        mix_values(k - 3, 1 - s)
                skewed(pe, TILES, 5, step)

            def choose(w, base):
                for c in range(CHUNKS):
                    for k in range(DC):
                        last = pe.matmul(S[0:EXPERTS, c * 512:(c + 1) * 512], kc(w, 8)[:, k, :],
                                         XT[:, k, c * 512:(c + 1) * 512], start=k == 0, stop=k == DC - 1)
                last.then_inc(prep_mm, 1)
                pe.wait_ge(prep_dve, base)
                for i in range(TILES):
                    last = pe.transpose(S[:, 1024 + i * 8:1024 + (i + 1) * 8], gateT[0:8, i * P:(i + 1) * P],
                                        ident[0:8, 0:8])
                last.then_inc(prep_mm, 1)

            cross("xa0")
            inner("sa", SA_ROWS)
            g, w = G["ffn"], W["ffn"]
            pe.wait_ge(*loaded["ffn"])
            hold(pe, G["sa"]["xt"], TILES)
            choose(w["gate_w"], 1)
            pe.wait_ge(prep_dve, 2)
            pe.matmul(S[:, 1280:1288], ones[:, :], hot2[:, 0:8], start=True, stop=True)
            pe.wait_ge(*loaded["ssm"])
            pe.wait_ge(*loaded["four"])
            pe.matmul(S[:, 1288:1289], W["four"]["sines"], W["ssm"]["a"], start=True, stop=True)\
                .then_inc(prep_mm, 1)
            bw, ct = kc(W["ssm"]["bw"], D), kc(W["ssm"]["ct"], D)
            fwd, inv = kc(W["four"]["fwd"], D), kc(W["four"]["inv"], D)
            hold(pe, G["sa"]["pt_lo"], TILES)
            for at, a, b in ((0, bw, fwd), (512, inv, ct)):
                for m in range(DC):
                    for k in range(DC):
                        last = pe.matmul(AB[:, at + m * D:at + (m + 1) * D], a[:, k, m * P:(m + 1) * P], b[:, k, :],
                                         start=k == 0, stop=k == DC - 1)
            last.then_inc(prep_mm, 1)
            we = w["we"].rearrange("p (c e h) -> p c e h", c=DC, e=EXPERTS)

            def experts(i, s):
                for n in range(2 * EXPERTS):
                    e, hh = n // 2, n % 2
                    hold(pe, g["relued"], 16 * i + n - 3)
                    o = (n % 4) * 512
                    for k in range(DC):
                        last = pe.matmul(S[:, o:o + P], we[:, k, e, hh * P:(hh + 1) * P],
                                         XT[:, k, bass.ts(i, P)], start=k == 0, stop=k == DC - 1)
                    last.then_inc(g["expert"].sem, 1)

            def back(i, s):
                hold(pe, g["added"], 14 * (i + 1))
                hold(pe, g["relued"], 16 * (i + 1))
                hold(pe, g["resid"], i)
                for hh in range(DC):
                    last = pe.transpose(M[:, 256 + hh * P:256 + (hh + 1) * P],
                                        acc[:, s * D + hh * P:s * D + (hh + 1) * P], ident)
                last.then_inc(g["projected"].sem, 1)

            pe.wait_ge(prep_dve, 3)

            def step(k, s, h):
                if live(k, 1, TILES):
                    back(k - 1, 1 - s)
                if live(k, 0, TILES):
                    experts(k, s)
                if live(k, 1, TILES):
                    hold(pe, g["xt"], k - 1)
                    turn_rows(g, k - 1)
            skewed(pe, TILES, 1, step)
            cross("xa1")
            g, w = G["ssm"], W["ssm"]
            pe.wait_ge(tables, 1)
            hold(pe, G["xa1"]["weighted"], 4 * SEQS)
            pe.transpose(S[:, 1024:1024 + P], tabR[:, :], ident)
            pe.transpose(S[:, 1024 + P:1024 + 2 * P], tabI[:, :], ident).then_inc(prep_mm, 1)
            pe.wait_ge(prep_dve, 5)

            def project(i, s):
                hold(pe, g["x_copied"], i + 1)
                hold(pe, g["rotated"], i)
                for k in range(DC):
                    last = pe.matmul(AB[:, 0:D], xs[:, s * D + k * P:s * D + (k + 1) * P], kc(wb[:, :], D)[:, k, :],
                                     start=k == 0, stop=k == DC - 1)
                last.then_inc(g["v_projected"].sem, 1)

            def sum_over_time(i, s):
                hold(pe, g["rotated"], i + 1)
                hold(pe, g["modulated"], i)
                for c in range(DC):
                    last = pe.matmul(S[:, c * P:(c + 1) * P], rot[:, s * D + c * P:s * D + (c + 1) * P],
                                     W["const"]["tri"], start=True, stop=True)
                last.then_inc(g["summed"].sem, 1)

            def out(i, s):
                hold(pe, g["modulated"], i + 1)
                hold(pe, g["resid"], i)
                for c in range(DC):
                    last = pe.matmul(M[:, 256:512], rot2[:, s * D + c * P:s * D + (c + 1) * P],
                                     kc(cg[:, :], D)[:, c, :], start=c == 0, stop=c == DC - 1)
                last.then_inc(g["projected"].sem, 1)

            def step(k, s, h):
                if live(k, 1, TILES):
                    sum_over_time(k - 1, 1 - s)
                if live(k, 0, TILES):
                    project(k, s)
                if live(k, 2, TILES):
                    out(k - 2, s)
            skewed(pe, TILES, 2, step)
            g = G["rope"]

            def step(k, s, h):
                hold(pe, g["roped"], k + 1)
                hold(pe, g["xt"], k)
                for c in range(DC):
                    last = pe.transpose(C[:, c * P:(c + 1) * P], rot[:, c * P:(c + 1) * P], ident)
                last.then_inc(g["turned"].sem, 1)
            skewed(pe, TILES, 0, step)
            inner("la", LA_ROWS)
            g, w = G["moe"], W["moe"]
            pe.wait_ge(*loaded["moe"])
            hold(pe, G["la"]["xt"], TILES)
            choose(w["router_w"], 7)
            pe.wait_ge(logits_taken, 2)

            def turn_combination():
                pe.wait_ge(prep_dve, 8)
                for i in range(TILES):
                    pe.transpose(AB[0:8, i * P:(i + 1) * P], comb[:, i * 8:(i + 1) * 8], ident).then_inc(prep_mm, 1)

            def add_biases():
                pe.wait_ge(prep_dve, 9)
                for i in range(TILES):
                    if i >= 2:
                        pe.wait_ge(prep_dve, 9 + i - 1)
                    pe.matmul(sums[2 + i % 2], combT[0:8, i * P:(i + 1) * P], w["b3"][0:8, :],
                              start=True, stop=True).then_inc(prep_mm, 1)
                pe.wait_ge(prep_dve, 9 + TILES)

            def hidden(m, u, h):
                c, s = u % 2, (u // 2) % 2
                w1 = [part_of(w12[s], part).rearrange("p (c n) -> p c n", c=DC) for part in range(2)]
                xt = [part_of(xt_split, part).rearrange("p (c n) -> p c n", c=DC) for part in range(2)]
                if c == 0:
                    hold(pe, g["w_split"], 2 * h + s + 1)
                for f in range(FT):
                    hold(pe, g["gated"], 8 * m + f - 1)
                    for half_ in range(2):
                        o = (f % 2) * 1024 + half_ * 512
                        for k in range(DC):
                            r = slice(half_ * FF + f * P, half_ * FF + (f + 1) * P)
                            last = split_product(S[:, o:o + CHUNK], [a[:, k, r] for a in w1],
                                                 [a[:, k, c * CHUNK:(c + 1) * CHUNK] for a in xt],
                                                 k == 0, k == DC - 1)
                    last.then_inc(g["hidden"].sem, 1)

            def down(m, u):
                s = (u // 2) % 2
                wd = [part_of(w3[s], part).rearrange("p (f n) -> p f n", f=FT) for part in range(2)]
                units = [part_of(hid[u % 2], part).rearrange("p (f n) -> p f n", f=FT) for part in range(2)]
                hold(pe, g["gated_lo"], 8 * (m + 1))
                for i in range(4):
                    hold(pe, g["out"], 4 * m + i - 3)
                    for f in range(FT):
                        last = split_product(sums[i], [a[:, f, i * P:(i + 1) * P] for a in units],
                                             [a[:, f, :] for a in wd], f == 0, f == FT - 1)
                    last.then_inc(g["chunk_out"].sem, 1)

            def step(k, u, h):
                first = isinstance(k, int) and k == 1
                if first:
                    turn_combination()
                if live(k, 0, CHUNKS * EXPERTS):
                    hidden(k, u, h)
                if first:
                    add_biases()
                if live(k, 1, CHUNKS * EXPERTS):
                    down(k - 1, (u - 1) % 4)
            skewed(pe, CHUNKS * EXPERTS, 1, step, unroll=4)

        @block.scalar
        def _(act):
            def copy_outputs(g, h):
                hold(act, g["o_turned"], h + 1)
                act.activation(ot[:, :].rearrange("p (a b q) -> p b a q", a=2, b=2),
                               C[:, 0:256].rearrange("p (b a q) -> p b a q", b=2, a=2), ACT.Copy)\
                   .then_inc(g["o_copied"].sem, 1)

            def copy_turned(g, h):
                hold(act, g["turned"], h + 1)
                act.activation(XT[:, :, bass.ts(h, P)], C[:, 0:256].rearrange("p (c n) -> p c n", c=DC), ACT.Copy)\
                   .then_inc(g["xt"].sem, 1)

            skewed(act, TILES, 0, lambda k, s, h: copy_turned(G["ln"], k))

            def cross(st):
                g, w = G[st], W[st]
                act.wait_ge(*loaded[st])

                def copy_keys(b, s):
                    hold(act, g["k_projected"], b + 1)
                    for hf in range(2):
                        last = act.activation(k_part(0, s)[:, hf * KEYS:(hf + 1) * KEYS],
                                              AB[:, hf * KEYS:(hf + 1) * KEYS], ACT.Identity,
                                              bias=w["bk"][:, hf:hf + 1])
                    last.then_inc(g["k_hi"].sem, 1)

                def copy_values(b, s):
                    hold(act, g["v_summed"], b + 1)
                    act.activation(v_part(0, s), vsum[:, :], ACT.Copy).then_inc(g["v_hi"].sem, 1)

                def copy_probs(b, s, chunks):
                    for c in chunks:
                        hold(act, g["p_turned"], 4 * b + c + 1)
                        act.activation(p_part(0, s)[:, c * 512:(c + 1) * 512],
                                       AB[:, (c % 2) * 512:(c % 2 + 1) * 512], ACT.Copy).then_inc(g["pt_hi"].sem, 1)

                def exps(b, s):
                    for n in range(PAIRS):
                        hold(act, g["masked"], 8 * b + n + 1)
                        p = probs[:, s * 2048 + n * KEYS:s * 2048 + (n + 1) * KEYS]
                        act.activation(p, p, ACT.Exp, bias=mx[:, s * HEADS + n:s * HEADS + n + 1], scale=-1.0,
                                       accum_out=ssum[:, s * HEADS + n:s * HEADS + n + 1])\
                           .then_inc(g["powered"].sem, 1)

                def plain_exps(b, s):
                    hold(act, g["maxima"], 2 * b + 2)
                    for n in range(PAIRS):
                        o = (n % 4) * 512 + (n // 4) * KEYS
                        last = act.activation(probs[:, s * 2048 + n * KEYS:s * 2048 + (n + 1) * KEYS], S[:, o:o + KEYS],
                                              ACT.Exp, bias=mx[:, s * HEADS + n:s * HEADS + n + 1],
                                              accum_out=ssum[:, s * HEADS + n:s * HEADS + n + 1])
                        if n % 2 == 1:
                            last.then_inc(g["weighted"].sem, 1)

                def step(k, s, h):
                    if live(k, 0, SEQS):
                        copy_keys(k, s)
                    if live(k, 2, SEQS) and st == "xa1":
                        plain_exps(k - 2, s)
                    if live(k, 1, SEQS):
                        copy_values(k - 1, 1 - s)
                    if live(k, 3, SEQS) and s == 0:
                        copy_outputs(g, h - 2)
                    for hf in range(2):
                        if live(k, 2, SEQS):
                            copy_probs(k - 2, s, (2 * hf, 2 * hf + 1))
                        if hf == 0 and live(k, 4, SEQS) and s == 1:
                            copy_turned(g, h - 2)
                    if live(k, 1, SEQS) and st == "xa0":
                        exps(k - 1, 1 - s)
                skewed(act, SEQS, 4, step)

            def inner(st, width, scale):
                g = G[st]

                def copy_projections(i, s):
                    hold(act, g["qk_summed" if st == "sa" else "qk_projected"], i + 1)
                    src = scratch[0:width, :] if st == "sa" else S[0:width, 1024:2048]
                    act.activation(k_part(0, s)[0:width], src, ACT.Copy).then_inc(g["qk_hi"].sem, 1)

                def exps(i, s, heads):
                    for n in heads:
                        p = probs[:, s * 2048 + n * SEQ:s * 2048 + (n + 1) * SEQ]
                        last = act.activation(p, p if st == "la" else S[:, n * SEQ:(n + 1) * SEQ], ACT.Exp, scale=scale,
                                              bias=mx[:, s * HEADS + n:s * HEADS + n + 1],
                                              accum_out=ssum[:, s * HEADS + n:s * HEADS + n + 1])
                    if n == HEADS - 1:
                        last.then_inc(g["exped"].sem, 1)

                def step(k, s, h):
                    if live(k, 2, TILES):
                        hold(act, g["v_summed"], k - 1)
                        act.activation(v_part(0, s)[:, 0:D], vsum[:, 0:D], ACT.Copy).then_inc(g["v_hi"].sem, 1)
                    if live(k, 3, TILES):
                        hold(act, g["p_turned"], k - 2)
                        act.activation(p_part(0, 1 - s)[:, 0:1024], AB[:, :], ACT.Copy).then_inc(g["pt_hi"].sem, 1)
                    if live(k, 2, TILES):
                        hold(act, g["maxima"], k - 1)
                        exps(k - 2, s, range(HEADS // 2))
                    if live(k, 5, TILES):
                        copy_turned(g, k - 5)
                    if live(k, 4, TILES):
                        copy_outputs(g, k - 4)
                    if live(k, 0, TILES):
                        copy_projections(k, s)
                    if live(k, 2, TILES):
                        exps(k - 2, s, range(HEADS // 2, HEADS))
                    if live(k, 4, TILES) and st == "la":
                        hold(act, g["resid"], k - 3)
                        hold(act, g["rstd"], k - 4)
                        act.activation(junk[:, :], tile(xn_all, k - 4), ACT.Square, scale=D ** -0.5,
                                       accum_out=mv[:, 0:1]).then_inc(g["squared"].sem, 1)
                skewed(act, TILES, 5, step)

            cross("xa0")
            inner("sa", P, SA_SCALE)
            g = G["ffn"]
            act.wait_ge(prep_mm, 4)
            act.activation(wb[:, :], AB[:, 0:512], ACT.Copy)
            act.activation(cg[:, :], AB[:, 512:1024], ACT.Copy).then_inc(prep_act, 1)
            act.wait_ge(prep_dve, 3)

            def relus(i, s):
                for n in range(2 * EXPERTS):
                    hold(act, g["expert"], 16 * i + n + 1)
                    if n < 2:
                        out = acc[:, s * D + n * P:s * D + (n + 1) * P]
                    else:
                        hold(act, g["added"], 14 * i + max(n - 5, 0))
                        out = relu[:, (n % 4) * P:(n % 4 + 1) * P]
                    act.activation(out, S[:, (n % 4) * 512:(n % 4) * 512 + P], ACT.Relu, bias=bec[:, n:n + 1],
                                   scale=counts[:, n // 2:n // 2 + 1]).then_inc(g["relued"].sem, 1)

            def step(k, s, h):
                if live(k, 0, TILES):
                    relus(k, s)
                if live(k, 1, TILES):
                    copy_turned(g, k - 1)
            skewed(act, TILES, 1, step)
            cross("xa1")
            g = G["ssm"]

            def step(k, s, h):
                hold(act, g["v_projected"], k - 1)
                act.sem_inc(act_passed, 1)
                act.activation(xs[:, s * D:(s + 1) * D].rearrange("p (c n) -> p c n", c=DC),
                               XT[:, :, bass.ts(k, P)], ACT.Copy).then_inc(g["x_copied"].sem, 1)
            hold(act, G["xa1"]["xt"], TILES)
            skewed(act, TILES, 0, step)
            g = G["rope"]

            def step(k, s, h):
                if live(k, 0, TILES):
                    hold(act, g["rstd"], k)
                    act.activation(junk[:, :], tile(xn_all, k), ACT.Square, scale=D ** -0.5,
                                   accum_out=mv[:, 0:1]).then_inc(g["squared"].sem, 1)
                if live(k, 1, TILES):
                    copy_turned(g, k - 1)
            hold(act, G["ssm"]["normed"], TILES)
            skewed(act, TILES, 1, step)
            inner("la", 4 * DH, LA_SCALE)
            g, w = G["moe"], W["moe"]
            hold(act, G["la"]["xt"], TILES)
            hold(act, G["la"]["summed_up"], TILES)
            act.activation(part_of(xt_split, 0), xt_all[:, :], ACT.Copy).then_inc(prep_act, 1)

            def step(k, u, h):
                m, e = k - 1, 2 * h + (u - 1) // 2
                s = u // 2
                if isinstance(k, int) and k == 1:
                    act.wait_ge(made, 5)
                    act.activation(wgt[:, 8:16], wgt[:, 0:8], ACT.Exp).then_inc(prep_act, 1)
                split, gates = u % 2 == 0 and live(k, 0, CHUNKS * EXPERTS), live(k, 1, CHUNKS * EXPERTS)
                if split:
                    act.wait_ge(w_loaded[s], 32 * (h + 1))
                    if not isinstance(k, int) or k >= 4:
                        hold(act, g["chunk_out"], 4 * (k - 2))
                for f in range(FT):
                    if split:
                        r = slice(f * 512, (f + 1) * 512)
                        act.activation(part_of(w12[s], 0)[:, r], w12_in[:, r], ACT.Copy).then_inc(g["w12_hi"].sem, 1)
                        r = slice(f * 256, (f + 1) * 256)
                        act.activation(part_of(w3[s], 0)[:, r], w3_in[:, r], ACT.Copy).then_inc(g["w3_hi"].sem, 1)
                    if gates:
                        hold(act, g["hidden"], 8 * m + f + 1)
                        hold(act, g["gated"], 8 * m + f - 1)
                        act.sem_inc(act_passed, 1)
                        act.activation(gated[:, (f % 2) * CHUNK:(f % 2 + 1) * CHUNK],
                                       S[:, (f % 2) * 1024:(f % 2) * 1024 + 512], ACT.Silu,
                                       bias=w["b1"][:, bass.ds(e * FT + f, 1)]).then_inc(g["silued"].sem, 1)
            skewed(act, CHUNKS * EXPERTS, 1, step, unroll=4)

        @block.gpsimd
        def _(pool):
            chain = Chain(pool, pool_chain)
            for i, value in enumerate((-0.5, LN_EPS, RMS_EPS)):
                pool.memset(half[:, i:i + 1], value).then_inc(made, 1)
            pool.memset(ones[:, :], 1.0).then_inc(made, 1)
            pool.wait_ge(made, 4)

            def inverse_root(g, h, eps, source, waited, signal, out=rstd[:, :]):
                hold(pool, g[waited], h + 1)
                chain.link(pool.tensor_tensor(var[:, :], source, half[:, eps:eps + 1], ALU.add))
                pool.tensor_tensor(out, var[:, :], half[:, 0:1], ALU.pow).then_inc(g[signal].sem, 1)

            def settle():
                pool.sem_inc(pool_passed, 1)

            def root_of_variance(g, h):
                inverse_root(g, h, 1, mv[:, 1:2], "stats", "rstd")

            def add_bias(g, h, bias, ready):
                hold(pool, ready, h + 1)
                pool.tensor_tensor(tile(x, h), tile(x, h), bias, ALU.add).then_inc(g["biased"].sem, 1)

            def ln_step(k, s, h):
                root_of_variance(G["ln"], k)
                chain.restart()
            skewed(pool, TILES, 0, ln_step)

            def split_values(g, i, s, cols):
                hold(pool, g["v_hi"], i + 1)
                pool.tensor_tensor(v_part(1, s)[:, 0:cols], vsum[:, 0:cols], v_part(0, s)[:, 0:cols], ALU.subtract)\
                    .then_inc(g["v_lo"].sem, 1)

            def cross(st):
                g, w, prev = G[st], W[st], G[PREV[st]]
                pool.wait_ge(*loaded[st])

                def negate_mask(b, s, h):
                    pool.wait_ge(mask_loaded[s], 64 * (h + 1))
                    hold(pool, g["masked"], 8 * (b - 1))
                    settle()
                    pool.tensor_scalar(neg[:, s * KEYS:(s + 1) * KEYS], mask_i[:, s * KEYS:(s + 1) * KEYS],
                                       1.0e9, -1.0e9, ALU.mult, ALU.add).then_inc(G["xa0"]["negated"].sem, 1)

                def weigh(b, s):
                    for c in range(4):
                        hold(pool, g["powered"], 8 * b + 2 * c + 2)
                        p = probs[:, s * 2048 + c * 512:s * 2048 + (c + 1) * 512].rearrange("p (n k) -> p n k", n=2)
                        gw = gp[:, s * KEYS:(s + 1) * KEYS].unsqueeze(1).broadcast_to([P, 2, KEYS])
                        pool.tensor_tensor(p, p, gw, ALU.mult).then_inc(g["weighted"].sem, 1)

                def step(k, s, h):
                    if live(k, 0, SEQS) and s == 0:
                        hold(pool, prev["normed"], h + 1)
                        add_bias(g, h, w["bo"], prev["resid"] if st == "xa1" else prev["normed"])
                    if live(k, 1, SEQS):
                        if st == "xa0":
                            negate_mask(k - 1, 1 - s, h - 1 if s == 0 else h)
                        split_values(g, k - 1, 1 - s, 2 * D)
                    if live(k, 3, SEQS) and s == 0:
                        root_of_variance(g, h - 2)
                    if live(k, 1, SEQS) and st == "xa0":
                        weigh(k - 1, 1 - s)
                    if st == "xa1" and live(k, 3, SEQS) and s == 0:
                        hold(pool, g["normed"], h - 1)
                        settle()
                        pool.tensor_copy(tile(xn_all, h - 2), xn[:, :]).then_inc(g["kept"].sem, 1)
                    chain.restart()
                skewed(pool, SEQS, 4, step)

            def copy_tile(g, prev_xt, k, s, readers):
                hold(pool, prev_xt, k + 1)
                hold(pool, g[readers], k - 1)
                settle()
                pool.tensor_copy(xs[:, s * D:(s + 1) * D].rearrange("p (c n) -> p c n", c=DC),
                                 XT[:, :, bass.ts(k, P)]).then_inc(g["x_copied"].sem, 1)

            def inner(st):
                g, w, prev = G[st], W[st], G[PREV[st]]
                pool.wait_ge(*loaded[st])

                def step(k, s, h):
                    if live(k, 0, TILES):
                        copy_tile(g, prev["xt"], k, s, "v_projected")
                        if st == "sa":
                            hold(pool, prev["normed"], k + 1)
                            add_bias(g, k, w["bo"], prev["resid"])
                    if live(k, 2, TILES):
                        split_values(g, k - 2, s, D)
                    if live(k, 4, TILES):
                        if st == "sa":
                            root_of_variance(g, k - 4)
                        else:
                            inverse_root(g, k - 4, 2, mv[:, 0:1], "squared", "rstd")
                            pool.tensor_tensor(tile(x, k - 4), tile(x, k - 4), tile(xn_all, k - 4), ALU.add)\
                                .then_inc(g["summed_up"].sem, 1)
                    chain.restart()
                skewed(pool, TILES, 5, step)

            cross("xa0")
            inner("sa")
            def times(out, a, b):
                return pool.tensor_tensor(out, a, b.broadcast_to([P, a.shape[1]]), ALU.mult)

            pool.wait_ge(prep_dve, 4)
            chain.mark(pool.memset(two[:, :], 2.0))
            chain.mark(pool.memset(tabR[:, 0:1], 1.0))
            chain.link(pool.memset(tabI[:, 0:1], 0.0))
            m, a, b = 1, (lr, li), (lr2, li2)
            while m < SEQ:
                lo, hi = slice(0, m), slice(m, 2 * m)
                (ar, ai), (br, bi) = a, b
                chain.mark(times(tabR[:, hi], tabR[:, lo], ar))
                chain.link(times(tabt[:, lo], tabI[:, lo], ai))
                chain.link(pool.tensor_tensor(tabR[:, hi], tabR[:, hi], tabt[:, lo], ALU.subtract))
                chain.mark(times(tabI[:, hi], tabI[:, lo], ar))
                chain.link(times(tabt[:, lo], tabR[:, lo], ai))
                chain.link(pool.tensor_tensor(tabI[:, hi], tabI[:, hi], tabt[:, lo], ALU.add))
                chain.mark(times(sq, ai, ai))
                chain.mark(times(sq2, ar, ar))
                chain.link(times(bi, ar, ai))
                chain.mark(pool.tensor_tensor(br, sq2, sq, ALU.subtract))
                chain.link(times(bi, bi, two[:, :]))
                a, b = b, a
                m *= 2
            settle()
            pool.tensor_copy(tabR[:, SEQ:], tabR[:, 0:SEQ]).then_inc(pool_chain, 1)
            pool.tensor_copy(tabI[:, SEQ:], tabI[:, 0:SEQ]).then_inc(pool_chain, 1)
            chain.n += 2
            chain.join()
            pool.sem_inc(tables, 1)
            chain.restart()

            def ffn_step(k, s, h):
                if live(k, 1, TILES):
                    root_of_variance(G["ffn"], k - 1)
                chain.restart()
            skewed(pool, TILES, 1, ffn_step)
            cross("xa1")
            g, w = G["ssm"], W["ssm"]
            pool.wait_ge(*loaded["ssm"])

            def ssm_step(k, s, h):
                if live(k, 0, TILES):
                    hold(pool, G["xa1"]["kept"], k + 1)
                    hold(pool, g["biased"], k)
                    chain.link(pool.tensor_tensor(junk[:, :], tile(xn_all, k), w["d"], ALU.mult))
                    pool.tensor_tensor(tile(x, k), tile(x, k), junk[:, :], ALU.add).then_inc(g["biased"].sem, 1)
                if live(k, 2, TILES):
                    root_of_variance(g, k - 2)
                chain.restart()
            skewed(pool, TILES, 2, ssm_step)
            def rope_step(k, s, h):
                hold(pool, G["rope"]["roped"], k - 1)
                inverse_root(G["rope"], k, 2, mv[:, 0:1], "squared", "rstd", rstd2[:, s:s + 1])
                chain.restart()
            skewed(pool, TILES, 0, rope_step)
            inner("la")
            g = G["moe"]

            def split_weights(e, s, h):
                pool.wait_ge(w_loaded[s], 32 * (h + 1))
                if not isinstance(e, int) or e >= 2:
                    hold(pool, g["chunk_out"], 8 * (e - 1))
                for f in range(FT):
                    r = slice(f * 256, (f + 1) * 256)
                    hold(pool, g["w3_hi"], 8 * e + f + 1)
                    pool.tensor_tensor(part_of(w3[s], 1)[:, r], w3_in[:, r], part_of(w3[s], 0)[:, r], ALU.subtract)
                    r = slice(f * 512, (f + 1) * 512)
                    hold(pool, g["w12_hi"], 8 * e + f + 1)
                    last = pool.tensor_tensor(part_of(w12[s], 1)[:, r], w12_in[:, r], part_of(w12[s], 0)[:, r],
                                              ALU.subtract)
                last.then_inc(g["w_split"].sem, 1)
            hold(pool, G["ffn"]["xt"], TILES)
            skewed(pool, EXPERTS, 0, split_weights)

        @block.vector
        def _(dve):
            chain = Chain(dve, dve_chain)
            dve.wait_ge(*loaded["x"])
            dve.wait_ge(*loaded["const"])
            K = W["const"]

            def settle():
                dve.sem_inc(dve_passed, 1)

            def tile_stats(g, h):
                chain.link(dve.bn_stats(stat6[:, :], tile(x, h)))
                dve.bn_aggr(mv[:, :], stat6[:, :]).then_inc(g["stats"].sem, 1)

            def normalise(g, h, out):
                hold(dve, g["rstd"], h + 1)
                dve.tensor_scalar(out, tile(x, h), mv[:, 0:1], rstd[:, :], ALU.subtract, ALU.mult)\
                   .then_inc(g["normed"].sem, 1)

            def add_output(g, h, src):
                hold(dve, g["projected"], h + 1)
                if "biased" in g:
                    hold(dve, g["biased"], h + 1)
                dve.tensor_tensor(tile(x, h), src, tile(x, h), ALU.add).then_inc(g["resid"].sem, 1)
                hold(dve, g["resid"], h + 1)
                settle()

            def ln_step(k, s, h):
                tile_stats(G["ln"], k)
                hold(dve, G["ln"]["turned"], k)
                normalise(G["ln"], k, xn[:, :])
                chain.restart()
            skewed(dve, TILES, 0, ln_step)

            def cross(st):
                g, w = G[st], W[st]
                dve.wait_ge(*loaded[st])

                def take_queries(h):
                    hold(dve, g["q_projected"], h + 1)
                    q = scratch[:, 0:256]
                    for hf in range(2):
                        last = dve.tensor_scalar(q[:, hf * P:(hf + 1) * P], C[:, 256 + hf * P:256 + (hf + 1) * P],
                                                 w["bq"][:, hf:hf + 1], DH ** -0.5, ALU.add, ALU.mult)
                    last.then_inc(g["q_taken"].sem, 1)
                    hold(dve, g["q_taken"], h + 1)
                    settle()
                    chain.link(dve.tensor_copy(qsplit[:, 0:256], q))
                    chain.link(dve.tensor_tensor(qsplit[:, 256:512], q, qsplit[:, 0:256], ALU.subtract))

                def copy_queries(h):
                    hold(dve, g["scored"], 2 * h)
                    for part in range(2):
                        src = qsplit[:, part * 256:(part + 1) * 256].rearrange("p (f b q) -> p b f q", f=2, b=2)
                        both = qbuf[:, part * 4096:(part + 1) * 4096].rearrange("p (b r) -> p b r", b=2)[:, :, 0:256]
                        blocks = both.rearrange("p b (f a q) -> p b f a q", f=2, a=2)
                        for par in range(2):
                            last = dve.tensor_scalar(blocks[:, :, :, par, :], src, K["par_x"][:, par:par + 1], None,
                                                     ALU.mult)
                            if part == 0 or par == 0:
                                chain.mark(last)
                    last.then_inc(g["q_copied"].sem, 1)
                    hold(dve, g["q_copied"], h + 1)
                    settle()

                def sum_values(b, s):
                    hold(dve, g["v_projected"], b + 1)
                    hold(dve, g["v_lo"], b)
                    dve.tensor_tensor(vsum[:, :].rearrange("p (k n) -> p k n", k=2),
                                      AB[:, 512:1024].rearrange("p (k n) -> p k n", k=2),
                                      w["bv"].unsqueeze(1).broadcast_to([P, 2, D]), ALU.add)\
                       .then_inc(g["v_summed"].sem, 1)

                def split_keys(b, s):
                    hold(dve, g["k_hi"], b + 1)
                    for hf in range(2):
                        r = slice(hf * KEYS, (hf + 1) * KEYS)
                        last = dve.scalar_tensor_tensor(out=k_part(1, s)[:, r], in0=AB[:, r],
                                                        scalar=w["bk"][:, hf:hf + 1], in1=k_part(0, s)[:, r],
                                                        op0=ALU.add, op1=ALU.subtract)
                    last.then_inc(g["k_copied"].sem, 1)

                def split_probs(b, s):
                    for c in range(4):
                        hold(dve, g["pt_hi"], 4 * b + c + 1)
                        r = slice(c * 512, (c + 1) * 512)
                        dve.tensor_tensor(p_part(1, s)[:, r], AB[:, (c % 2) * 512:(c % 2 + 1) * 512],
                                          p_part(0, s)[:, r], ALU.subtract).then_inc(g["pt_lo"].sem, 1)

                def mask_scores(b, s):
                    hold(dve, G["xa0"]["negated"], b + 1)
                    hold(dve, g["scored"], b + 1)
                    settle()
                    for n in range(PAIRS):
                        o = (n % 4) * 512 + (n // 4) * KEYS
                        dve.tensor_tensor_reduce(out=probs[:, s * 2048 + n * KEYS:s * 2048 + (n + 1) * KEYS],
                                                 in0=S[:, o:o + KEYS], in1=neg[:, s * KEYS:(s + 1) * KEYS],
                                                 scale=-1.0, scalar=BIG, op0=ALU.add, op1=ALU.min,
                                                 accum_out=mx[:, s * HEADS + n:s * HEADS + n + 1])\
                           .then_inc(g["masked"].sem, 1)

                def row_maxima(b, s):
                    banks = S.rearrange("p (j f k) -> p f j k", j=4, f=2)
                    hold(dve, g["scored"], b + 1)
                    for hf in range(2):
                        dve.tensor_reduce(mx[:, s * HEADS + 4 * hf:s * HEADS + 4 * hf + 4], banks[:, hf, :, :],
                                          AX.X, ALU.max, negate=True).then_inc(g["maxima"].sem, 1)

                def normalise_outputs(b, s, turned):
                    hold(dve, g["o_turned"], turned)
                    hold(dve, g["pv_done"], b + 1)
                    r = rsum[:, s * HEADS:s * HEADS + PAIRS]
                    chain.link(dve.reciprocal(r, ssum[:, s * HEADS:s * HEADS + PAIRS]))
                    for par in range(2):
                        rows = slice(par * SEQ, (par + 1) * SEQ)
                        last = dve.tensor_tensor(
                            obuf[rows, s * P:(s + 1) * P].rearrange("p (n d) -> p n d", n=PAIRS),
                            M[rows, 0:256].rearrange("p (n a d) -> p n a d", n=PAIRS, a=2)[:, :, par, :],
                            r[rows, :].unsqueeze(2).broadcast_to([SEQ, PAIRS, DH]), ALU.mult)
                    last.then_inc(g["o_normed"].sem, 1)

                def step(k, s, h):
                    closes = live(k, 3, SEQS) and s == 0
                    if live(k, 0, SEQS) and s == 0:
                        take_queries(h)
                    if live(k, 3, SEQS):
                        normalise_outputs(k - 3, 1 - s, h - 2 if s == 0 else h - 1)
                    if live(k, 0, SEQS):
                        split_keys(k, s)
                    if live(k, 1, SEQS):
                        sum_values(k - 1, 1 - s)
                    if live(k, 2, SEQS):
                        split_probs(k - 2, s)
                    if closes:
                        add_output(g, h - 2, C[:, 256:512])
                        tile_stats(g, h - 2)
                    if live(k, 1, SEQS):
                        (mask_scores if st == "xa0" else row_maxima)(k - 1, 1 - s)
                    if closes:
                        if st == "xa1":
                            hold(dve, g["kept"], h - 2)
                        normalise(g, h - 2, xn[:, :])
                    if live(k, 0, SEQS) and s == 0:
                        copy_queries(h)
                    chain.restart()
                skewed(dve, SEQS, 4, step)

            def inner(st, rows, scale):
                g, w = G[st], W[st]
                dve.wait_ge(*loaded[st])
                blocks_of = K["par_s" if st == "sa" else "par_x"]
                width = rows + 2 * DH

                def sum_projections(i, s):
                    hold(dve, g["qk_projected"], i + 1)
                    hold(dve, g["qk_copied"], i)
                    dve.tensor_tensor(scratch[0:width, :].rearrange("p (n q) -> p n q", n=PAIRS),
                                      S[0:width, 1024:2048].rearrange("p (n q) -> p n q", n=PAIRS),
                                      w["b"].unsqueeze(2).broadcast_to([P, PAIRS, P]), ALU.add)\
                       .then_inc(g["qk_summed"].sem, 1)

                def sum_values(i):
                    hold(dve, g["v_projected"], i + 1)
                    hold(dve, g["v_lo"], i)
                    if st == "sa":
                        sums = dve.tensor_tensor(vsum[:, 0:D], AB[:, 0:D], w["bv"], ALU.add)
                    else:
                        sums = dve.tensor_copy(vsum[:, 0:D], AB[:, 0:D])
                    sums.then_inc(g["v_summed"].sem, 1)

                def split_queries_and_keys(i, s):
                    hold(dve, g["qk_hi"], i + 1)
                    if st == "sa":
                        chain.link(dve.tensor_tensor(k_part(1, s)[0:width], scratch[0:width, :], k_part(0, s)[0:width],
                                                     ALU.subtract))
                    else:
                        dve.tensor_tensor(k_part(1, s)[0:width], S[0:width, 1024:2048], k_part(0, s)[0:width],
                                          ALU.subtract).then_inc(g["qk_summed"].sem, 1)
                        hold(dve, g["qk_summed"], i + 1)
                        settle()
                    for part in range(2):
                        src = k_part(part, s)[0:rows].rearrange("p (n q) -> p n q", q=SEQ)
                        out = q_part(part, s)[0:rows].rearrange("p (n a q) -> p n a q", n=HEADS, a=2)
                        for par in range(2):
                            chain.mark(dve.tensor_scalar(out[:, :, par, :], src, blocks_of[0:rows, par:par + 1], None,
                                                         ALU.mult))
                    chain.join()
                    for part in range(2):
                        last = dve.tensor_copy(k_part(part, s)[0:2 * DH], k_part(part, s)[rows:width])
                    last.then_inc(g["qk_copied"].sem, 1)

                def split_probs(i, s):
                    hold(dve, g["pt_hi"], i + 1)
                    dve.tensor_tensor(p_part(1, s)[:, 0:1024], AB[:, :], p_part(0, s)[:, 0:1024], ALU.subtract)\
                       .then_inc(g["pt_lo"].sem, 1)

                def row_maxima(i, s):
                    hold(dve, g["scored"], i + 1)
                    p = probs[:, s * 2048:s * 2048 + 1024].rearrange("p (n k) -> p n k", n=HEADS)
                    src = S[:, 0:1024].rearrange("p (n k) -> p n k", n=HEADS)
                    if st == "la":
                        chain.link(dve.tensor_tensor(p, src, K["causal"].unsqueeze(1).broadcast_to([P, HEADS, SEQ]),
                                                     ALU.add))
                        src = p
                    m = mx[:, s * HEADS:(s + 1) * HEADS]
                    chain.link(dve.tensor_reduce(m, src, AX.X, ALU.max, negate=True))
                    dve.tensor_scalar(m, m, scale, None, ALU.mult).then_inc(g["maxima"].sem, 1)

                def normalise_outputs(i, s):
                    hold(dve, g["exped"], i + 1)
                    z = ssum[:, s * HEADS:(s + 1) * HEADS]
                    r = rsum[:, s * HEADS:(s + 1) * HEADS]
                    chain.link(dve.reciprocal(r, z))
                    hold(dve, g["pv_done"], i + 1)
                    for b in range(2):
                        src = M[:, 0:256] if b == 0 else C[:, 256:512]
                        for par in range(2):
                            q = slice(par * SEQ, (par + 1) * SEQ)
                            last = dve.tensor_tensor(
                                obuf[q, s * D + b * P:s * D + (b + 1) * P].rearrange("p (n d) -> p n d", n=PAIRS),
                                src[q].rearrange("p (n a d) -> p n a d", n=PAIRS, a=2)[:, :, par, :],
                                r[q].rearrange("p (n b) -> p n b", b=2)[:, :, b:b + 1].broadcast_to([SEQ, PAIRS, DH]),
                                ALU.mult)
                    last.then_inc(g["o_normed"].sem, 1)

                def step(k, s, h):
                    if live(k, 2, TILES):
                        sum_values(k - 2)
                        row_maxima(k - 2, s)
                    if live(k, 5, TILES):
                        if st == "sa":
                            normalise(g, k - 5, xn[:, :])
                        else:
                            hold(dve, g["rstd"], k - 4)
                            dve.scalar_tensor_tensor(out=xn[:, :], in0=tile(xn_all, k - 5), scalar=rstd[:, :],
                                                     in1=w["norm2"], op0=ALU.mult, op1=ALU.mult)\
                               .then_inc(g["normed"].sem, 1)
                    if live(k, 3, TILES):
                        split_probs(k - 3, 1 - s)
                    if live(k, 0, TILES) and st == "sa":
                        sum_projections(k, s)
                    if live(k, 4, TILES):
                        if st == "sa":
                            add_output(g, k - 4, M[:, 256:512])
                            tile_stats(g, k - 4)
                        else:
                            hold(dve, g["projected"], k - 3)
                            dve.tensor_tensor(tile(xn_all, k - 4), M[:, 256:512], tile(xn_all, k - 4), ALU.add)\
                               .then_inc(g["resid"].sem, 1)
                    if live(k, 0, TILES):
                        split_queries_and_keys(k, s)
                    if live(k, 3, TILES):
                        normalise_outputs(k - 3, 1 - s)
                    chain.restart()
                skewed(dve, TILES, 5, step)

            def choose(bias, mm):
                dve.wait_ge(prep_mm, mm)
                dve.tensor_scalar(gateT[0:8, :], S[0:8, 0:TOKENS], bias[0:8, :], None, ALU.add).then_inc(prep_dve, 1)
                dve.wait_ge(prep_mm, mm + 1)
                chain.link(dve.tensor_copy(logit[:, :], S[:, 1024:1024 + 64]))
                dve.sem_inc(logits_taken, 1)
                for i in range(TILES):
                    r = slice(i * 8, (i + 1) * 8)
                    chain.mark(dve.max(top[:, r], logit[:, r]))
                chain.join()
                for i in range(TILES):
                    r = slice(i * 8, (i + 1) * 8)
                    chain.mark(dve.max_index(topi[:, r], top[:, r], logit[:, r]))
                chain.join()
                chain.link(dve.tensor_copy(topf[:, :], topi[:, :]))
                for i in range(TILES):
                    for rank, dst in ((0, hot), (1, hot2)):
                        chain.mark(dve.tensor_scalar(dst[:, i * 8:(i + 1) * 8], K["iota"],
                                                     topf[:, i * 8 + rank:i * 8 + rank + 1], None, ALU.is_equal))
                chain.join()

            cross("xa0")
            inner("sa", SA_ROWS, SA_SCALE)
            g, w = G["ffn"], W["ffn"]
            dve.wait_ge(*loaded["ffn"])
            choose(w["gate_b"], 1)
            chain.link(dve.tensor_tensor(hot[:, :], hot[:, :], hot2[:, :], ALU.add))
            dve.tensor_reduce(hot2[:, 0:8], hot[:, :].rearrange("p (t e) -> p e t", e=8), AX.X, ALU.add)\
               .then_inc(prep_dve, 1)
            dve.wait_ge(prep_mm, 3)
            chain.mark(dve.tensor_copy(omega, S[:, 1288:1289]))
            chain.link(dve.tensor_scalar(counts[:, :], S[:, 1280:1288], 1.0 / (2 * TOKENS), None, ALU.mult))
            dve.tensor_tensor(bec[:, :].rearrange("p (e f) -> p e f", e=8), w["be"].rearrange("p (e f) -> p e f", e=8),
                              counts[:, :].unsqueeze(2).broadcast_to([P, 8, 2]), ALU.mult).then_inc(prep_dve, 1)
            chain.link(dve.tensor_tensor(sq, omega, omega, ALU.mult))
            chain.link(dve.tensor_scalar(den, sq, 1.0, None, ALU.add))
            chain.link(dve.reciprocal(sq2, den))
            chain.link(dve.tensor_scalar(sq, sq, -1.0, 1.0, ALU.mult, ALU.add))
            chain.link(dve.tensor_tensor(lr, sq, sq2, ALU.mult))
            dve.tensor_scalar(li, omega, sq2, -2.0, ALU.mult, ALU.mult).then_inc(prep_dve, 1)
            dve.wait_ge(prep_dve, 4)
            chain.restart()

            def add_experts(i, s):
                for n in range(2, 2 * EXPERTS):
                    hold(dve, g["relued"], 16 * i + n + 1)
                    if n >= 4:
                        hold(dve, g["added"], 14 * i + n - 3)
                    a = acc[:, s * D + (n % 2) * P:s * D + (n % 2 + 1) * P]
                    dve.tensor_tensor(a, a, relu[:, (n % 4) * P:(n % 4 + 1) * P], ALU.add).then_inc(g["added"].sem, 1)

            def step(k, s, h):
                if live(k, 1, TILES):
                    add_output(g, k - 1, M[:, 256:512])
                    tile_stats(g, k - 1)
                if live(k, 0, TILES):
                    add_experts(k, s)
                if live(k, 1, TILES):
                    normalise(g, k - 1, xn[:, :])
                chain.restart()
            skewed(dve, TILES, 1, step)
            cross("xa1")
            g = G["ssm"]
            dve.wait_ge(prep_mm, 5)
            dve.wait_ge(tables, 1)
            dve.tensor_copy(rowR[:, :], S[:, 1024:1024 + P])
            dve.tensor_copy(rowI[:, :], S[:, 1024 + P:1024 + 2 * P]).then_inc(prep_dve, 1)
            dve.wait_ge(prep_dve, 5)
            chain.restart()

            def turn_phase(src, real, imag, forward, out, s):
                a = acc[:, 0:D].rearrange("p (c n) -> p c n", c=DC)
                v = src.rearrange("p (c n) -> p c n", c=DC)
                chain.mark(dve.tensor_tensor(a, v, real.unsqueeze(1).broadcast_to([P, DC, P]), ALU.mult))
                b = acc[:, D:2 * D]
                chain.mark(dve.tensor_tensor(b[:, 0:P], src[:, P:2 * P], imag, ALU.mult))
                chain.link(dve.tensor_tensor(b[:, P:2 * P], src[:, 0:P], imag, ALU.mult))
                chain.mark(dve.tensor_tensor(out[:, s * D:s * D + P], acc[:, 0:P], b[:, 0:P],
                                             ALU.subtract if forward else ALU.add))
                return dve.tensor_tensor(out[:, s * D + P:(s + 1) * D], acc[:, P:2 * P], b[:, P:2 * P],
                                         ALU.add if forward else ALU.subtract)

            def step(k, s, h):
                if live(k, 3, TILES):
                    normalise(g, k - 3, tile(xn_all, k - 3))
                if live(k, 0, TILES):
                    hold(dve, g["v_projected"], k + 1)
                    turn_phase(AB[:, 0:D], rowR[:, :], rowI[:, :], False, rot, s).then_inc(g["rotated"].sem, 1)
                    hold(dve, g["rotated"], k + 1)
                if live(k, 1, TILES):
                    hold(dve, g["summed"], k)
                    turn_phase(S[:, 0:D], tabR[:, :], tabI[:, :], True, rot2, 1 - s).then_inc(g["modulated"].sem, 1)
                    hold(dve, g["modulated"], k)
                if live(k, 2, TILES):
                    add_output(g, k - 2, M[:, 256:512])
                    tile_stats(g, k - 2)
                chain.restart()
            skewed(dve, TILES, 3, step)
            g = G["rope"]
            dve.wait_ge(*loaded["la"])

            def step(k, s, h):
                hold(dve, g["rstd"], k + 1)
                hold(dve, g["roped"], k)
                xr = rot2[:, 0:D]
                chain.link(dve.scalar_tensor_tensor(out=xr, in0=tile(xn_all, k), scalar=rstd2[:, s:s + 1],
                                                    in1=W["la"]["norm1"], op0=ALU.mult, op1=ALU.mult))
                xe, xo = (xr.rearrange("p (n a) -> p n a", a=2)[:, :, a] for a in range(2))
                for j, (v, tab) in enumerate(((xe, "cos"), (xo, "sin"), (xe, "sin"), (xo, "cos"))):
                    chain.mark(dve.tensor_tensor(acc[:, j * P:(j + 1) * P], v, K[tab], ALU.mult))
                chain.join()
                hold(dve, g["turned"], k)
                dve.tensor_tensor(rot[:, 0:P], acc[:, 0:P], acc[:, P:2 * P], ALU.subtract)
                dve.tensor_tensor(rot[:, P:2 * P], acc[:, 2 * P:3 * P], acc[:, 3 * P:4 * P], ALU.add)\
                   .then_inc(g["roped"].sem, 1)
                chain.restart()
            skewed(dve, TILES, 0, step)
            inner("la", LA_ROWS, LA_SCALE)
            g, w = G["moe"], W["moe"]
            dve.wait_ge(*loaded["moe"])
            dve.wait_ge(prep_act, 2)
            dve.tensor_tensor(part_of(xt_split, 1), xt_all[:, :], part_of(xt_split, 0), ALU.subtract)\
               .then_inc(prep_dve, 1)
            choose(w["router_b"], 6)
            tops = top[:, :].rearrange("p (t r) -> p t r", r=8)
            dve.tensor_tensor(wgt[:, 0:8], tops[:, :, 1], tops[:, :, 0], ALU.subtract).then_inc(made, 1)
            dve.wait_ge(prep_act, 3)
            chain.link(dve.tensor_scalar(wgt[:, 16:24], wgt[:, 8:16], 1.0, None, ALU.add))
            chain.link(dve.reciprocal(wgt[:, 24:32], wgt[:, 16:24]))
            chain.link(dve.tensor_tensor(wgt[:, 16:24], wgt[:, 8:16], wgt[:, 24:32], ALU.mult))
            for dst, wi in ((hot, 24), (hot2, 16)):
                v = dst[:, :].rearrange("p (t e) -> p t e", e=8)
                chain.mark(dve.tensor_tensor(v, v, wgt[:, wi:wi + 8].unsqueeze(2).broadcast_to([P, 8, 8]), ALU.mult))
            chain.join()
            dve.tensor_tensor(comb[:, :], hot[:, :], hot2[:, :], ALU.add).then_inc(prep_dve, 1)
            dve.wait_ge(prep_dve, 8)
            chain.restart()

            def take_combination():
                dve.wait_ge(prep_mm, 15)
                dve.tensor_copy(combT[0:8, :], AB[0:8, 0:TOKENS]).then_inc(prep_dve, 1)

            def add_biases():
                for i in range(TILES):
                    dve.wait_ge(prep_mm, 16 + i)
                    dve.tensor_tensor(tile(x, i), sums[2 + i % 2], tile(x, i), ALU.add).then_inc(prep_dve, 1)
                dve.wait_ge(prep_dve, 9 + TILES)

            def gate(m, u, h):
                c = u % 2
                e = 2 * h + u // 2
                hi, lo = (part_of(hid[c], part).rearrange("p (f n) -> p f n", f=FT) for part in range(2))
                if not isinstance(m, int) or m >= 2:
                    hold(dve, g["chunk_out"], 4 * (m - 1))
                for f in range(FT):
                    hold(dve, g["silued"], 8 * m + f + 1)
                    hold(dve, g["gated_lo"], 8 * m + f)
                    dve.scalar_tensor_tensor(out=product, in0=S[:, (f % 2) * 1024 + 512:(f % 2 + 1) * 1024],
                                             scalar=w["b2"][:, bass.ds(e * FT + f, 1)],
                                             in1=gated[:, (f % 2) * CHUNK:(f % 2 + 1) * CHUNK],
                                             op0=ALU.add, op1=ALU.mult).then_inc(g["gated"].sem, 1)
                    hold(dve, g["gated"], 8 * m + f + 1)
                    dve.tensor_copy(hi[:, f, :], product).then_inc(g["gated_hi"].sem, 1)
                    hold(dve, g["gated_hi"], 8 * m + f + 1)
                    dve.tensor_tensor(lo[:, f, :], product, hi[:, f, :], ALU.subtract).then_inc(g["gated_lo"].sem, 1)

            def combine(m, u, e):
                c = u % 2
                for i in range(4):
                    tok = c * 4 + i
                    hold(dve, g["chunk_out"], 4 * m + i + 1)
                    hold(dve, g["out"], 4 * m - 4)
                    xt = x[:, tok * D:(tok + 1) * D]
                    dve.scalar_tensor_tensor(out=xt, in0=sums[i],
                                             scalar=comb[:, bass.ds(e + tok * 8, 1)], in1=xt,
                                             op0=ALU.mult, op1=ALU.add).then_inc(g["out"].sem, 1)

            def step(m, u, h):
                first = isinstance(m, int) and m == 1
                if first:
                    take_combination()
                if live(m, 0, CHUNKS * EXPERTS):
                    gate(m, u, h)
                if first:
                    add_biases()
                if live(m, 1, CHUNKS * EXPERTS):
                    combine(m - 1, (u - 1) % 4, 2 * h + u // 2 if u % 2 else 2 * h + u // 2 - 1)
            skewed(dve, CHUNKS * EXPERTS, 1, step, unroll=4)



def channels_first(w):
    return w.reshape(DC, P, -1).transpose(1, 0, 2)


def column(b):
    return b.reshape(DC, P).T


def rows(b):
    return np.broadcast_to(b, (P, b.shape[-1]))


def padded(a):
    out = np.zeros((P, a.shape[1]), a.dtype)
    out[:a.shape[0]] = a
    return out


def by_parity(wo):
    return wo.reshape(PAIRS, 2, DH, D).transpose(0, 2, 1, 3).reshape(P, 2, D)


def constants():
    p = np.arange(P)
    c = {"ident": np.eye(P)}
    par = (p[:, None] // DH) % 2 == np.arange(2)[None, :]
    c["par_x"] = par
    rot_par = ((p[:, None] - 2 * DH) // ROT) % 2 == np.arange(2)[None, :]
    c["par_s"] = np.where(p[:, None] < 2 * DH, par, rot_par)
    c["iota"] = np.tile(np.arange(8), (P, 1))
    c["causal"] = np.where(np.arange(SEQ)[None, :] > (p % SEQ)[:, None], -1.0e9, 0.0)
    same = p[:, None] // SEQ == p[None, :] // SEQ
    c["tri"] = same & (p[:, None] <= p[None, :])
    half = D // 2
    theta = (1.0 / np.float32(10000.0) ** (np.arange(half, dtype=np.float32) / np.float32(half))).astype(np.float32)
    ang = ((p % SEQ).astype(np.float32)[:, None] * theta[None, :]).astype(np.float32).astype(np.float64)
    c["cos"], c["sin"] = np.cos(ang), np.sin(ang)
    return c


def fourier():
    n, k = np.arange(D), np.arange(P)
    ang = 2 * np.pi * ((n[:, None] * k[None, :]) % D) / D
    alternate = 1.0 - 2.0 * (n % 2)
    fwd = np.concatenate([np.cos(ang), -np.sin(ang)], axis=1)
    fwd[:, P] = alternate
    inv = np.concatenate([np.cos(ang), -np.sin(ang)], axis=1) * 2.0 / D
    inv[:, 0] = 1.0 / D
    inv[:, P] = alternate / D
    j = np.arange(1, P + 1)
    turns = (j[:, None] * k[None, :]) % D
    sines = -2.0 * np.sin(2 * np.pi * turns / D)
    sines[turns % P == 0] = 0.0
    return {"fwd": channels_first(fwd), "inv": channels_first(inv), "sines": sines}


def pack(name, parts):
    fields = PACKS[name]
    return np.ascontiguousarray(np.concatenate(
        [np.asarray(parts[f]).reshape(P, fields[f]).astype(np.float32, copy=False) for f in fields], axis=1))


def lay_out(v):
    out = {}
    out["x"] = v["x"].reshape(TILES, P, D).transpose(1, 0, 2).reshape(P, TILES * D)
    out["ctx"] = v["ctx_1024"].transpose(0, 2, 1).reshape(SEQS, DC, P, KEYS).transpose(0, 2, 1, 3)\
        .reshape(SEQS, P, DC * KEYS)
    out["gp"] = v["fside_BxSxS2_0"]
    out["mask"] = v["mask_BxSxS2_ik1"]
    out["const"] = pack("const", constants())
    out["four"] = pack("four", fourier())

    def cross(q, k, vv, o, bq, bk, bv, bo):
        return {"wq": channels_first(q), "wk": channels_first(k), "wv": channels_first(vv), "wo": by_parity(o),
                "bq": column(bq), "bk": column(bk), "bv": rows(bv), "bo": rows(bo)}
    out["xa0"] = pack("xa0", cross(*(v["L0_xattn_w" + n] for n in ("q_k", "k_k", "v_k", "o_k", "q_b", "k_b", "v_b", "o_b"))))
    out["xa1"] = pack("xa1", cross(*(v["L1_xattn_" + n] for n in ("W_q", "W_k", "W_v", "W_o", "b_q", "b_k", "b_v", "b_o"))))
    a = {n: v["L0_attn_" + n] for n in ("Wq", "bq", "Wk", "bk", "Wv", "bv", "Wr", "br", "Wo", "bo")}
    w = np.concatenate([a["Wq"].reshape(D, PAIRS, 2 * DH), a["Wr"].reshape(D, PAIRS, 2 * ROT),
                        a["Wk"].reshape(D, PAIRS, 2 * DH)], axis=2)
    b = np.concatenate([a["bq"].reshape(PAIRS, 2 * DH), a["br"].reshape(PAIRS, 2 * ROT),
                        a["bk"].reshape(PAIRS, 2 * DH)], axis=1)
    out["sa"] = pack("sa", {"w": channels_first(w.reshape(D, -1)), "wv": channels_first(a["Wv"]),
                            "wo": by_parity(a["Wo"]), "b": b.T, "bv": rows(a["bv"]), "bo": rows(a["bo"])})
    out["ffn"] = pack("ffn", {
        "gate_w": channels_first(v["L0_ffn_gate_w"].T), "gate_b": padded(v["L0_ffn_gate_b"][:, None]),
        "we": channels_first(v["L0_ffn_expert_w"].transpose(2, 0, 1).reshape(D, -1)),
        "be": v["L0_ffn_expert_b"].reshape(EXPERTS, DC, P).transpose(2, 0, 1)})
    out["ssm"] = pack("ssm", {"bw": channels_first(v["L1_attn_B_w"]), "ct": channels_first(v["L1_attn_C_w"].T),
                              "a": v["L1_attn_a_params"][:, None], "d": rows(v["L1_attn_D"])})
    f = {n: v["L1_ffn_" + n] for n in ("norm1_w", "Wq", "Wk", "Wv", "Wo", "norm2_w", "router_w", "router_b",
                                       "W1", "b1", "W2", "b2", "W3", "b3")}
    groups = np.arange(HEADS) // (HEADS // 4)
    wk = f["Wk"].reshape(D, 4, DH)[:, groups].reshape(D, PAIRS, 2 * DH)
    wv = f["Wv"].reshape(D, 4, DH)[:, groups].reshape(D, D)
    w = np.concatenate([f["Wq"].reshape(D, PAIRS, 2 * DH), wk], axis=2)
    out["la"] = pack("la", {"w": channels_first(w.reshape(D, -1)), "wv": channels_first(wv), "wo": by_parity(f["Wo"]),
                            "norm1": rows(f["norm1_w"]), "norm2": rows(f["norm2_w"])})

    def feature_columns(b):
        return b.reshape(EXPERTS, FT, P).transpose(2, 0, 1)
    out["moe"] = pack("moe", {"router_w": channels_first(f["router_w"]), "router_b": padded(f["router_b"][:, None]),
                              "b1": feature_columns(f["b1"]), "b2": feature_columns(f["b2"]), "b3": padded(f["b3"])})
    both = np.concatenate([f["W1"], f["W2"]], axis=2)
    out["w12"] = both.reshape(EXPERTS, DC, P, 2 * FF).transpose(0, 2, 1, 3).reshape(EXPERTS, P, DC * 2 * FF)
    out["w3"] = f["W3"].reshape(EXPERTS, FT, P, D).transpose(0, 2, 1, 3).reshape(EXPERTS, P, FT * D)
    return {n: np.ascontiguousarray(a) for n, a in out.items()}


def program(nc, arrays):
    t = {}
    for name, a in arrays.items():
        t[name] = nc.dram_tensor(f"in_{name}", a.shape, mybir.dt.from_np(a.dtype), kind="ExternalInput").ap()
    t["out"] = nc.dram_tensor("out_x", (P, TILES * D), F32, kind="ExternalOutput").ap()
    build(nc, t)


def kernel(**inputs):
    import concourse.bacc as bacc
    from concourse.bass_utils import run_bass_kernel_spmd as run

    nc = bacc.Bacc("TRN2", target_bir_lowering=False, num_devices=1)
    arrays = lay_out({n: np.asarray(a) for n, a in inputs.items()})
    program(nc, arrays)
    r = run(nc, [{f"in_{n}": a for n, a in arrays.items()}], core_ids=[0])
    return np.ascontiguousarray(
        r.results[0]["out_x"].reshape(P, TILES, D).transpose(1, 0, 2).reshape(SEQS, SEQ, D))
```
